# Optimizing a Trainium2 kernel written in Bass

```python
import numpy as np
import jax
import jax.numpy as jnp

def _softmax(x, axis=-1):
    return jax.nn.softmax(x, axis=axis)

def _gelu(x):
    return jax.nn.gelu(x, approximate=True)

def _silu(x):
    return jax.nn.silu(x)

def _sigmoid(x):
    return jax.nn.sigmoid(x)

def _layernorm(x, axis=-1, eps=1e-05):
    m = jnp.mean(x, axis=axis, keepdims=True)
    v = jnp.var(x, axis=axis, keepdims=True)
    return (x - m) / jnp.sqrt(v + eps)

def _scatter_add(tgt, idx, src, axis=0):
    return tgt.at[idx].add(src)

def _segment_sum(src, seg, n):
    return jax.ops.segment_sum(src, seg, n)
kernel_name = 'mk_pixart_seq_d1_seqx_r4_dc4010'

def setup_inputs(seed: int=0):
    np.random.seed(seed)
    _w = jnp.asarray

    def _rec_inputs():
        import jax
        import jax.numpy as jnp
        _rk = jax.random.key(seed)
        x = -0.0005207 + 1.001 * jax.random.normal(jax.random.fold_in(_rk, 1), (4, 1024, 256), jnp.float32)
        _lenS = 1024 - jax.random.randint(jax.random.fold_in(_rk, 7), (4,), 0, max(1, 1024 // 4) + 1, jnp.int32)
        _lenS2 = 64 - jax.random.randint(jax.random.fold_in(_rk, 8), (4,), 0, max(1, 64 // 4) + 1, jnp.int32)
        cond_1024 = 0.000887014 + 1.03683 * jax.random.normal(jax.random.fold_in(_rk, 11), (4, 256), jnp.float32)
        _ctx_768P = jax.random.normal(jax.random.fold_in(_rk, 12), (4, 16, 192), jnp.float32)
        _ctx_768c = jax.random.dirichlet(jax.random.fold_in(_rk, 512), 0.3 * jnp.ones((16,), jnp.float32), (4, 64))
        _ctx_768t = jnp.einsum('bsk,bkd->bsd', _ctx_768c, _ctx_768P)
        _ctx_768t = _ctx_768t * jax.lax.rsqrt(jnp.mean(jnp.square(_ctx_768t)) + 1e-12) * 0.953939
        ctx_768 = 0.000599585 + 1.00006 * (_ctx_768t + 0.3 * jax.random.normal(jax.random.fold_in(_rk, 612), (4, 64, 192), jnp.float32))
        return (x, cond_1024, ctx_768)
    x, cond_1024, ctx_768 = _rec_inputs()

    def _L0_xcond_setup():
        import jax, jax.numpy as jnp
        import numpy as np
        B, N, M = (2, 256, 128)
        D, H, DH = (256, 16, 64)
        MID = H * DH
        DC = 192
        MULT = 4
        EPS = 1e-05

        def _ln(x, w, b):
            mu = jnp.mean(x, -1, keepdims=True)
            var = jnp.mean((x - mu) ** 2, -1, keepdims=True)
            return (x - mu) * jax.lax.rsqrt(var + EPS) * w + b

        def _sincos(n, d):
            inv = 1.0 / 10000.0 ** (jnp.arange(0, d, 2, dtype=jnp.float32) / d)
            ang = jnp.arange(n, dtype=jnp.float32)[:, None] * inv[None, :]
            return (jnp.sin(ang), jnp.cos(ang))

        def _rope(x, sin, cos):
            s = sin[None, None]
            c = cos[None, None]
            xe = x[..., ::2]
            xo = x[..., 1::2]
            re = xe * c - xo * s
            ro = xe * s + xo * c
            return jnp.stack((re, ro), axis=-1).reshape(x.shape)

        def _heads(t):
            b, n, _ = t.shape
            return t.reshape(b, n, H, DH).transpose(0, 2, 1, 3)

        def _attn(xq, ctx, wq, wkv, wo, bo):
            q = _heads(xq @ wq)
            k, v = jnp.split(ctx @ wkv, 2, axis=-1)
            k = _heads(k)
            v = _heads(v)
            sq, cq = _sincos(q.shape[2], DH)
            sk, ck = _sincos(k.shape[2], DH)
            q = _rope(q, sq, cq)
            k = _rope(k, sk, ck)
            sim = jnp.einsum('bhnd,bhmd->bhnm', q, k) * DH ** (-0.5)
            a = jax.nn.softmax(sim, axis=-1)
            o = jnp.einsum('bhnm,bhmd->bhnd', a, v)
            o = o.transpose(0, 2, 1, 3).reshape(xq.shape[0], xq.shape[1], MID)
            return o @ wo + bo

        def _adaln(x, c, lw, lb, gw, gb, bw, bb):
            g = (c @ gw + gb)[:, None, :]
            bt = (c @ bw + bb)[:, None, :]
            return _ln(x, lw, lb) * (1.0 + g) + bt
        ks = jax.random.split(jax.random.key(seed), 24)
        s = 0.02
        inp = {'x': jax.random.normal(ks[0], (B, N, D), jnp.float32), 'cond': jax.random.normal(ks[1], (B, D), jnp.float32), 'context': jax.random.normal(ks[2], (B, M, DC), jnp.float32), 'ln1_w': jnp.ones((D,), jnp.float32), 'ln1_b': jnp.zeros((D,), jnp.float32), 'g1_w': jax.random.normal(ks[3], (D, D), jnp.float32) * s, 'g1_b': jnp.zeros((D,), jnp.float32), 'b1_w': jax.random.normal(ks[4], (D, D), jnp.float32) * s, 'b1_b': jnp.zeros((D,), jnp.float32), 'ln2_w': jnp.ones((D,), jnp.float32), 'ln2_b': jnp.zeros((D,), jnp.float32), 'g2_w': jax.random.normal(ks[5], (D, D), jnp.float32) * s, 'g2_b': jnp.zeros((D,), jnp.float32), 'b2_w': jax.random.normal(ks[6], (D, D), jnp.float32) * s, 'b2_b': jnp.zeros((D,), jnp.float32), 'sa_wq': jax.random.normal(ks[7], (D, MID), jnp.float32) * s, 'sa_wkv': jax.random.normal(ks[8], (D, 2 * MID), jnp.float32) * s, 'sa_wo': jax.random.normal(ks[9], (MID, D), jnp.float32) * s, 'sa_bo': jnp.zeros((D,), jnp.float32), 'ca_lnc_w': jnp.ones((DC,), jnp.float32), 'ca_lnc_b': jnp.zeros((DC,), jnp.float32), 'ca_wq': jax.random.normal(ks[10], (D, MID), jnp.float32) * s, 'ca_wkv': jax.random.normal(ks[11], (DC, 2 * MID), jnp.float32) * s, 'ca_wo': jax.random.normal(ks[12], (MID, D), jnp.float32) * s, 'ca_bo': jnp.zeros((D,), jnp.float32), 'ff_w1': jax.random.normal(ks[13], (D, MULT * D), jnp.float32) * s, 'ff_b1': jnp.zeros((MULT * D,), jnp.float32), 'ff_w2': jax.random.normal(ks[14], (MULT * D, D), jnp.float32) * s, 'ff_b2': jnp.zeros((D,), jnp.float32)}
        return inp
    _L0_xcond_all = _L0_xcond_setup()
    _L0_xcond_in = {k: v for k, v in _L0_xcond_all.items() if k in ('ln1_w', 'ln1_b', 'g1_w', 'g1_b', 'b1_w', 'b1_b', 'ln2_w', 'ln2_b', 'g2_w', 'g2_b', 'b2_w', 'b2_b', 'sa_wq', 'sa_wkv', 'sa_wo', 'sa_bo', 'ca_lnc_w', 'ca_lnc_b', 'ca_wq', 'ca_wkv', 'ca_wo', 'ca_bo', 'ff_w1', 'ff_b1', 'ff_w2', 'ff_b2')}
    del _L0_xcond_all
    return {'x': x, 'cond_1024': cond_1024, 'ctx_768': ctx_768, 'L0_xcond_ln1_w': _L0_xcond_in['ln1_w'], 'L0_xcond_ln1_b': _L0_xcond_in['ln1_b'], 'L0_xcond_g1_w': _L0_xcond_in['g1_w'], 'L0_xcond_g1_b': _L0_xcond_in['g1_b'], 'L0_xcond_b1_w': _L0_xcond_in['b1_w'], 'L0_xcond_b1_b': _L0_xcond_in['b1_b'], 'L0_xcond_ln2_w': _L0_xcond_in['ln2_w'], 'L0_xcond_ln2_b': _L0_xcond_in['ln2_b'], 'L0_xcond_g2_w': _L0_xcond_in['g2_w'], 'L0_xcond_g2_b': _L0_xcond_in['g2_b'], 'L0_xcond_b2_w': _L0_xcond_in['b2_w'], 'L0_xcond_b2_b': _L0_xcond_in['b2_b'], 'L0_xcond_sa_wq': _L0_xcond_in['sa_wq'], 'L0_xcond_sa_wkv': _L0_xcond_in['sa_wkv'], 'L0_xcond_sa_wo': _L0_xcond_in['sa_wo'], 'L0_xcond_sa_bo': _L0_xcond_in['sa_bo'], 'L0_xcond_ca_lnc_w': _L0_xcond_in['ca_lnc_w'], 'L0_xcond_ca_lnc_b': _L0_xcond_in['ca_lnc_b'], 'L0_xcond_ca_wq': _L0_xcond_in['ca_wq'], 'L0_xcond_ca_wkv': _L0_xcond_in['ca_wkv'], 'L0_xcond_ca_wo': _L0_xcond_in['ca_wo'], 'L0_xcond_ca_bo': _L0_xcond_in['ca_bo'], 'L0_xcond_ff_w1': _L0_xcond_in['ff_w1'], 'L0_xcond_ff_b1': _L0_xcond_in['ff_b1'], 'L0_xcond_ff_w2': _L0_xcond_in['ff_w2'], 'L0_xcond_ff_b2': _L0_xcond_in['ff_b2']}

def reference(x, cond_1024, ctx_768, L0_xcond_ln1_w, L0_xcond_ln1_b, L0_xcond_g1_w, L0_xcond_g1_b, L0_xcond_b1_w, L0_xcond_b1_b, L0_xcond_ln2_w, L0_xcond_ln2_b, L0_xcond_g2_w, L0_xcond_g2_b, L0_xcond_b2_w, L0_xcond_b2_b, L0_xcond_sa_wq, L0_xcond_sa_wkv, L0_xcond_sa_wo, L0_xcond_sa_bo, L0_xcond_ca_lnc_w, L0_xcond_ca_lnc_b, L0_xcond_ca_wq, L0_xcond_ca_wkv, L0_xcond_ca_wo, L0_xcond_ca_bo, L0_xcond_ff_w1, L0_xcond_ff_b1, L0_xcond_ff_w2, L0_xcond_ff_b2):
    import jax
    import jax.numpy as jnp

    def _L0_xcond_ref(x, cond, context, ln1_w, ln1_b, g1_w, g1_b, b1_w, b1_b, ln2_w, ln2_b, g2_w, g2_b, b2_w, b2_b, sa_wq, sa_wkv, sa_wo, sa_bo, ca_lnc_w, ca_lnc_b, ca_wq, ca_wkv, ca_wo, ca_bo, ff_w1, ff_b1, ff_w2, ff_b2):
        import jax, jax.numpy as jnp
        import numpy as np
        B, N, M = (2, 256, 128)
        D, H, DH = (256, 16, 64)
        MID = H * DH
        DC = 192
        MULT = 4
        EPS = 1e-05

        def _ln(x, w, b):
            mu = jnp.mean(x, -1, keepdims=True)
            var = jnp.mean((x - mu) ** 2, -1, keepdims=True)
            return (x - mu) * jax.lax.rsqrt(var + EPS) * w + b

        def _sincos(n, d):
            inv = 1.0 / 10000.0 ** (jnp.arange(0, d, 2, dtype=jnp.float32) / d)
            ang = jnp.arange(n, dtype=jnp.float32)[:, None] * inv[None, :]
            return (jnp.sin(ang), jnp.cos(ang))

        def _rope(x, sin, cos):
            s = sin[None, None]
            c = cos[None, None]
            xe = x[..., ::2]
            xo = x[..., 1::2]
            re = xe * c - xo * s
            ro = xe * s + xo * c
            return jnp.stack((re, ro), axis=-1).reshape(x.shape)

        def _heads(t):
            b, n, _ = t.shape
            return t.reshape(b, n, H, DH).transpose(0, 2, 1, 3)

        def _attn(xq, ctx, wq, wkv, wo, bo):
            q = _heads(xq @ wq)
            k, v = jnp.split(ctx @ wkv, 2, axis=-1)
            k = _heads(k)
            v = _heads(v)
            sq, cq = _sincos(q.shape[2], DH)
            sk, ck = _sincos(k.shape[2], DH)
            q = _rope(q, sq, cq)
            k = _rope(k, sk, ck)
            sim = jnp.einsum('bhnd,bhmd->bhnm', q, k) * DH ** (-0.5)
            a = jax.nn.softmax(sim, axis=-1)
            o = jnp.einsum('bhnm,bhmd->bhnd', a, v)
            o = o.transpose(0, 2, 1, 3).reshape(xq.shape[0], xq.shape[1], MID)
            return o @ wo + bo

        def _adaln(x, c, lw, lb, gw, gb, bw, bb):
            g = (c @ gw + gb)[:, None, :]
            bt = (c @ bw + bb)[:, None, :]
            return _ln(x, lw, lb) * (1.0 + g) + bt
        attn_in = _adaln(x, cond, ln1_w, ln1_b, g1_w, g1_b, b1_w, b1_b)
        x = _attn(attn_in, attn_in, sa_wq, sa_wkv, sa_wo, sa_bo) + x
        cross_in = _adaln(x, cond, ln1_w, ln1_b, g1_w, g1_b, b1_w, b1_b)
        ctx_n = _ln(context, ca_lnc_w, ca_lnc_b)
        x = _attn(cross_in, ctx_n, ca_wq, ca_wkv, ca_wo, ca_bo) + x
        ffn_in = _adaln(x, cond, ln2_w, ln2_b, g2_w, g2_b, b2_w, b2_b)
        h = jax.nn.gelu(ffn_in @ ff_w1 + ff_b1, approximate=False)
        x = h @ ff_w2 + ff_b2 + x
        return x
    x = _L0_xcond_ref(x, cond_1024, ctx_768, L0_xcond_ln1_w, L0_xcond_ln1_b, L0_xcond_g1_w, L0_xcond_g1_b, L0_xcond_b1_w, L0_xcond_b1_b, L0_xcond_ln2_w, L0_xcond_ln2_b, L0_xcond_g2_w, L0_xcond_g2_b, L0_xcond_b2_w, L0_xcond_b2_b, L0_xcond_sa_wq, L0_xcond_sa_wkv, L0_xcond_sa_wo, L0_xcond_sa_bo, L0_xcond_ca_lnc_w, L0_xcond_ca_lnc_b, L0_xcond_ca_wq, L0_xcond_ca_wkv, L0_xcond_ca_wo, L0_xcond_ca_bo, L0_xcond_ff_w1, L0_xcond_ff_b1, L0_xcond_ff_w2, L0_xcond_ff_b2)
    return x

_drawn_inputs = setup_inputs


def setup_inputs(seed=0):
    import zlib

    import numpy as np

    out = dict(_drawn_inputs(seed))
    spreads = {'L0_xcond_ln1_w': (1.0, 0.6),
     'L0_xcond_ln1_b': (0.0, 0.384),
     'L0_xcond_g1_b': (0.0, 0.8),
     'L0_xcond_b1_b': (0.0, 0.359),
     'L0_xcond_ln2_w': (1.0, 0.6),
     'L0_xcond_ln2_b': (0.0, 0.618),
     'L0_xcond_g2_b': (0.0, 0.695),
     'L0_xcond_b2_b': (0.0, 0.764),
     'L0_xcond_sa_bo': (0.0, 0.1),
     'L0_xcond_ca_lnc_w': (1.0, 0.6),
     'L0_xcond_ca_lnc_b': (0.0, 0.532),
     'L0_xcond_ca_bo': (0.0, 0.1),
     'L0_xcond_ff_b1': (0.0, 0.273),
     'L0_xcond_ff_b2': (0.0, 0.1)}
    factors = {'L0_xcond_g1_w': 7.959, 'L0_xcond_sa_wq': 8.0, 'L0_xcond_ca_wq': 8.0}
    for name, (base, spread) in spreads.items():
        noise = np.random.default_rng([zlib.crc32(name.encode()), seed]).standard_normal(out[name].shape)
        drawn = base * np.exp(spread * noise) if base else spread * noise
        out[name] = jnp.asarray(drawn.astype(out[name].dtype))
    for name, factor in factors.items():
        out[name] = (out[name] * factor).astype(out[name].dtype)
    return out
```

```python
from contextlib import ExitStack

import numpy as np

import concourse.bass as bass
from concourse import mybir

F32 = mybir.dt.float32
F32R = mybir.dt.float32r
ALU = mybir.AluOpType
ACT = mybir.ActivationFunctionType
AX = mybir.AxisListType

P = 128
B, N, D = 4, 1024, 256
H, DH = 16, 64
MID = H * DH
M, DC = 64, 192
F = 4 * D
KD = D // P
HP = H // 2
PAIRS = HP * B
KT = N // P
HALF = 512
TOK = B * N
GROUPS = TOK // HALF
GT = HALF // P
EPS = 1e-5
SCALE = DH ** -0.5
PREP_JOBS = 44


class Counter:

    def __init__(self, sem, per_round, step=1, start=0):
        self.sem, self.per, self.step, self.start = sem, per_round, step, start

    def at(self, r, n):
        return (r * self.per + n) * self.step + self.start


def after(eng, counter, r, n):
    eng.wait_ge(counter.sem, counter.at(r, n))


def after_sp(sp, counter, r, n, carrier):
    sp.wait_ge(counter.sem, counter.at(r, n))
    sp.sem_inc(carrier, 1)


def split_products(hi_a, lo_a, hi_b, lo_b):
    return ((hi_a, hi_b), (hi_a, lo_b), (lo_a, hi_b))


def as_f32(ap):
    return ap.bitcast(F32)


class Layernorm:

    def __init__(self, nc, sb, ps, sem, name):
        self.stats = sb(f"{name}_stats", [P, GT, 6], F32)
        self.moments = sb(f"{name}_moments", [P, GT, 2], F32)
        self.var_eps = sb(f"{name}_var_eps", [P, GT], F32)
        self.rstd = sb(f"{name}_rstd", [P, GT], F32)
        self.minus_half = sb(f"{name}_minus_half", [P, GT], F32)
        self.xn = sb(f"{name}_xn", [P, GT, D], F32)
        self.y = sb(f"{name}_y", [P, KD, HALF], F32)
        self.turned = [ps(f"{name}_turned{k}", [P, HALF], F32) for k in range(KD)]
        self.s_half = sem(f"{name}_half")
        self.s_carrier = sem(f"{name}_carrier")
        self.s_stat = Counter(sem(f"{name}_stat"), GT)
        self.s_mom = Counter(sem(f"{name}_mom"), GT)
        self.s_var = Counter(sem(f"{name}_var"), 1)
        self.s_rstd = Counter(sem(f"{name}_rstd"), 1)
        self.s_xn = Counter(sem(f"{name}_xn"), GT, start=GT)
        self.s_turned = Counter(sem(f"{name}_turned"), KD, start=KD)
        self.s_mod = Counter(sem(f"{name}_mod"), 2 * KD, start=2 * KD)
        self.s_lo = Counter(sem(f"{name}_lo"), KD, start=KD)

    def start_dve(self, nc, dve):
        nc.vector.memset(self.minus_half[:], -0.5).then_inc(self.s_half, 1)
        dve.sem_inc(self.s_xn.sem, GT)
        dve.sem_inc(self.s_lo.sem, KD)

    def start_pe(self, pe):
        pe.sem_inc(self.s_turned.sem, KD)

    def start_act(self, act):
        act.sem_inc(self.s_mod.sem, 2 * KD)


def phase_setup(nc, io, keep, sem):
    with ExitStack() as ctx:
        sb = lambda n, s, d: ctx.enter_context(nc.sbuf_tensor(n, s, d))
        ps = lambda n, s, d: ctx.enter_context(nc.psum_tensor(n, s, d))
        cond = sb("cond", [P, KD, B], F32)
        gw = sb("gate_weights", [P, 4, KD, D], F32)
        vec = sb("gate_vectors", [P, 8, KD], F32)
        gate = sb("gates", [P, 4, KD, B], F32)
        gate_ps = ps("gate_ps", [P, 4, KD, B], F32)
        s_in, s_mm, s_g, s_f, s_h = (sem(f"setup_{n}") for n in ("in", "mm", "g", "f", "h"))
        loads = [(keep.ident[:], io["ident"]), (keep.neg_block[:], io["neg_block"].rearrange("p (a q) -> p a q", q=P)),
                 (cond[:], io["cond"].rearrange("p (k b) -> p k b", b=B)),
                 (vec[:], io["gate_vec"].rearrange("p (v k) -> p v k", k=KD))]
        loads += [(gw[:, n], io[f"gate_w{n}"].rearrange("(k p) d -> p k d", p=P)) for n in range(4)]
        with nc.Block() as block:
            @block.sync
            def _(sp):
                for dst, src in loads:
                    sp.dma_start(dst, src).then_inc(s_in, 16)

            @block.tensor
            def _(pe):
                pe.wait_ge(s_in, 16 * len(loads))
                for n in range(4):
                    for k_out in range(KD):
                        for k in range(KD):
                            mm = nc.tensor.matmul(gate_ps[:, n, k_out], gw[:, n, k, k_out * P:(k_out + 1) * P],
                                                  cond[:, k], start=(k == 0), stop=(k == KD - 1))
                mm.then_inc(s_mm, 1)

            @block.vector
            def _(dve):
                dve.wait_ge(s_in, 16 * len(loads))
                dve.wait_ge(s_mm, 1)
                for n in range(4):
                    for k in range(KD):
                        last = nc.vector.tensor_scalar(gate[:, n, k], gate_ps[:, n, k], vec[:, 4 + n, k:k + 1],
                                                       1.0 if n % 2 == 0 else 0.0, ALU.add, ALU.add)
                last.then_inc(s_g, 1)
                dve.wait_ge(s_g, 1)
                for m in range(2):
                    for k in range(KD):
                        nc.vector.tensor_scalar(keep.mod_a[:, m, k], gate[:, 2 * m, k], vec[:, 2 * m, k:k + 1], None,
                                                ALU.mult).then_inc(s_f, 1)
                        nc.vector.scalar_tensor_tensor(out=keep.mod_c[:, m, k], in0=gate[:, 2 * m, k],
                                                       scalar=vec[:, 2 * m + 1, k:k + 1], in1=gate[:, 2 * m + 1, k],
                                                       op0=ALU.mult, op1=ALU.add).then_inc(s_f, 1)


def dve_norm(nc, dve, ln, x_tile, g):
    for j in range(GT):
        nc.vector.bn_stats(ln.stats[:, j], x_tile(j)).then_inc(ln.s_stat.sem, 1)
    after(dve, ln.s_xn, g - 1, GT)
    for j in range(GT):
        after(dve, ln.s_stat, g, j + 1)
        dve.sem_inc(ln.s_carrier, 1)
        nc.vector.bn_aggr(ln.moments[:, j], ln.stats[:, j]).then_inc(ln.s_mom.sem, 1)
    after(dve, ln.s_mom, g, GT)
    nc.vector.tensor_scalar(ln.var_eps[:], ln.moments[:, :, 1], EPS, None, ALU.add).then_inc(ln.s_var.sem, 1)
    after(dve, ln.s_rstd, g, 1)
    after(dve, ln.s_turned, g - 1, KD)
    for j in range(GT):
        nc.vector.tensor_scalar(ln.xn[:, j], x_tile(j), ln.moments[:, j, 0:1], ln.rstd[:, j:j + 1],
                                ALU.subtract, ALU.mult).then_inc(ln.s_xn.sem, 1)


def pool_rstd(nc, pool, ln, g):
    after(pool, ln.s_var, g, 1)
    nc.gpsimd.tensor_tensor(ln.rstd[:], ln.var_eps[:], ln.minus_half[:], ALU.pow).then_inc(ln.s_rstd.sem, 1)


def pe_turn(nc, pe, ln, ident, g):
    after(pe, ln.s_mod, g - 1, 2 * KD)
    for k in range(KD):
        for j in range(GT):
            if k == 0:
                after(pe, ln.s_xn, g, j + 1)
            mm = nc.tensor.transpose(ln.turned[k][:, j * P:(j + 1) * P], ln.xn[:, j, k * P:(k + 1) * P], ident)
        mm.then_inc(ln.s_turned.sem, 1)


def act_modulate(nc, act, ln, keep, m, g):
    batch = g // (N // HALF)
    after(act, ln.s_lo, g - 1, KD)
    for k in range(KD):
        after(act, ln.s_turned, g, k + 1)
        scale = keep.mod_a[:, m, k, bass.ds(batch, 1)]
        bias = keep.mod_c[:, m, k, bass.ds(batch, 1)]
        nc.scalar.activation(ln.y[:, k], ln.turned[k][:], ACT.Identity, scale=scale,
                             bias=bias).then_inc(ln.s_mod.sem, 1)
        nc.scalar.activation(keep.xt_hi[:, k, bass.ds(g * HALF, HALF)], ln.turned[k][:], ACT.Identity, scale=scale,
                             bias=bias).then_inc(ln.s_mod.sem, 1)


def dve_modulated_lo(nc, dve, ln, keep, g):
    for k in range(KD):
        after(dve, ln.s_mod, g, 2 * k + 2)
        cols = bass.ds(g * HALF, HALF)
        nc.vector.tensor_tensor(keep.xt_lo[:, k, cols], ln.y[:, k], as_f32(keep.xt_hi[:, k, cols]),
                                ALU.subtract).then_inc(ln.s_lo.sem, 1)


def phase_first_norm(nc, io, keep, sem):
    with ExitStack() as ctx:
        sb = lambda n, s, d: ctx.enter_context(nc.sbuf_tensor(n, s, d))
        ps = lambda n, s, d: ctx.enter_context(nc.psum_tensor(n, s, d))
        ln = Layernorm(nc, sb, ps, sem, "n1")
        x_sb = sb("x_first", [P, 2, GT, D], F32)
        s_x = [Counter(sem(f"n1_x{u}"), 1, 16) for u in range(2)]
        s_used = Counter(sem("n1_x_used"), 1, start=2)
        x_d = io["x"].rearrange("(g j p) d -> g p j d", p=P, j=GT)
        with nc.Block() as block:
            @block.sync
            def _(sp):
                with sp.Fori(0, GROUPS // 2) as i:
                    for u in range(2):
                        after_sp(sp, s_used, 2 * i + u - 2, 1, keep.s_carrier)
                        sp.dma_start(x_sb[:, u], x_d[2 * i + u]).then_inc(s_x[u].sem, 16)

            @block.vector
            def _(dve):
                ln.start_dve(nc, dve)
                dve.sem_inc(s_used.sem, 2)
                with dve.Fori(0, GROUPS // 2) as i:
                    for u in range(2):
                        g = 2 * i + u
                        after(dve, s_x[u], i, 1)
                        dve_norm(nc, dve, ln, lambda j: x_sb[:, u, j], g)
                        after(dve, ln.s_xn, g, GT)
                        dve.sem_inc(s_used.sem, 1)
                        dve_modulated_lo(nc, dve, ln, keep, g)

            @block.gpsimd
            def _(pool):
                pool.wait_ge(ln.s_half, 1)
                with pool.Fori(0, GROUPS) as g:
                    pool_rstd(nc, pool, ln, g)

            @block.tensor
            def _(pe):
                ln.start_pe(pe)
                with pe.Fori(0, GROUPS) as g:
                    pe_turn(nc, pe, ln, keep.ident[:], g)

            @block.scalar
            def _(act):
                ln.start_act(act)
                with act.Fori(0, GROUPS) as g:
                    act_modulate(nc, act, ln, keep, 0, g)



def phase_self_attention(nc, io, keep, sem, o_dram):
    with ExitStack() as ctx:
        sb = lambda n, s, d: ctx.enter_context(nc.sbuf_tensor(n, s, d))
        ps = lambda n, s, d: ctx.enter_context(nc.psum_tensor(n, s, d))
        w_raw = sb("w_raw", [P, KD, 3, P], F32)
        w_hi = sb("w_hi", [P, KD, 3, P], F32R)
        w_lo = sb("w_lo", [P, KD, 3, P], F32R)
        cos = sb("cos", [P, N], F32)
        sin = sb("sin", [P, N], F32)
        z = [sb("q_rows", [P, N], F32), sb("k_rows", [P, N], F32)]
        z_swap = [sb("q_swapped", [P, N], F32), sb("k_swapped", [P, N], F32)]
        vt = sb("v_turned", [P, N], F32)
        q1 = [sb(f"q_first{u}", [P, 2, N], F32R) for u in range(2)]
        q2 = [sb(f"q_second{u}", [P, 2, N], F32R) for u in range(2)]
        k1 = [sb(f"k_first{u}", [P, 2, N], F32R) for u in range(2)]
        k2 = [sb(f"k_second{u}", [P, 2, N], F32R) for u in range(2)]
        v = [sb(f"v_tokens{u}", [P, KT, P], F32) for u in range(2)]
        maxima = sb("maxima", [P, 2, KT, 2], F32)
        row_max = sb("row_max", [P, 2, KT], F32)
        probs = [[sb(f"probs{h}{i}", [P, N], F32) for i in range(2)] for h in range(2)]
        sums = [sb(f"sums{h}", [P, N], F32) for h in range(2)]
        o_raw = sb("o_raw", [P, N], F32)
        ones = sb("ones", [P, DH], F32)
        scores = [ps(f"scores{h}", [P, N], F32) for h in range(2)]
        o_ps = ps("o_ps", [P, N], F32)
        work = ps("work", [P, 2, HALF], F32)

        s_const = sem("sa_const")
        s_table = sem("sa_table")
        s_carrier = sem("sa_carrier")
        s_w = Counter(sem("sa_w"), 1, 16)
        s_whi = Counter(sem("sa_whi"), 1)
        s_wlo = Counter(sem("sa_wlo"), 1)
        s_job = Counter(sem("sa_job"), PREP_JOBS)
        s_evac = Counter(sem("sa_evac"), 8)
        s_red = Counter(sem("sa_red"), 36)
        s_swap = [Counter(sem(f"sa_swap{n}"), 4, 16) for n in range(2)]
        s_sin = Counter(sem("sa_sin"), 2)
        s_rope = Counter(sem("sa_rope"), 4)
        s_hi = Counter(sem("sa_hi"), 8)
        s_lo = Counter(sem("sa_lo"), 4)
        s_comb = Counter(sem("sa_comb"), 2)
        s_recip = Counter(sem("sa_recip"), 2)
        s_store = Counter(sem("sa_store"), 1, 16)
        s_score = Counter(sem("sa_score"), 2 * KT, start=2 * KT)
        s_exp = Counter(sem("sa_exp"), 2 * KT, start=2 * KT)
        s_pv = Counter(sem("sa_pv"), KT, start=KT)
        s_acc = Counter(sem("sa_acc"), 2 * (KT - 1), start=2 * (KT - 1))
        s_oraw = Counter(sem("sa_oraw"), 1, start=1)

        proj = [("proj", zz, half) for zz in range(3) for half in range(2)]
        top = [("max", 0, i) for i in range(2 * KT)] + [("max", 1, i) for i in range(2)] + [("turn", 0, 0)] \
            + [("max", 1, i) for i in range(2, 2 * KT)] + [("turn", 1, 0)]
        jobs = proj + [("sum", 0, 0), ("sum", 0, 1), ("vturn", 0, 0), ("vturn", 0, 1)] + top
        index = {job: n for n, job in enumerate(jobs)}
        plan = [jobs[0:2], jobs[2:4], jobs[4:6], jobs[6:8], jobs[8:9], jobs[9:10], [], []]
        rest, cuts = jobs[10:-1], [0, 4, 8, 12, 17, 21, 25, 29, 33]
        plan += [rest[cuts[i]:cuts[i + 1]] for i in range(8)]
        assert sum(map(len, plan)) == PREP_JOBS - 1 and len(jobs) == PREP_JOBS
        by_act = [j for j in jobs if j[0] in ("proj", "vturn")]
        by_dve = [j for j in jobs if j[0] in ("sum", "max", "turn")]

        def job_read(eng, p, n, first):
            r, n = (p, n - 2) if n >= 2 else (p - 1, n - 2 + PREP_JOBS)
            if first and n > PREP_JOBS - 3:
                return
            job = jobs[n]
            if job in by_act:
                after(eng, s_evac, r, by_act.index(job) + 1)
            else:
                after(eng, s_red, r, by_dve.index(job) + 1)

        def add_index(kt, h):
            return (max(kt, 1) - 1) * 2 + h + 1

        x_cols = lambda xt, k, b, half: xt[:, k, bass.ds(b * N + half * HALF, HALF)]

        with nc.Block() as block:
            @block.sync
            def _(sp):
                sp.dma_start(cos[:], io["cos"]).then_inc(s_table, 16)
                sp.dma_start(sin[:], io["sin"]).then_inc(s_table, 16)
                sp.dma_start(w_raw[:], io["w_self"][0]).then_inc(s_w.sem, 16)

                def swap(n, p, first):
                    after_sp(sp, s_evac, p, 2 * n + 2, keep.s_carrier)
                    if not first:
                        after_sp(sp, s_rope, p - 1, 2 * n + 2, keep.s_carrier)
                    for q in range(4):
                        sp.dma_start(z_swap[n][32 * q:32 * q + 32], z[n][32 * (q ^ 1):32 * (q ^ 1) + 32]) \
                          .then_inc(s_swap[n].sem, 16)

                def body(p, first=False):
                    swap(0, p, first)
                    swap(1, p, first)
                    after_sp(sp, s_red, p, 2, keep.s_carrier)
                    sp.dma_start(o_dram[bass.ds(p, 1)].rearrange("o p n -> (o p) n"), o_raw[:]) \
                      .then_inc(s_store.sem, 16)
                    after_sp(sp, s_whi, p, 1, keep.s_carrier)
                    after_sp(sp, s_wlo, p, 1, keep.s_carrier)
                    w_next = io["w_self"][bass.ds(((p + 1) // B) % HP, 1)].rearrange("o p k z m -> (o p) k z m")
                    sp.dma_start(w_raw[:], w_next).then_inc(s_w.sem, 16)

                body(0, first=True)
                with sp.Fori(0, PAIRS // 2) as i:
                    for u in range(2):
                        body(2 * i + u + 1)
                after_sp(sp, s_red, PAIRS + 1, 2, keep.s_carrier)
                sp.dma_start(o_dram[PAIRS + 1], o_raw[:]).then_inc(s_store.sem, 16)
                after_sp(sp, s_store, PAIRS + 1, 1, keep.s_carrier)

            @block.tensor
            def _(pe):
                pe.sem_inc(s_score.sem, 2 * KT)
                pe.sem_inc(s_pv.sem, KT)

                def run_job(job, p, u, first=False):
                    kind, h, i = job
                    n = index[job]
                    job_read(pe, p, n, first)
                    bank = work[:, n % 2]
                    if kind == "proj":
                        if (h, i) == (0, 0):
                            after(pe, s_whi, p, 1)
                            after(pe, s_wlo, p, 1)
                        steps = [(w, x, k) for k in range(KD)
                                 for w, x in split_products(w_hi, w_lo, keep.xt_hi, keep.xt_lo)]
                        for m, (w, x, k) in enumerate(steps):
                            mm = nc.tensor.matmul(bank, w[:, k, h], x_cols(x, k, p % B, i), start=(m == 0),
                                                  stop=(m == len(steps) - 1))
                    elif kind == "sum":
                        if first:
                            pe.wait_ge(s_const, 4)
                        elif i == 0:
                            after(pe, s_acc, p - 2, 2 * (KT - 1))
                        for hh in range(2):
                            mm = nc.tensor.matmul(work[hh * DH:(hh + 1) * DH, n % 2], ones[:],
                                                  sums[hh][:, i * HALF:(i + 1) * HALF], start=True, stop=True)
                    elif kind == "vturn":
                        if i == 0:
                            after(pe, s_evac, p, 6)
                        for c in range(4):
                            mm = nc.tensor.transpose(work[:, n % 2, c * P:(c + 1) * P],
                                                     vt[:, (4 * i + c) * P:(4 * i + c + 1) * P], keep.ident[:])
                    elif kind == "max":
                        if (h, i) == (0, 0):
                            after(pe, s_hi, p, 8)
                            after(pe, s_lo, p, 4)
                        qt, half = i // 2, i % 2
                        mm = nc.tensor.matmul(bank, q1[u][:, h, qt * P:(qt + 1) * P],
                                              k1[u][:, h, half * HALF:(half + 1) * HALF], start=True, stop=True)
                    else:
                        after(pe, s_comb, p, h + 1)
                        mm = nc.tensor.transpose(work[0:KT, n % 2, 0:P], row_max[:, h], keep.ident[:])
                    mm.then_inc(s_job.sem, 1)

                def qk(t, kt, h, u):
                    if kt == 0:
                        after(pe, s_exp, t - 1, 2 * KT - 1 + h)
                        after(pe, s_red, t, by_dve.index(("turn", h, 0)) + 1)
                    else:
                        after(pe, s_exp, t, 2 * kt - 1 + h)
                    for q_side, k_side, start in ((q1, k1, True), (q2, k2, False)):
                        for half in range(2):
                            cols = slice(half * HALF, (half + 1) * HALF)
                            mm = nc.tensor.matmul(scores[h][:, cols], k_side[u][:, h, kt * P:(kt + 1) * P],
                                                  q_side[u][:, h, cols], start=start, stop=not start)
                    mm.then_inc(s_score.sem, 1)

                def pv(t, kt, u):
                    after(pe, s_exp, t, 2 * kt + 2)
                    if kt == 0:
                        after(pe, s_oraw, t - 1, 1)
                        after(pe, s_evac, t, 8)
                    for half in range(2):
                        cols = slice(half * HALF, (half + 1) * HALF)
                        for h in range(2):
                            mm = nc.tensor.matmul(o_ps[h * DH:(h + 1) * DH, cols], v[u][:, kt, h * DH:(h + 1) * DH],
                                                  probs[h][kt % 2][:, cols], start=(kt == 0), stop=(kt == KT - 1))
                    mm.then_inc(s_pv.sem, 1)

                for job in jobs:
                    run_job(job, 0, 0, first=True)
                with pe.Fori(0, PAIRS // 2) as i:
                    for u in range(2):
                        t = 2 * i + u
                        for kt in range(KT):
                            for h in range(2):
                                qk(t, kt, h, u)
                                for job in plan[2 * kt + h]:
                                    run_job(job, t + 1, 1 - u)
                            if kt:
                                pv(t, kt - 1, u)
                        pv(t, KT - 1, u)
                        run_job(jobs[-1], t + 1, 1 - u)
                after(pe, s_acc, PAIRS - 1, 2 * (KT - 1))
                after(pe, s_red, PAIRS, 36)
                for half in range(2):
                    for h in range(2):
                        mm = nc.tensor.matmul(work[h * DH:(h + 1) * DH, half], ones[:],
                                              sums[h][:, half * HALF:(half + 1) * HALF], start=True, stop=True)
                mm.then_inc(s_job.sem, 1)

            @block.scalar
            def _(act):
                act.sem_inc(s_exp.sem, 2 * KT)
                act.sem_inc(s_oraw.sem, 1)

                def split_w(p):
                    after(act, s_w, p, 1)
                    nc.scalar.activation(w_hi[:], w_raw[:], ACT.Copy).then_inc(s_whi.sem, 1)

                def evac(job, p, u, first=False):
                    n = index[job]
                    after(act, s_job, p, n + 1)
                    kind, zz, i = job
                    if kind == "vturn":
                        if not first:
                            after(act, s_pv, p - 2, KT)
                        dst = v[u][:, 4 * i:4 * i + 4].rearrange("p c m -> p (c m)")
                    else:
                        dst = (z + [vt])[zz][:, i * HALF:(i + 1) * HALF]
                        if zz < 2 and not first:
                            after(act, s_lo, p - 1, 2 * zz + 2)
                    nc.scalar.activation(dst, work[:, n % 2], ACT.Copy).then_inc(s_evac.sem, 1)

                def high_halves(n, p, u):
                    after(act, s_rope, p, 2 * n + 2)
                    top, bot = slice(0, DH), slice(DH, P)
                    if n == 0:
                        places = [(q1[u][top, 0], top), (q1[u][bot, 0], top), (q1[u][top, 1], bot), (q1[u][bot, 1], bot)]
                    else:
                        places = [(k1[u][top, 0], top), (k2[u][top, 0], top), (k1[u][bot, 1], bot), (k2[u][bot, 1], bot)]
                    for dst, rows in places:
                        nc.scalar.activation(dst, z[n][rows], ACT.Copy).then_inc(s_hi.sem, 1)

                def exp(t, kt, h):
                    after(act, s_score, t, 2 * kt + h + 1)
                    r, k_old = (t, kt - 2) if kt >= 2 else (t - 1, kt - 2 + KT)
                    after(act, s_pv, r, k_old + 1)
                    after(act, s_acc, r, add_index(k_old, h))
                    nc.scalar.activation(probs[h][kt % 2][:], scores[h][:], ACT.Exp, scale=SCALE) \
                      .then_inc(s_exp.sem, 1)

                split_w(0)
                for job in proj:
                    evac(job, 0, 0, first=True)
                for i in range(2):
                    evac(("vturn", 0, i), 0, 0, first=True)
                after(act, s_job, 0, 6)
                split_w(1)
                high_halves(0, 0, 0)
                high_halves(1, 0, 0)
                with act.Fori(0, PAIRS // 2) as i:
                    for u in range(2):
                        t = 2 * i + u
                        p = t + 1
                        for kt in range(KT):
                            for h in range(2):
                                exp(t, kt, h)
                                for job in plan[2 * kt + h]:
                                    if job in by_act:
                                        evac(job, p, 1 - u)
                            if kt == 2:
                                after(act, s_job, p, 6)
                                split_w(p + 1)
                                high_halves(0, p, 1 - u)
                            if kt == 3:
                                high_halves(1, p, 1 - u)
                        after(act, s_pv, t, KT)
                        after(act, s_store, p, 1)
                        nc.scalar.activation(o_raw[:], o_ps[:], ACT.Copy).then_inc(s_oraw.sem, 1)

            @block.vector
            def _(dve):
                nc.vector.memset(ones[:], 1.0).then_inc(s_const, 1)
                for h in range(2):
                    nc.vector.memset(sums[h][:], 1.0).then_inc(s_const, 1)
                nc.vector.memset(o_raw[:], 0.0).then_inc(s_const, 1)
                for u in range(2):
                    nc.vector.memset(as_f32(q2[u][:]), 0.0).then_inc(s_const, 1)
                    nc.vector.memset(as_f32(k2[u][:]), 0.0).then_inc(s_const, 1)
                n_const = 8
                dve.wait_ge(s_const, n_const)
                for u in range(2):
                    nc.vector.memset(as_f32(k2[u][DH:DH + KT, 0]), 1.0).then_inc(s_const, 1)
                    nc.vector.memset(as_f32(k2[u][0:KT, 1]), 1.0).then_inc(s_const, 1)
                dve.wait_ge(s_const, n_const + 4)
                dve.wait_ge(s_table, 32)

                def lo_w(p):
                    after(dve, s_whi, p, 1)
                    nc.vector.tensor_tensor(w_lo[:], w_raw[:], as_f32(w_hi[:]), ALU.subtract).then_inc(s_wlo.sem, 1)

                def normalise(p, jobs_done, first=False):
                    for i in range(2):
                        bank = work[:, i]
                        dve.wait_ge(s_job.sem, jobs_done[i])
                        nc.vector.reciprocal(bank, bank).then_inc(s_recip.sem, 1)
                    for i in range(2):
                        half = slice(i * HALF, (i + 1) * HALF)
                        after(dve, s_recip, p, i + 1)
                        if i == 0 and not first:
                            after(dve, s_oraw, p - 2, 1)
                        nc.vector.tensor_tensor(o_raw[:, half], o_raw[:, half], work[:, i], ALU.mult) \
                            .then_inc(s_red.sem, 1)

                def rope(n, p):
                    after(dve, s_evac, p, 2 * n + 2)
                    after(dve, s_swap[n], p, 4)
                    nc.vector.tensor_tensor(z[n][:], z[n][:], cos[:], ALU.mult).then_inc(s_rope.sem, 1)
                    after(dve, s_rope, p, 2 * n + 1)
                    after(dve, s_sin, p, n + 1)
                    nc.vector.tensor_tensor(z[n][:], z[n][:], z_swap[n][:], ALU.add).then_inc(s_rope.sem, 1)

                def low_halves(n, p, u):
                    top, bot = slice(0, DH), slice(DH, P)
                    hi = (q1 if n == 0 else k1)[u]
                    after(dve, s_hi, p, 4 * n + 4)
                    for h, rows in ((0, top), (1, bot)):
                        dst = q2[u][rows, h] if n == 0 else k1[u][bot if h == 0 else top, h]
                        nc.vector.tensor_tensor(dst, z[n][rows], as_f32(hi[rows, h]), ALU.subtract) \
                          .then_inc(s_lo.sem, 1)

                def reduce(job, p, u):
                    kind, h, i = job
                    n = index[job]
                    if kind == "max":
                        after(dve, s_job, p, n + 1)
                        nc.vector.tensor_reduce(maxima[:, h, i // 2, i % 2:i % 2 + 1], work[:, n % 2], AX.X, ALU.max) \
                          .then_inc(s_red.sem, 1)
                        if i == 2 * KT - 1:
                            after(dve, s_red, p, by_dve.index(job) + 1)
                            nc.vector.tensor_reduce(row_max[:, h], maxima[:, h], AX.X, ALU.max) \
                              .then_inc(s_comb.sem, 1)
                    else:
                        after(dve, s_job, p, n + 1)
                        rows = slice(DH, DH + KT) if h == 0 else slice(0, KT)
                        turned = work[0:KT, n % 2, 0:P].rearrange("p (a q) -> p a q", a=1).to_broadcast([KT, KT, P])
                        nc.vector.tensor_tensor(q2[u][rows, h].rearrange("p (a q) -> p a q", q=P), turned,
                                                keep.neg_block[0:KT], ALU.mult).then_inc(s_red.sem, 1)

                def body(p, u, first=False):
                    rope(0, p)
                    rope(1, p)
                    normalise(p, [s_job.at(p, index[("sum", 0, i)] + 1) for i in range(2)], first)
                    lo_w(p + 1)
                    low_halves(0, p, u)
                    low_halves(1, p, u)
                    for job in by_dve[2:]:
                        reduce(job, p, u)

                lo_w(0)
                body(0, 0, first=True)
                with dve.Fori(0, PAIRS // 2) as i:
                    for u in range(2):
                        body(2 * i + u + 1, 1 - u)
                normalise(PAIRS + 1, [s_job.at(PAIRS + 1, 1)] * 2)

            @block.gpsimd
            def _(pool):
                pool.sem_inc(s_acc.sem, 2 * (KT - 1))
                pool.wait_ge(s_table, 32)

                def sine(n, p):
                    after(pool, s_swap[n], p, 4)
                    nc.gpsimd.tensor_tensor(z_swap[n][:], z_swap[n][:], sin[:], ALU.mult).then_inc(s_sin.sem, 1)

                def add(t, kt, h):
                    after(pool, s_exp, t, 2 * kt + h + 1)
                    if kt == 1:
                        after(pool, s_job, t + 1, index[("sum", 0, 1)] + 1)
                        first_term = probs[h][0][:]
                    else:
                        after(pool, s_acc, t, add_index(kt - 1, h))
                        first_term = sums[h][:]
                    nc.gpsimd.tensor_tensor(sums[h][:], first_term, probs[h][kt % 2][:], ALU.add) \
                      .then_inc(s_acc.sem, 1)

                sine(0, 0)
                sine(1, 0)
                with pool.Fori(0, PAIRS // 2) as i:
                    for u in range(2):
                        t = 2 * i + u
                        sine(0, t + 1)
                        sine(1, t + 1)
                        for kt in range(1, KT):
                            for h in range(2):
                                add(t, kt, h)

def phase_project(nc, io, keep, sem, name, o_pairs, wo, bias, m):
    first = m == 0
    chunk_tiles = GT // 2
    chunk = chunk_tiles * P
    with ExitStack() as ctx:
        sb = lambda n, s, d: ctx.enter_context(nc.sbuf_tensor(f"{name}_{n}", s, d))
        ps = lambda n, s, d: ctx.enter_context(nc.psum_tensor(f"{name}_{n}", s, d))
        ln = Layernorm(nc, lambda n, s, d: ctx.enter_context(nc.sbuf_tensor(n, s, d)),
                       lambda n, s, d: ctx.enter_context(nc.psum_tensor(n, s, d)), sem, f"{name}_ln")
        w_raw = sb("w_raw", [P, HP, D], F32)
        w_hi = sb("w_hi", [P, HP, D], F32R)
        w_lo = sb("w_lo", [P, HP, D], F32R)
        bias_row = sb("bias", [P, D], F32)
        o_raw = [sb(f"o_raw{c}", [P, HP, chunk], F32) for c in range(2)]
        o_hi = [sb(f"o_hi{c}", [P, HP, chunk], F32R) for c in range(2)]
        o_lo = [sb(f"o_lo{c}", [P, HP, chunk], F32R) for c in range(2)]
        x_bias = sb("x_bias", [P, GT, D], F32)
        x_old = sb("x_old", [P, GT, D], F32) if first else None
        acc = [ps(f"acc{c}", [P, chunk_tiles, D], F32) for c in range(2)]
        s_w = sem(f"{name}_w")
        s_w_hi = sem(f"{name}_w_hi")
        s_w_lo = sem(f"{name}_w_lo")
        s_carrier = sem(f"{name}_carrier")
        s_o = [Counter(sem(f"{name}_o{c}"), 1, 16) for c in range(2)]
        s_xold = Counter(sem(f"{name}_xold"), 1, 16)
        s_hi = Counter(sem(f"{name}_hi"), 2, start=2)
        s_lo = Counter(sem(f"{name}_lo"), 2, start=2)
        s_mm = Counter(sem(f"{name}_mm"), 2, start=2)
        s_xb = Counter(sem(f"{name}_xb"), GT, start=GT)
        s_x = Counter(sem(f"{name}_x"), 2, start=2)
        x_d = io["x"].rearrange("(g j p) d -> g p j d", p=P, j=GT)
        o_d = o_pairs.rearrange("(h b) p n -> b p h n", b=B)

        with nc.Block() as block:
            @block.sync
            def _(sp):
                sp.dma_start(w_raw[:], io[wo].rearrange("(h p) d -> p h d", p=P)).then_inc(s_w, 16)
                sp.dma_start(bias_row[:], io[bias].partition_broadcast(P)).then_inc(s_w, 16)
                with sp.Fori(0, GROUPS) as g:
                    for c in range(2):
                        after_sp(sp, s_hi, g - 1, c + 1, keep.s_carrier)
                        after_sp(sp, s_lo, g - 1, c + 1, keep.s_carrier)
                        start = (g % 2) * HALF + c * chunk
                        src = o_d[bass.ds(g // 2, 1), :, :, bass.ds(start, chunk)].rearrange("o p h n -> (o p) h n")
                        sp.dma_start(o_raw[c][:], src).then_inc(s_o[c].sem, 16)
                    if first:
                        after_sp(sp, s_xb, g - 1, GT, keep.s_carrier)
                        sp.dma_start(x_old[:], x_d[bass.ds(g, 1)].rearrange("o p j d -> (o p) j d")) \
                          .then_inc(s_xold.sem, 16)

            @block.gpsimd
            def _(pool):
                pool.sem_inc(s_xb.sem, GT)
                pool.wait_ge(s_w, 32)
                pool.wait_ge(ln.s_half, 1)

                def old_rows(g):
                    if first:
                        after(pool, s_xold, g, 1)
                    after(pool, s_x, g - 1, 2)
                    for j in range(GT):
                        src = x_old[:, j] if first else keep.x[:, bass.ds(g * GT + j, 1)].rearrange("p o d -> p (o d)")
                        nc.gpsimd.tensor_tensor(x_bias[:, j], src, bias_row[:], ALU.add).then_inc(s_xb.sem, 1)

                old_rows(0)
                with pool.Fori(1, GROUPS) as g:
                    old_rows(g)
                    pool_rstd(nc, pool, ln, g - 1)
                pool_rstd(nc, pool, ln, GROUPS - 1)

            @block.scalar
            def _(act):
                act.sem_inc(s_hi.sem, 2)
                ln.start_act(act)
                act.wait_ge(s_w, 32)
                nc.scalar.activation(w_hi[:], w_raw[:], ACT.Copy).then_inc(s_w_hi, 1)

                def halves(g):
                    for c in range(2):
                        after(act, s_o[c], g, 1)
                        after(act, s_mm, g - 1, c + 1)
                        nc.scalar.activation(o_hi[c][:], o_raw[c][:], ACT.Copy).then_inc(s_hi.sem, 1)

                halves(0)
                with act.Fori(1, GROUPS) as g:
                    halves(g)
                    act_modulate(nc, act, ln, keep, m, g - 1)
                act_modulate(nc, act, ln, keep, m, GROUPS - 1)

            @block.tensor
            def _(pe):
                pe.sem_inc(s_mm.sem, 2)
                ln.start_pe(pe)
                pe.wait_ge(s_w_hi, 1)
                pe.wait_ge(s_w_lo, 1)

                def products(g, c):
                    after(pe, s_lo, g, c + 1)
                    after(pe, s_hi, g, c + 1)
                    after(pe, s_x, g - 1, c + 1)
                    for j in range(chunk_tiles):
                        steps = [(o, w, h) for h in range(HP) for o, w in split_products(o_hi[c], o_lo[c], w_hi, w_lo)]
                        for n, (o, w, h) in enumerate(steps):
                            mm = nc.tensor.matmul(acc[c][:, j], o[:, h, j * P:(j + 1) * P], w[:, h], start=(n == 0),
                                                  stop=(n == len(steps) - 1))
                    mm.then_inc(s_mm.sem, 1)

                products(0, 0)
                products(0, 1)
                with pe.Fori(1, GROUPS) as g:
                    products(g, 0)
                    pe_turn(nc, pe, ln, keep.ident[:], g - 1)
                    products(g, 1)
                pe_turn(nc, pe, ln, keep.ident[:], GROUPS - 1)

            @block.vector
            def _(dve):
                dve.sem_inc(s_lo.sem, 2)
                dve.sem_inc(s_x.sem, 2)
                ln.start_dve(nc, dve)
                dve.wait_ge(s_w_hi, 1)
                nc.vector.tensor_tensor(w_lo[:], w_raw[:], as_f32(w_hi[:]), ALU.subtract).then_inc(s_w_lo, 1)

                def low_half(g, c):
                    after(dve, s_hi, g, c + 1)
                    nc.vector.tensor_tensor(o_lo[c][:], o_raw[c][:], as_f32(o_hi[c][:]), ALU.subtract) \
                      .then_inc(s_lo.sem, 1)

                def new_rows(g, c):
                    after(dve, s_mm, g, c + 1)
                    after(dve, s_xb, g, GT)
                    tiles = bass.ds(g * GT + c * chunk_tiles, chunk_tiles)
                    nc.vector.tensor_tensor(keep.x[:, tiles], acc[c][:], x_bias[:, c * chunk_tiles:(c + 1) * chunk_tiles],
                                            ALU.add).then_inc(s_x.sem, 1)

                def norm(g):
                    after(dve, s_x, g, 2)
                    dve.sem_inc(s_carrier, 1)
                    dve_norm(nc, dve, ln, lambda j: keep.x[:, bass.ds(g * GT + j, 1)].rearrange("p o d -> p (o d)"), g)
                    dve_modulated_lo(nc, dve, ln, keep, g)

                low_half(0, 0)
                low_half(0, 1)
                with dve.Fori(1, GROUPS) as g:
                    low_half(g, 0)
                    new_rows(g - 1, 0)
                    low_half(g, 1)
                    new_rows(g - 1, 1)
                    norm(g - 1)
                new_rows(GROUPS - 1, 0)
                new_rows(GROUPS - 1, 1)
                norm(GROUPS - 1)

def phase_context(nc, io, keep, sem, kv_dram):
    ct = B * M // P
    kw = (P, DC - P)
    with ExitStack() as ctx:
        sb = lambda n, s, d: ctx.enter_context(nc.sbuf_tensor(f"cx_{n}", s, d))
        ps = lambda n, s, d: ctx.enter_context(nc.psum_tensor(f"cx_{n}", s, d))
        rows = sb("rows", [P, ct, DC], F32)
        scale = sb("scale", [P, 2], F32)
        shift = sb("shift", [P, 2], F32)
        stats = sb("stats", [P, ct, 6], F32)
        moments = sb("moments", [P, ct, 2], F32)
        var_eps = sb("var_eps", [P, ct], F32)
        minus_half = sb("minus_half", [P, ct], F32)
        rstd = sb("rstd", [P, ct], F32)
        xn = sb("xn", [P, ct, DC], F32)
        y = sb("y", [P, 2, ct * P], F32)
        y_hi = sb("y_hi", [P, 2, ct * P], F32R)
        y_lo = sb("y_lo", [P, 2, ct * P], F32R)
        w_raw = sb("w_raw", [P, 2, 2, P], F32)
        w_hi = sb("w_hi", [P, 2, 2, P], F32R)
        w_lo = sb("w_lo", [P, 2, 2, P], F32R)
        cos = sb("cos", [P, M], F32)
        sin = sb("sin", [P, M], F32)
        z = sb("k_rows", [P, B, M], F32)
        z_swap = sb("k_swapped", [P, B, M], F32)
        kv = sb("kv", [P, B, 4, P], F32R)
        turned = ps("turned", [P, 2, ct * P], F32)
        k_ps = ps("k_ps", [P, B * M], F32)
        v_ps = ps("v_ps", [P, ct, P], F32)
        s_in, s_stat, s_mom, s_var, s_rstd, s_xn, s_turned, s_mod, s_ylo, s_half, s_zero, s_carrier = (
            sem(f"cx_{n}") for n in ("in", "stat", "mom", "var", "rstd", "xn", "turned", "mod", "ylo", "half", "zero",
                                     "carrier"))
        s_w = Counter(sem("cx_w"), 1, 16)
        s_whi = Counter(sem("cx_whi"), 1)
        s_wlo = Counter(sem("cx_wlo"), 1)
        s_k = Counter(sem("cx_k"), 1)
        s_v = Counter(sem("cx_v"), 1)
        s_evac = Counter(sem("cx_evac"), 1)
        s_swap = Counter(sem("cx_swap"), 4, 16)
        s_sin = Counter(sem("cx_sin"), 1)
        s_rope = Counter(sem("cx_rope"), 2)
        s_hi = Counter(sem("cx_hi"), 6)
        s_lo = Counter(sem("cx_lo"), 6, start=6)
        s_store = Counter(sem("cx_store"), 1, 16)
        top, bot = slice(0, DH), slice(DH, P)
        k_places = [(top, slice(0, M)), (bot, slice(M, 2 * M))]
        v_places = [(par, h) for par in range(2) for h in range(2)]

        with nc.Block() as block:
            @block.sync
            def _(sp):
                for dst, src in ((rows[:], io["ctx"].rearrange("(j p) d -> p j d", p=P)), (scale[:], io["lnc_w"]),
                                 (shift[:], io["lnc_b"]), (cos[:], io["cos"][:, 0:M]), (sin[:], io["sin"][:, 0:M])):
                    sp.dma_start(dst, src).then_inc(s_in, 16)
                sp.dma_start(w_raw[:], io["w_ctx"][0]).then_inc(s_w.sem, 16)

                def body(r, last=False):
                    after_sp(sp, s_evac, r, 1, keep.s_carrier)
                    if isinstance(r, int) is False:
                        after_sp(sp, s_rope, r - 1, 2, keep.s_carrier)
                    for q in range(4):
                        sp.dma_start(z_swap[32 * q:32 * q + 32], z[32 * (q ^ 1):32 * (q ^ 1) + 32]) \
                          .then_inc(s_swap.sem, 16)
                    if not last:
                        after_sp(sp, s_whi, r, 1, keep.s_carrier)
                        after_sp(sp, s_wlo, r, 1, keep.s_carrier)
                        src = io["w_ctx"][bass.ds((r + 1) % HP, 1)].rearrange("o p k z m -> (o p) k z m")
                        sp.dma_start(w_raw[:], src).then_inc(s_w.sem, 16)
                    after_sp(sp, s_hi, r, 6, keep.s_carrier)
                    after_sp(sp, s_lo, r, 6, keep.s_carrier)
                    sp.dma_start(kv_dram[bass.ds(r * B, B)].rearrange("b p n -> p b n"),
                                 as_f32(kv[:].rearrange("p b f n -> p b (f n)"))).then_inc(s_store.sem, 16)

                body(0)
                with sp.Fori(1, HP) as r:
                    body(r)
                after_sp(sp, s_store, HP - 1, 1, keep.s_carrier)
                after_sp(sp, s_w, HP, 1, keep.s_carrier)

            @block.gpsimd
            def _(pool):
                nc.gpsimd.memset(minus_half[:], -0.5).then_inc(s_half, 1)
                nc.gpsimd.memset(as_f32(kv[:]), 0.0).then_inc(s_zero, 1)
                pool.wait_ge(s_var, 1)
                pool.wait_ge(s_half, 1)
                nc.gpsimd.tensor_tensor(rstd[:], var_eps[:], minus_half[:], ALU.pow).then_inc(s_rstd, 1)
                with pool.Fori(0, HP) as r:
                    after(pool, s_swap, r, 4)
                    nc.gpsimd.tensor_tensor(z_swap[:], z_swap[:], sin[:].unsqueeze(1).to_broadcast([P, B, M]),
                                            ALU.mult).then_inc(s_sin.sem, 1)

            @block.vector
            def _(dve):
                dve.sem_inc(s_lo.sem, 6)
                dve.wait_ge(s_in, 80)
                for j in range(ct):
                    nc.vector.bn_stats(stats[:, j], rows[:, j]).then_inc(s_stat, 1)
                for j in range(ct):
                    dve.wait_ge(s_stat, j + 1)
                    nc.vector.bn_aggr(moments[:, j], stats[:, j]).then_inc(s_mom, 1)
                dve.wait_ge(s_mom, ct)
                nc.vector.tensor_scalar(var_eps[:], moments[:, :, 1], EPS, None, ALU.add).then_inc(s_var, 1)
                dve.wait_ge(s_rstd, 1)
                for j in range(ct):
                    nc.vector.tensor_scalar(xn[:, j], rows[:, j], moments[:, j, 0:1], rstd[:, j:j + 1], ALU.subtract,
                                            ALU.mult).then_inc(s_xn, 1)
                after(dve, s_whi, 0, 1)
                nc.vector.tensor_tensor(w_lo[:], w_raw[:], as_f32(w_hi[:]), ALU.subtract).then_inc(s_wlo.sem, 1)
                for k in range(2):
                    dve.wait_ge(s_mod, 2 * k + 2)
                    n = kw[k]
                    nc.vector.tensor_tensor(y_lo[0:n, k], y[0:n, k], as_f32(y_hi[0:n, k]), ALU.subtract) \
                        .then_inc(s_ylo, 1)
                dve.wait_ge(s_zero, 1)
                with dve.Fori(0, HP) as r:
                    after(dve, s_evac, r, 1)
                    after(dve, s_swap, r, 4)
                    nc.vector.tensor_tensor(z[:], z[:], cos[:].unsqueeze(1).to_broadcast([P, B, M]), ALU.mult) \
                        .then_inc(s_rope.sem, 1)
                    after(dve, s_whi, r + 1, 1)
                    nc.vector.tensor_tensor(w_lo[:], w_raw[:], as_f32(w_hi[:]), ALU.subtract).then_inc(s_wlo.sem, 1)
                    after(dve, s_sin, r, 1)
                    after(dve, s_rope, r, 1)
                    nc.vector.tensor_tensor(z[:], z[:], z_swap[:], ALU.add).then_inc(s_rope.sem, 1)
                    for n, (par, h) in enumerate(v_places):
                        after(dve, s_hi, r, 4)
                        half = k_places[h][0]
                        nc.vector.tensor_tensor(kv[half, par::2, 3, h * DH:(h + 1) * DH],
                                                v_ps[par * M:(par + 1) * M, :, h * DH:(h + 1) * DH],
                                                as_f32(kv[half, par::2, 2, h * DH:(h + 1) * DH]), ALU.subtract) \
                            .then_inc(s_lo.sem, 1)
                    for n, (half, cols) in enumerate(k_places):
                        after(dve, s_hi, r, 5 + n)
                        nc.vector.tensor_tensor(kv[half, :, 1, cols], z[half], as_f32(kv[half, :, 0, cols]),
                                                ALU.subtract).then_inc(s_lo.sem, 1)

            @block.scalar
            def _(act):
                def split_w(r):
                    after(act, s_w, r, 1)
                    nc.scalar.activation(w_hi[:], w_raw[:], ACT.Copy).then_inc(s_whi.sem, 1)

                split_w(0)
                act.wait_ge(s_in, 80)
                for k in range(2):
                    n = kw[k]
                    act.wait_ge(s_turned, 2)
                    for dst in (y, y_hi):
                        nc.scalar.activation(dst[0:n, k], turned[0:n, k], ACT.Identity, scale=scale[0:n, k:k + 1],
                                             bias=shift[0:n, k:k + 1]).then_inc(s_mod, 1)
                act.wait_ge(s_zero, 1)

                def body(r, stored):
                    after(act, s_k, r, 1)
                    after(act, s_lo, r - 1, 6)
                    nc.scalar.activation(z[:].rearrange("p b m -> p (b m)"), k_ps[:], ACT.Copy) \
                        .then_inc(s_evac.sem, 1)
                    after(act, s_v, r, 1)
                    split_w(r + 1)
                    if stored:
                        after(act, s_store, r - 1, 1)
                    for par, h in v_places:
                        half = k_places[h][0]
                        nc.scalar.activation(kv[half, par::2, 2, h * DH:(h + 1) * DH],
                                             v_ps[par * M:(par + 1) * M, :, h * DH:(h + 1) * DH], ACT.Copy) \
                            .then_inc(s_hi.sem, 1)
                    after(act, s_rope, r, 2)
                    for half, cols in k_places:
                        nc.scalar.activation(kv[half, :, 0, cols], z[half], ACT.Copy).then_inc(s_hi.sem, 1)

                body(0, False)
                with act.Fori(1, HP) as r:
                    body(r, True)

            @block.tensor
            def _(pe):
                for k in range(2):
                    for j in range(ct):
                        pe.wait_ge(s_xn, j + 1)
                        mm = nc.tensor.transpose(turned[0:kw[k], k, j * P:(j + 1) * P],
                                                 xn[:, j, k * P:k * P + kw[k]], keep.ident[:])
                    mm.then_inc(s_turned, 1)
                pe.wait_ge(s_ylo, 2)
                steps = lambda: [(a, b, k) for k in range(2) for a, b in split_products(w_hi, w_lo, y_hi, y_lo)]
                with pe.Fori(0, HP) as r:
                    after(pe, s_whi, r, 1)
                    after(pe, s_wlo, r, 1)
                    after(pe, s_lo, r - 1, 6)
                    for n, (w, x, k) in enumerate(steps()):
                        mm = nc.tensor.matmul(k_ps[:], w[0:kw[k], k, 0], x[0:kw[k], k], start=(n == 0), stop=(n == 5))
                    mm.then_inc(s_k.sem, 1)
                    for j in range(ct):
                        for n, (w, x, k) in enumerate(steps()):
                            mm = nc.tensor.matmul(v_ps[:, j], x[0:kw[k], k, j * P:(j + 1) * P], w[0:kw[k], k, 1],
                                                  start=(n == 0), stop=(n == 5))
                    mm.then_inc(s_v.sem, 1)


def phase_cross_attention(nc, io, keep, sem, kv_dram, o_dram):
    with ExitStack() as ctx:
        sb = lambda n, s, d: ctx.enter_context(nc.sbuf_tensor(f"ca_{n}", s, d))
        ps = lambda n, s, d: ctx.enter_context(nc.psum_tensor(f"ca_{n}", s, d))
        w_raw = sb("w_raw", [P, KD, P], F32)
        w_hi = sb("w_hi", [P, KD, P], F32R)
        w_lo = sb("w_lo", [P, KD, P], F32R)
        cos = sb("cos", [P, N], F32)
        sin = sb("sin", [P, N], F32)
        z = sb("q_rows", [P, N], F32)
        z_swap = sb("q_swapped", [P, N], F32)
        q_hi = [sb(f"q_hi{u}", [P, N], F32R) for u in range(2)]
        q_lo = [sb(f"q_lo{u}", [P, N], F32R) for u in range(2)]
        kv = [sb(f"kv{u}", [P, 4, P], F32R) for u in range(2)]
        row_max = sb("row_max", [P, 2, KT], F32)
        neg_max = sb("neg_max", [2 * KT, KT, P], F32R)
        heads_raw = sb("heads_raw", [2 * KT, P], F32)
        heads = sb("heads", [2 * KT, P], F32R)
        ones_raw = sb("ones_raw", [P, P], F32)
        ones = sb("ones", [P, P], F32R)
        probs = sb("probs", [P, N], F32)
        p_hi = sb("p_hi", [P, N], F32R)
        p_lo = sb("p_lo", [P, N], F32R)
        inv_sum = sb("inv_sum", [P, N], F32)
        o_sb = sb("o_sb", [P, N], F32)
        work = ps("work", [P, N], F32)
        scores = ps("scores", [P, N], F32)
        o_ps = ps("o_ps", [P, N], F32)
        sum_ps = ps("sum_ps", [P, N], F32)

        s_in, s_const, s_carrier = (sem(f"ca_{n}") for n in ("in", "const", "carrier"))
        s_w = Counter(sem("ca_w"), 1, 16)
        s_whi = Counter(sem("ca_whi"), 1)
        s_wlo = Counter(sem("ca_wlo"), 1)
        s_proj = Counter(sem("ca_proj"), 2)
        s_evac = Counter(sem("ca_evac"), 2)
        s_swap = Counter(sem("ca_swap"), 4, 16)
        s_sin = Counter(sem("ca_sin"), 1)
        s_rope = Counter(sem("ca_rope"), 2)
        s_hi = Counter(sem("ca_hi"), 1)
        s_lo = Counter(sem("ca_lo"), 1)
        s_kv = [Counter(sem(f"ca_kv{u}"), 1, 16) for u in range(2)]
        s_max = Counter(sem("ca_max"), 2)
        s_mred = Counter(sem("ca_mred"), 2)
        s_turn = Counter(sem("ca_turn"), 1)
        s_shift = Counter(sem("ca_shift"), 1)
        s_score = Counter(sem("ca_score"), 1, start=2)
        s_exp = Counter(sem("ca_exp"), 2, start=4)
        s_plo = Counter(sem("ca_plo"), 1, start=2)
        s_pv = Counter(sem("ca_pv"), 2, start=4)
        s_inv = Counter(sem("ca_inv"), 1, start=2)
        s_out = Counter(sem("ca_out"), 1, start=2)
        s_store = Counter(sem("ca_store"), 1, 16, start=32)
        halves = [slice(i * HALF, (i + 1) * HALF) for i in range(2)]
        pair_kv = lambda u: [kv[u][:, n] for n in range(4)]

        with nc.Block() as block:
            @block.sync
            def _(sp):
                for dst, src in ((cos[:], io["cos"]), (sin[:], io["sin"]), (heads_raw[:], io["heads"]),
                                 (ones_raw[:], io["ones_block"])):
                    sp.dma_start(dst, src).then_inc(s_in, 16)
                for u in range(2):
                    sp.dma_start(as_f32(kv[u][:].rearrange("p f n -> p (f n)")), kv_dram[u]).then_inc(s_kv[u].sem, 16)
                sp.dma_start(w_raw[:], io["w_cross"][0]).then_inc(s_w.sem, 16)

                def swap(r, first=False):
                    after_sp(sp, s_evac, r, 2, keep.s_carrier)
                    if not first:
                        after_sp(sp, s_rope, r - 1, 2, keep.s_carrier)
                    for q in range(4):
                        sp.dma_start(z_swap[32 * q:32 * q + 32], z[32 * (q ^ 1):32 * (q ^ 1) + 32]) \
                          .then_inc(s_swap.sem, 16)

                def weights(r):
                    after_sp(sp, s_whi, r - 1, 1, keep.s_carrier)
                    after_sp(sp, s_wlo, r - 1, 1, keep.s_carrier)
                    src = io["w_cross"][bass.ds((r // B) % HP, 1)].rearrange("o p k m -> (o p) k m")
                    sp.dma_start(w_raw[:], src).then_inc(s_w.sem, 16)

                weights(1)
                swap(0, first=True)
                weights(2)
                swap(1)
                with sp.Fori(0, PAIRS // 2) as i:
                    for u in range(2):
                        t = 2 * i + u
                        swap(t + 2)
                        weights(t + 3)
                        after_sp(sp, s_out, t, 1, keep.s_carrier)
                        sp.dma_start(o_dram[bass.ds(t, 1)].rearrange("o p n -> (o p) n"), o_sb[:]) \
                          .then_inc(s_store.sem, 16)
                        after_sp(sp, s_pv, t, 2, keep.s_carrier)
                        sp.dma_start(as_f32(kv[u][:].rearrange("p f n -> p (f n)")),
                                     kv_dram[bass.ds((t + 2) % PAIRS, 1)].rearrange("o p n -> (o p) n")) \
                          .then_inc(s_kv[u].sem, 16)
                after_sp(sp, s_store, PAIRS - 1, 1, keep.s_carrier)
                after_sp(sp, s_w, PAIRS + 2, 1, keep.s_carrier)
                for u in range(2):
                    after_sp(sp, s_kv[u], PAIRS // 2, 1, keep.s_carrier)

            @block.gpsimd
            def _(pool):
                pool.sem_inc(s_store.sem, 32)
                pool.wait_ge(s_in, 64)
                with pool.Fori(0, PAIRS + 2) as r:
                    after(pool, s_swap, r, 4)
                    nc.gpsimd.tensor_tensor(z_swap[:], z_swap[:], sin[:], ALU.mult).then_inc(s_sin.sem, 1)

            @block.tensor
            def _(pe):
                pe.sem_inc(s_score.sem, 2)
                pe.sem_inc(s_pv.sem, 4)
                pe.wait_ge(s_const, 2)

                def queries(r):
                    after(pe, s_whi, r, 1)
                    after(pe, s_wlo, r, 1)
                    for i in range(2):
                        steps = [(w, x, k) for k in range(KD) for w, x in split_products(w_hi, w_lo, keep.xt_hi, keep.xt_lo)]
                        for n, (w, x, k) in enumerate(steps):
                            cols = bass.ds((r % B) * N + i * HALF, HALF)
                            mm = nc.tensor.matmul(work[:, halves[i]], w[:, k], x[:, k, cols], start=(n == 0),
                                                  stop=(n == len(steps) - 1))
                        mm.then_inc(s_proj.sem, 1)

                def maxima(r, u, kv_round):
                    after(pe, s_kv[u], kv_round, 1)
                    after(pe, s_hi, r, 1)
                    for qt in range(KT):
                        mm = nc.tensor.matmul(work[:, qt * P:(qt + 1) * P], q_hi[u][:, qt * P:(qt + 1) * P], pair_kv(u)[0],
                                              start=True, stop=True)
                        if qt % 4 == 3:
                            mm.then_inc(s_max.sem, 1)

                def turn(r):
                    after(pe, s_mred, r, 2)
                    after(pe, s_exp, r - 1, 2)
                    nc.tensor.transpose(scores[0:2 * KT, 0:P], row_max[:].rearrange("p h q -> p (h q)"),
                                        keep.ident[:]).then_inc(s_turn.sem, 1)

                def score(r, u):
                    after(pe, s_shift, r, 1)
                    after(pe, s_lo, r, 1)
                    k_hi, k_lo = pair_kv(u)[:2]
                    for i in range(2):
                        sh = neg_max[:].rearrange("r a q -> r (a q)")[:, halves[i]]
                        steps = [(k_hi, q_hi[u][:, halves[i]]), (k_hi, q_lo[u][:, halves[i]]),
                                 (k_lo, q_hi[u][:, halves[i]]), (heads[:], sh)]
                        for n, (a, b) in enumerate(steps):
                            mm = nc.tensor.matmul(scores[:, halves[i]], a, b, start=(n == 0), stop=(n == 3))
                    mm.then_inc(s_score.sem, 1)

                def outputs(r, u):
                    after(pe, s_exp, r, 2)
                    after(pe, s_plo, r, 1)
                    after(pe, s_inv, r - 1, 1)
                    v_hi, v_lo = pair_kv(u)[2:]
                    for i in range(2):
                        for n, p in enumerate((p_hi, p_lo)):
                            mm = nc.tensor.matmul(sum_ps[:, halves[i]], ones[:], p[:, halves[i]], start=(n == 0),
                                                  stop=(n == 1))
                    mm.then_inc(s_pv.sem, 1)
                    after(pe, s_out, r - 1, 1)
                    for i in range(2):
                        steps = split_products(v_hi, v_lo, p_hi[:, halves[i]], p_lo[:, halves[i]])
                        for n, (a, b) in enumerate(steps):
                            mm = nc.tensor.matmul(o_ps[:, halves[i]], a, b, start=(n == 0), stop=(n == 2))
                    mm.then_inc(s_pv.sem, 1)

                queries(0)
                after(pe, s_evac, 0, 2)
                queries(1)
                after(pe, s_evac, 1, 2)
                maxima(0, 0, 0)
                turn(0)
                with pe.Fori(0, PAIRS // 2) as i:
                    for u in range(2):
                        t = 2 * i + u
                        after(pe, s_mred, t, 2)
                        queries(t + 2)
                        score(t, u)
                        after(pe, s_evac, t + 2, 2)
                        maxima(t + 1, 1 - u, i + u)
                        outputs(t, u)
                        turn(t + 1)

            @block.scalar
            def _(act):
                act.sem_inc(s_exp.sem, 4)
                act.wait_ge(s_in, 64)
                nc.scalar.activation(ones[:], ones_raw[:], ACT.Copy).then_inc(s_const, 1)
                nc.scalar.activation(heads[:], heads_raw[:], ACT.Copy).then_inc(s_const, 1)

                def split_w(r, proj_done=True):
                    after(act, s_w, r, 1)
                    if proj_done:
                        after(act, s_proj, r - 1, 2)
                    nc.scalar.activation(w_hi[:], w_raw[:], ACT.Copy).then_inc(s_whi.sem, 1)

                def evac(r, first=False):
                    for i in range(2):
                        after(act, s_proj, r, i + 1)
                        if i == 0 and not first:
                            after(act, s_lo, r - 1, 1)
                        nc.scalar.activation(z[:, halves[i]], work[:, halves[i]], ACT.Copy).then_inc(s_evac.sem, 1)

                def high_half(r, u):
                    after(act, s_rope, r, 2)
                    after(act, s_score, r - 2, 1)
                    nc.scalar.activation(q_hi[u][:], z[:], ACT.Copy).then_inc(s_hi.sem, 1)

                split_w(0, proj_done=False)
                evac(0, first=True)
                split_w(1)
                high_half(0, 0)
                evac(1)
                split_w(2)
                high_half(1, 1)
                with act.Fori(0, PAIRS // 2) as i:
                    for u in range(2):
                        t = 2 * i + u
                        evac(t + 2)
                        split_w(t + 3)
                        after(act, s_score, t, 1)
                        after(act, s_plo, t - 1, 1)
                        nc.scalar.activation(probs[:], scores[:], ACT.Exp, scale=SCALE).then_inc(s_exp.sem, 1)
                        after(act, s_pv, t - 1, 2)
                        nc.scalar.activation(p_hi[:], scores[:], ACT.Exp, scale=SCALE).then_inc(s_exp.sem, 1)
                        high_half(t + 2, u)

            @block.vector
            def _(dve):
                dve.sem_inc(s_plo.sem, 2)
                dve.sem_inc(s_inv.sem, 2)
                dve.sem_inc(s_out.sem, 2)
                dve.wait_ge(s_in, 64)

                def lo_w(r):
                    after(dve, s_whi, r, 1)
                    nc.vector.tensor_tensor(w_lo[:], w_raw[:], as_f32(w_hi[:]), ALU.subtract).then_inc(s_wlo.sem, 1)

                def rope(r):
                    after(dve, s_evac, r, 2)
                    after(dve, s_swap, r, 4)
                    nc.vector.tensor_tensor(z[:], z[:], cos[:], ALU.mult).then_inc(s_rope.sem, 1)
                    after(dve, s_rope, r, 1)
                    after(dve, s_sin, r, 1)
                    nc.vector.tensor_tensor(z[:], z[:], z_swap[:], ALU.add).then_inc(s_rope.sem, 1)

                def low_half(r, u):
                    after(dve, s_hi, r, 1)
                    nc.vector.tensor_tensor(q_lo[u][:], z[:], as_f32(q_hi[u][:]), ALU.subtract).then_inc(s_lo.sem, 1)

                def reduce(r, first=False):
                    if not first:
                        after(dve, s_turn, r - 1, 1)
                    for i in range(2):
                        after(dve, s_max, r, i + 1)
                        dst = row_max[:].rearrange("p h q -> p q h")[:, 4 * i:4 * i + 4]
                        nc.vector.tensor_reduce(dst, work[:, halves[i]].rearrange("p (q h m) -> p q h m", h=2, m=M), AX.X,
                                                ALU.max).then_inc(s_mred.sem, 1)

                def shift(r):
                    after(dve, s_turn, r, 1)
                    after(dve, s_score, r - 1, 1)
                    turned = scores[0:2 * KT, 0:P].unsqueeze(1).to_broadcast([2 * KT, KT, P])
                    nc.vector.tensor_tensor(neg_max[:], turned, keep.neg_block[:], ALU.mult).then_inc(s_shift.sem, 1)

                lo_w(0)
                rope(0)
                lo_w(1)
                low_half(0, 0)
                rope(1)
                lo_w(2)
                low_half(1, 1)
                reduce(0, first=True)
                shift(0)
                with dve.Fori(0, PAIRS // 2) as i:
                    for u in range(2):
                        t = 2 * i + u
                        reduce(t + 1)
                        lo_w(t + 3)
                        after(dve, s_exp, t, 2)
                        after(dve, s_pv, t - 1, 2)
                        nc.vector.tensor_tensor(p_lo[:], probs[:], as_f32(p_hi[:]), ALU.subtract).then_inc(s_plo.sem, 1)
                        rope(t + 2)
                        after(dve, s_pv, t, 1)
                        after(dve, s_out, t - 1, 1)
                        nc.vector.reciprocal(inv_sum[:], sum_ps[:]).then_inc(s_inv.sem, 1)
                        shift(t + 1)
                        low_half(t + 2, u)
                        after(dve, s_inv, t, 1)
                        after(dve, s_pv, t, 2)
                        after(dve, s_store, t - 1, 1)
                        nc.vector.tensor_tensor(o_sb[:], o_ps[:], inv_sum[:], ALU.mult).then_inc(s_out.sem, 1)

def phase_feed_forward(nc, io, keep, sem, out):
    tiles, ring, skew = F // P, 4, 2
    with ExitStack() as ctx:
        sb = lambda n, s, d: ctx.enter_context(nc.sbuf_tensor(f"ff_{n}", s, d))
        ps = lambda n, s, d: ctx.enter_context(nc.psum_tensor(f"ff_{n}", s, d))
        w1_raw = sb("w1_raw", [P, KD, F], F32)
        w1_hi = sb("w1_hi", [P, KD, F], F32R)
        w1_lo = sb("w1_lo", [P, KD, F], F32R)
        w2_raw = sb("w2_raw", [P, tiles, D], F32)
        w2_hi = sb("w2_hi", [P, tiles, D], F32R)
        w2_lo = sb("w2_lo", [P, tiles, D], F32R)
        b1 = sb("b1", [P, tiles], F32)
        bias_row = sb("bias", [P, D], F32)
        hidden = sb("hidden", [P, ring, HALF], F32)
        h_hi = sb("h_hi", [P, ring, HALF], F32R)
        h_lo = sb("h_lo", [P, ring, HALF], F32R)
        x_bias = sb("x_bias", [P, GT, D], F32)
        out_sb = sb("out_sb", [P, GT, D], F32)
        h_ps = [ps(f"h_ps{i}", [P, HALF], F32) for i in range(ring)]
        acc = [ps(f"acc{j}", [P, HALF], F32) for j in range(GT)]
        s_w = sem("ff_w")
        s_w_hi = sem("ff_w_hi")
        s_w_lo = sem("ff_w_lo")
        s_carrier = sem("ff_carrier")
        s_hmm = Counter(sem("ff_hmm"), tiles)
        s_gelu = Counter(sem("ff_gelu"), tiles, start=tiles)
        s_hi = Counter(sem("ff_hi"), tiles)
        s_lo = Counter(sem("ff_lo"), tiles, start=tiles)
        s_mm = Counter(sem("ff_mm"), tiles, start=tiles)
        s_xb = Counter(sem("ff_xb"), GT)
        s_out = Counter(sem("ff_out"), GT, start=GT)
        s_store = Counter(sem("ff_store"), 1, 16, start=0)
        out_d = out.rearrange("(g j p) d -> g p j d", p=P, j=GT)

        def before(g, i, back):
            return (g, i - back + 1) if i >= back else (g - 1, i - back + 1 + tiles)

        with nc.Block() as block:
            @block.sync
            def _(sp):
                sp.dma_start(w1_raw[:], io["ff_w1"].rearrange("(k p) f -> p k f", p=P)).then_inc(s_w, 16)
                sp.dma_start(w2_raw[:], io["ff_w2"].rearrange("(i p) d -> p i d", p=P)).then_inc(s_w, 16)
                sp.dma_start(b1[:], io["ff_b1"]).then_inc(s_w, 16)
                sp.dma_start(bias_row[:], io["ff_b2"].partition_broadcast(P)).then_inc(s_w, 16)
                with sp.Fori(0, GROUPS) as g:
                    after_sp(sp, s_out, g, GT, keep.s_carrier)
                    sp.dma_start(out_d[bass.ds(g, 1)].rearrange("o p j d -> (o p) j d"), out_sb[:]) \
                      .then_inc(s_store.sem, 16)
                after_sp(sp, s_store, GROUPS - 1, 1, keep.s_carrier)

            @block.gpsimd
            def _(pool):
                pool.wait_ge(s_w, 64)
                with pool.Fori(0, GROUPS) as g:
                    after(pool, s_out, g - 1, GT)
                    for j in range(GT):
                        src = keep.x[:, bass.ds(g * GT + j, 1)].rearrange("p o d -> p (o d)")
                        nc.gpsimd.tensor_tensor(x_bias[:, j], src, bias_row[:], ALU.add).then_inc(s_xb.sem, 1)

            @block.scalar
            def _(act):
                act.sem_inc(s_gelu.sem, tiles)
                act.wait_ge(s_w, 64)
                nc.scalar.activation(w1_hi[:], w1_raw[:], ACT.Copy).then_inc(s_w_hi, 1)
                nc.scalar.activation(w2_hi[:], w2_raw[:], ACT.Copy).then_inc(s_w_hi, 1)
                with act.Fori(0, GROUPS) as g:
                    for i in range(tiles):
                        after(act, s_lo, *before(g, i, ring))
                        after(act, s_hmm, g, i + 1)
                        nc.scalar.activation(hidden[:, i % ring], h_ps[i % ring][:], ACT.Gelu, bias=b1[:, i:i + 1]) \
                          .then_inc(s_gelu.sem, 1)
                        after(act, s_mm, *before(g, i, ring))
                        after(act, s_gelu, g, i + 1)
                        nc.scalar.activation(h_hi[:, i % ring], hidden[:, i % ring], ACT.Copy).then_inc(s_hi.sem, 1)

            @block.tensor
            def _(pe):
                pe.sem_inc(s_mm.sem, tiles)
                pe.wait_ge(s_w_hi, 2)
                pe.wait_ge(s_w_lo, 2)

                def hidden_products(g, i):
                    after(pe, s_gelu, *before(g, i, ring))
                    cols = bass.ds(g * HALF, HALF)
                    steps = [(w, x, k) for k in range(KD) for w, x in split_products(w1_hi, w1_lo, keep.xt_hi, keep.xt_lo)]
                    for n, (w, x, k) in enumerate(steps):
                        mm = nc.tensor.matmul(h_ps[i % ring][:], w[:, k, i * P:(i + 1) * P], x[:, k, cols],
                                              start=(n == 0), stop=(n == len(steps) - 1))
                    mm.then_inc(s_hmm.sem, 1)

                def out_products(g, i):
                    after(pe, s_hi, g, i + 1)
                    after(pe, s_lo, g, i + 1)
                    if i == 0:
                        after(pe, s_out, g - 1, GT)
                    for j in range(GT):
                        for n, (h, w) in enumerate(split_products(h_hi, h_lo, w2_hi, w2_lo)):
                            mm = nc.tensor.matmul(acc[j][:, 0:D], h[:, i % ring, j * P:(j + 1) * P], w[:, i],
                                                  start=(i == 0 and n == 0), stop=(i == tiles - 1 and n == 2))
                    mm.then_inc(s_mm.sem, 1)

                def group(g, first=False):
                    for i in range(tiles):
                        hidden_products(g, i)
                        if i >= skew:
                            out_products(g, i - skew)
                        elif not first:
                            out_products(g - 1, i - skew + tiles)

                group(0, first=True)
                with pe.Fori(1, GROUPS) as g:
                    group(g)
                for i in range(tiles - skew, tiles):
                    out_products(GROUPS - 1, i)

            @block.vector
            def _(dve):
                dve.sem_inc(s_lo.sem, tiles)
                dve.sem_inc(s_out.sem, GT)
                for n, (raw, hi, lo) in enumerate(((w1_raw, w1_hi, w1_lo), (w2_raw, w2_hi, w2_lo))):
                    dve.wait_ge(s_w_hi, n + 1)
                    nc.vector.tensor_tensor(lo[:], raw[:], as_f32(hi[:]), ALU.subtract).then_inc(s_w_lo, 1)

                def low_halves(g, i):
                    after(dve, s_hi, g, i + 1)
                    nc.vector.tensor_tensor(h_lo[:, i % ring], hidden[:, i % ring], as_f32(h_hi[:, i % ring]),
                                            ALU.subtract).then_inc(s_lo.sem, 1)

                def sums(g, stored):
                    after(dve, s_mm, g, tiles)
                    after(dve, s_xb, g, GT)
                    if stored:
                        after(dve, s_store, g - 1, 1)
                    for j in range(GT):
                        nc.vector.tensor_tensor(out_sb[:, j], acc[j][:, 0:D], x_bias[:, j], ALU.add) \
                          .then_inc(s_out.sem, 1)

                def group(g, last_sums):
                    for i in range(tiles):
                        low_halves(g, i)
                        if i == skew:
                            last_sums()

                group(0, lambda: None)
                group(1, lambda: sums(0, False))
                with dve.Fori(2, GROUPS) as g:
                    group(g, lambda: sums(g - 1, True))
                sums(GROUPS - 1, True)

class Keep:
    pass


ROPE_ORDER = np.concatenate([np.arange(0, DH, 2), np.arange(1, DH, 2)])


def build(nc, io, out):
    with ExitStack() as used:
        sem = lambda name: used.enter_context(nc.semaphore("s_" + name))
        sb = lambda n, s, d: used.enter_context(nc.sbuf_tensor(n, s, d))
        keep = Keep()
        keep.s_carrier = sem("sp_carrier")
        keep.ident = sb("ident_sb", [P, P], F32)
        keep.neg_block = sb("neg_block_sb", [2 * KT, KT, P], F32)
        keep.mod_a = sb("mod_a", [P, 2, KD, B], F32)
        keep.mod_c = sb("mod_c", [P, 2, KD, B], F32)
        keep.xt_hi = sb("xt_hi", [P, KD, TOK], F32R)
        keep.xt_lo = sb("xt_lo", [P, KD, TOK], F32R)
        o_self = nc.dram_tensor("o_self", [PAIRS + 2, P, N], F32, kind="Internal").ap()
        o_cross = nc.dram_tensor("o_cross", [PAIRS, P, N], F32, kind="Internal").ap()
        kv_ctx = nc.dram_tensor("kv_ctx", [PAIRS, P, 4 * P], F32, kind="Internal").ap()
        phase_setup(nc, io, keep, sem)
        phase_first_norm(nc, io, keep, sem)
        phase_self_attention(nc, io, keep, sem, o_self)
        keep.x = sb("x_rows", [P, TOK // P, D], F32)
        phase_project(nc, io, keep, sem, "po", o_self[2:PAIRS + 2], "sa_wo", "sa_bo", 0)
        phase_context(nc, io, keep, sem, kv_ctx)
        phase_cross_attention(nc, io, keep, sem, kv_ctx, o_cross)
        phase_project(nc, io, keep, sem, "pc", o_cross, "ca_wo", "ca_bo", 1)
        phase_feed_forward(nc, io, keep, sem, out)

def table(positions):
    f32 = np.float32
    inv = (f32(1.0) / np.power(f32(10000.0), np.arange(0, DH, 2, dtype=f32) / f32(DH))).astype(f32)
    ang = (inv[:, None] * np.arange(positions, dtype=f32)[None, :]).astype(f32)
    c, s = np.cos(ang).astype(f32), np.sin(ang).astype(f32)
    return np.ascontiguousarray(np.tile(c, (4, 1))), np.ascontiguousarray(np.concatenate([-s, s, -s, s]))


def layouts(inputs):
    get = lambda n: np.asarray(inputs["L0_xcond_" + n])
    cols = lambda v: v.reshape(KD, P).T
    order = (np.arange(H)[:, None] * DH + ROPE_ORDER[None, :]).reshape(-1)
    block = np.zeros((16, KT, P), np.float32)
    for r in range(16):
        block[r, r % KT] = -1.0
    cos, sin = table(N)
    pair = lambda w: w.reshape(w.shape[0], HP, P)
    wkv = get("sa_wkv")
    w_self = np.stack([pair(get("sa_wq")[:, order]), pair(wkv[:, :MID][:, order]), pair(wkv[:, MID:])], 2)
    w_self = w_self.reshape(KD, P, HP, 3, P).transpose(2, 1, 0, 3, 4)
    heads = np.zeros((2 * KT, P), np.float32)
    ones = np.zeros((P, P), np.float32)
    for h in range(2):
        heads[h * KT:(h + 1) * KT, h * M:(h + 1) * M] = 1.0
        ones[h * M:(h + 1) * M, h * DH:(h + 1) * DH] = 1.0
    ckv = get("ca_wkv")
    pad = np.zeros((2 * P, HP, 2, P), np.float32)
    pad[:DC] = np.stack([pair(ckv[:, :MID][:, order]), pair(ckv[:, MID:])], 2)
    vec_pad = lambda v: np.concatenate([v, np.zeros(2 * P - DC, np.float32)])
    vecs = [get(n) for n in ("ln1_w", "ln1_b", "ln2_w", "ln2_b", "g1_b", "b1_b", "g2_b", "b2_b")]
    arrays = {
        "x": np.asarray(inputs["x"]).reshape(TOK, D),
        "cond": np.asarray(inputs["cond_1024"]).reshape(B, KD, P).transpose(2, 1, 0).reshape(P, KD * B),
        "gate_vec": np.stack([cols(v) for v in vecs], 1).reshape(P, -1),
        "gate_w0": get("g1_w"), "gate_w1": get("b1_w"), "gate_w2": get("g2_w"), "gate_w3": get("b2_w"),
        "ident": np.eye(P, dtype=np.float32), "neg_block": block.reshape(16, KT * P), "cos": cos, "sin": sin,
        "w_self": w_self, "heads": heads, "ones_block": ones,
        "w_ctx": pad.reshape(2, P, HP, 2, P).transpose(2, 1, 0, 3, 4),
        "w_cross": pair(get("ca_wq")[:, order]).reshape(KD, P, HP, P).transpose(2, 1, 0, 3),
        "ctx": np.asarray(inputs["ctx_768"]).reshape(B * M, DC),
        "lnc_w": cols(vec_pad(get("ca_lnc_w"))), "lnc_b": cols(vec_pad(get("ca_lnc_b"))),
        "sa_wo": get("sa_wo"), "sa_bo": get("sa_bo"), "ca_wo": get("ca_wo"), "ca_bo": get("ca_bo"),
        "ff_w1": get("ff_w1"), "ff_b1": get("ff_b1").reshape(F // P, P).T, "ff_w2": get("ff_w2"),
        "ff_b2": get("ff_b2"),
    }
    return {n: np.ascontiguousarray(a) for n, a in arrays.items()}



def kernel(**inputs):
    import concourse.bacc as bacc
    from concourse.bass_utils import run_bass_kernel_spmd

    nc = bacc.Bacc("TRN2", target_bir_lowering=False, num_devices=1)
    arrays = {f"in_{n}": a for n, a in layouts(inputs).items()}
    io = {n[3:]: nc.dram_tensor(n, a.shape, mybir.dt.from_np(a.dtype), kind="ExternalInput").ap()
          for n, a in arrays.items()}
    out = nc.dram_tensor("out_rows", (TOK, D), F32, kind="ExternalOutput").ap()
    build(nc, io, out)
    result = run_bass_kernel_spmd(nc, [arrays], core_ids=[0])
    return result.results[0]["out_rows"].reshape(B, N, D)
```

```python
from contextlib import ExitStack

import numpy as np

import concourse.bass as bass
from concourse import mybir

F32 = mybir.dt.float32
F32R = mybir.dt.float32r
ALU = mybir.AluOpType
ACT = mybir.ActivationFunctionType
AX = mybir.AxisListType

P = 128
B, N, D = 4, 1024, 256
H, DH = 16, 64
MID = H * DH
M, DC = 64, 192
F = 4 * D
KD = D // P
HP = H // 2
PAIRS = HP * B
KT = N // P
HALF = 512
TOK = B * N
GROUPS = TOK // HALF
GT = HALF // P
EPS = 1e-5
SCALE = DH ** -0.5
PREP_JOBS = 44


class Counter:

    def __init__(self, sem, per_round, step=1, start=0):
        self.sem, self.per, self.step, self.start = sem, per_round, step, start

    def at(self, r, n):
        return (r * self.per + n) * self.step + self.start


def after(eng, counter, r, n):
    eng.wait_ge(counter.sem, counter.at(r, n))


def after_sp(sp, counter, r, n, carrier):
    sp.wait_ge(counter.sem, counter.at(r, n))
    sp.sem_inc(carrier, 1)


def split_products(hi_a, lo_a, hi_b, lo_b):
    return ((hi_a, hi_b), (hi_a, lo_b), (lo_a, hi_b))


def as_f32(ap):
    return ap.bitcast(F32)


class Layernorm:

    def __init__(self, nc, sb, ps, sem, name, carrier):
        self.stats = sb(f"{name}_stats", [P, GT, 6], F32)
        self.moments = sb(f"{name}_moments", [P, GT, 2], F32)
        self.var_eps = sb(f"{name}_var_eps", [P, GT], F32)
        self.rstd = sb(f"{name}_rstd", [P, GT], F32)
        self.minus_half = sb(f"{name}_minus_half", [P, GT], F32)
        self.xn = sb(f"{name}_xn", [P, GT, D], F32)
        self.y = sb(f"{name}_y", [P, KD, HALF], F32)
        self.turned = [ps(f"{name}_turned{k}", [P, HALF], F32) for k in range(KD)]
        self.s_half = sem(f"{name}_half")
        self.s_carrier = carrier
        self.s_stat = Counter(sem(f"{name}_stat"), GT)
        self.s_mom = Counter(sem(f"{name}_mom"), GT)
        self.s_var = Counter(sem(f"{name}_var"), 1)
        self.s_rstd = Counter(sem(f"{name}_rstd"), 1)
        self.s_xn = Counter(sem(f"{name}_xn"), GT, start=GT)
        self.s_turned = Counter(sem(f"{name}_turned"), KD, start=KD)
        self.s_mod = Counter(sem(f"{name}_mod"), 2 * KD, start=2 * KD)
        self.s_lo = Counter(sem(f"{name}_lo"), KD, start=KD)

    def start_dve(self, nc, dve):
        nc.vector.memset(self.minus_half[:], -0.5).then_inc(self.s_half, 1)
        dve.sem_inc(self.s_xn.sem, GT)
        dve.sem_inc(self.s_lo.sem, KD)

    def start_pe(self, pe):
        pe.sem_inc(self.s_turned.sem, KD)

    def start_act(self, act):
        act.sem_inc(self.s_mod.sem, 2 * KD)


def phase_setup(nc, io, keep, sem):
    with ExitStack() as ctx:
        sb = lambda n, s, d: ctx.enter_context(nc.sbuf_tensor(n, s, d))
        ps = lambda n, s, d: ctx.enter_context(nc.psum_tensor(n, s, d))
        cond = sb("cond", [P, KD, B], F32)
        gw = sb("gate_weights", [P, 4, KD, D], F32)
        vec = sb("gate_vectors", [P, 8, KD], F32)
        gate = sb("gates", [P, 4, KD, B], F32)
        gate_ps = ps("gate_ps", [P, 4, KD, B], F32)
        s_in, s_mm, s_g, s_f, s_h = (sem(f"setup_{n}") for n in ("in", "mm", "g", "f", "h"))
        loads = [(keep.ident[:], io["ident"]), (keep.neg_block[:], io["neg_block"].rearrange("p (a q) -> p a q", q=P)),
                 (cond[:], io["cond"].rearrange("p (k b) -> p k b", b=B)),
                 (vec[:], io["gate_vec"].rearrange("p (v k) -> p v k", k=KD))]
        loads += [(gw[:, n], io[f"gate_w{n}"].rearrange("(k p) d -> p k d", p=P)) for n in range(4)]
        with nc.Block() as block:
            @block.sync
            def _(sp):
                for dst, src in loads:
                    sp.dma_start(dst, src).then_inc(s_in, 16)

            @block.tensor
            def _(pe):
                pe.wait_ge(s_in, 16 * len(loads))
                for n in range(4):
                    for k_out in range(KD):
                        for k in range(KD):
                            mm = nc.tensor.matmul(gate_ps[:, n, k_out], gw[:, n, k, k_out * P:(k_out + 1) * P],
                                                  cond[:, k], start=(k == 0), stop=(k == KD - 1))
                mm.then_inc(s_mm, 1)

            @block.vector
            def _(dve):
                dve.wait_ge(s_in, 16 * len(loads))
                dve.wait_ge(s_mm, 1)
                for n in range(4):
                    for k in range(KD):
                        last = nc.vector.tensor_scalar(gate[:, n, k], gate_ps[:, n, k], vec[:, 4 + n, k:k + 1],
                                                       1.0 if n % 2 == 0 else 0.0, ALU.add, ALU.add)
                last.then_inc(s_g, 1)
                dve.wait_ge(s_g, 1)
                for m in range(2):
                    for k in range(KD):
                        nc.vector.tensor_scalar(keep.mod_a[:, m, k], gate[:, 2 * m, k], vec[:, 2 * m, k:k + 1], None,
                                                ALU.mult).then_inc(s_f, 1)
                        nc.vector.scalar_tensor_tensor(out=keep.mod_c[:, m, k], in0=gate[:, 2 * m, k],
                                                       scalar=vec[:, 2 * m + 1, k:k + 1], in1=gate[:, 2 * m + 1, k],
                                                       op0=ALU.mult, op1=ALU.add).then_inc(s_f, 1)


def dve_norm(nc, dve, ln, x_tile, g):
    for j in range(GT):
        nc.vector.bn_stats(ln.stats[:, j], x_tile(j)).then_inc(ln.s_stat.sem, 1)
    after(dve, ln.s_xn, g - 1, GT)
    for j in range(GT):
        after(dve, ln.s_stat, g, j + 1)
        dve.sem_inc(ln.s_carrier, 1)
        nc.vector.bn_aggr(ln.moments[:, j], ln.stats[:, j]).then_inc(ln.s_mom.sem, 1)
    after(dve, ln.s_mom, g, GT)
    nc.vector.tensor_scalar(ln.var_eps[:], ln.moments[:, :, 1], EPS, None, ALU.add).then_inc(ln.s_var.sem, 1)
    after(dve, ln.s_rstd, g, 1)
    after(dve, ln.s_turned, g - 1, KD)
    for j in range(GT):
        nc.vector.tensor_scalar(ln.xn[:, j], x_tile(j), ln.moments[:, j, 0:1], ln.rstd[:, j:j + 1],
                                ALU.subtract, ALU.mult).then_inc(ln.s_xn.sem, 1)


def pool_rstd(nc, pool, ln, g):
    after(pool, ln.s_var, g, 1)
    nc.gpsimd.tensor_tensor(ln.rstd[:], ln.var_eps[:], ln.minus_half[:], ALU.pow).then_inc(ln.s_rstd.sem, 1)


def pe_turn(nc, pe, ln, ident, g):
    after(pe, ln.s_mod, g - 1, 2 * KD)
    for k in range(KD):
        for j in range(GT):
            if k == 0:
                after(pe, ln.s_xn, g, j + 1)
            mm = nc.tensor.transpose(ln.turned[k][:, j * P:(j + 1) * P], ln.xn[:, j, k * P:(k + 1) * P], ident)
        mm.then_inc(ln.s_turned.sem, 1)


def act_modulate(nc, act, ln, keep, m, g):
    batch = g // (N // HALF)
    after(act, ln.s_lo, g - 1, KD)
    for k in range(KD):
        after(act, ln.s_turned, g, k + 1)
        scale = keep.mod_a[:, m, k, bass.ds(batch, 1)]
        bias = keep.mod_c[:, m, k, bass.ds(batch, 1)]
        nc.scalar.activation(ln.y[:, k], ln.turned[k][:], ACT.Identity, scale=scale,
                             bias=bias).then_inc(ln.s_mod.sem, 1)
        nc.scalar.activation(keep.xt_hi[:, k, bass.ds(g * HALF, HALF)], ln.turned[k][:], ACT.Identity, scale=scale,
                             bias=bias).then_inc(ln.s_mod.sem, 1)


def dve_modulated_lo(nc, dve, ln, keep, g):
    for k in range(KD):
        after(dve, ln.s_mod, g, 2 * k + 2)
        cols = bass.ds(g * HALF, HALF)
        nc.vector.tensor_tensor(keep.xt_lo[:, k, cols], ln.y[:, k], as_f32(keep.xt_hi[:, k, cols]),
                                ALU.subtract).then_inc(ln.s_lo.sem, 1)


def phase_first_norm(nc, io, keep, sem):
    with ExitStack() as ctx:
        sb = lambda n, s, d: ctx.enter_context(nc.sbuf_tensor(n, s, d))
        ps = lambda n, s, d: ctx.enter_context(nc.psum_tensor(n, s, d))
        ln = Layernorm(nc, sb, ps, sem, "n1", keep.s_carrier)
        x_sb = sb("x_first", [P, 2, GT, D], F32)
        s_x = [Counter(sem(f"n1_x{u}"), 1, 16) for u in range(2)]
        s_used = Counter(sem("n1_x_used"), 1, start=2)
        x_d = io["x"].rearrange("(g j p) d -> g p j d", p=P, j=GT)
        with nc.Block() as block:
            @block.sync
            def _(sp):
                with sp.Fori(0, GROUPS // 2) as i:
                    for u in range(2):
                        after_sp(sp, s_used, 2 * i + u - 2, 1, keep.s_carrier)
                        sp.dma_start(x_sb[:, u], x_d[2 * i + u]).then_inc(s_x[u].sem, 16)

            @block.vector
            def _(dve):
                ln.start_dve(nc, dve)
                dve.sem_inc(s_used.sem, 2)
                with dve.Fori(0, GROUPS // 2) as i:
                    for u in range(2):
                        g = 2 * i + u
                        after(dve, s_x[u], i, 1)
                        dve_norm(nc, dve, ln, lambda j: x_sb[:, u, j], g)
                        after(dve, ln.s_xn, g, GT)
                        dve.sem_inc(s_used.sem, 1)
                        dve_modulated_lo(nc, dve, ln, keep, g)

            @block.gpsimd
            def _(pool):
                pool.wait_ge(ln.s_half, 1)
                with pool.Fori(0, GROUPS) as g:
                    pool_rstd(nc, pool, ln, g)

            @block.tensor
            def _(pe):
                ln.start_pe(pe)
                with pe.Fori(0, GROUPS) as g:
                    pe_turn(nc, pe, ln, keep.ident[:], g)

            @block.scalar
            def _(act):
                ln.start_act(act)
                with act.Fori(0, GROUPS) as g:
                    act_modulate(nc, act, ln, keep, 0, g)



def phase_self_attention(nc, io, keep, sem, o_dram):
    with ExitStack() as ctx:
        sb = lambda n, s, d: ctx.enter_context(nc.sbuf_tensor(n, s, d))
        ps = lambda n, s, d: ctx.enter_context(nc.psum_tensor(n, s, d))
        w_raw = sb("w_raw", [P, KD, 3, P], F32)
        w_hi = sb("w_hi", [P, KD, 3, P], F32R)
        w_lo = sb("w_lo", [P, KD, 3, P], F32R)
        cos = sb("cos", [P, N], F32)
        sin = sb("sin", [P, N], F32)
        z = [sb("q_rows", [P, N], F32), sb("k_rows", [P, N], F32)]
        z_swap = [sb("q_swapped", [P, N], F32), sb("k_swapped", [P, N], F32)]
        vt = sb("v_turned", [P, N], F32)
        q1 = [sb(f"q_first{u}", [P, 2, N], F32R) for u in range(2)]
        q2 = [sb(f"q_second{u}", [P, 2, N], F32R) for u in range(2)]
        k1 = [sb(f"k_first{u}", [P, 2, N], F32R) for u in range(2)]
        k2 = [sb(f"k_second{u}", [P, 2, N], F32R) for u in range(2)]
        v = [sb(f"v_tokens{u}", [P, KT, P], F32) for u in range(2)]
        maxima = sb("maxima", [P, 2, KT, 2], F32)
        row_max = sb("row_max", [P, 2, KT], F32)
        probs = [[sb(f"probs{h}{i}", [P, N], F32) for i in range(2)] for h in range(2)]
        sums = [sb(f"sums{h}", [P, N], F32) for h in range(2)]
        o_raw = sb("o_raw", [P, N], F32)
        compact = sb("compact_sums", [P, 2 * N // P], F32)
        ones = sb("ones", [P, DH], F32)
        scores = [ps(f"scores{h}", [P, N], F32) for h in range(2)]
        o_ps = ps("o_ps", [P, N], F32)
        work = ps("work", [P, 2, HALF], F32)

        divisor = z_swap[1]
        s_const = sem("sa_const")
        n_const = 12
        s_table = sem("sa_table")
        s_w = Counter(sem("sa_w"), 1, 16)
        s_whi = Counter(sem("sa_whi"), 1)
        s_wlo = Counter(sem("sa_wlo"), 1)
        s_proj, s_proj_read = (Counter(sem(f"sa_{n}"), 6) for n in ("proj", "proj_read"))
        s_vturn, s_vturn_read = (Counter(sem(f"sa_{n}"), 2) for n in ("vturn", "vturn_read"))
        s_max, s_max_read = (Counter(sem(f"sa_{n}"), 4 * KT) for n in ("max", "max_read"))
        s_turn, s_turn_read = (Counter(sem(f"sa_{n}"), 2) for n in ("turn", "turn_read"))
        s_sum, s_sum_read = (Counter(sem(f"sa_{n}"), 2, start=2) for n in ("sum", "sum_read"))
        s_swap = [Counter(sem(f"sa_swap{n}"), 4, 16) for n in range(2)]
        s_sin = Counter(sem("sa_sin"), 2)
        s_rope = Counter(sem("sa_rope"), 4)
        s_qhi = Counter(sem("sa_qhi"), 4)
        s_khi = Counter(sem("sa_khi"), 4)
        s_qlo = Counter(sem("sa_qlo"), 2)
        s_klo = Counter(sem("sa_klo"), 2)
        s_comb = Counter(sem("sa_comb"), 2)
        s_score = Counter(sem("sa_score"), 2 * KT)
        s_exp = Counter(sem("sa_exp"), 2 * KT)
        s_pv = Counter(sem("sa_pv"), KT, start=KT)
        s_acc = Counter(sem("sa_acc"), 2 * (KT - 1), start=2 * (KT - 1))
        s_oraw = Counter(sem("sa_oraw"), 1, start=1)
        s_sum_out = Counter(sem("sa_sum_out"), 2, 16, start=32)
        s_sum_in = Counter(sem("sa_sum_in"), 1, 16, start=16)
        s_recip = Counter(sem("sa_recip"), 1, start=1)
        s_inv_out = Counter(sem("sa_inv_out"), 1, 16, start=16)
        s_inv_in = Counter(sem("sa_inv_in"), 2, 16, start=32)
        s_norm = Counter(sem("sa_norm"), 1, start=2)
        s_store = Counter(sem("sa_store"), 1, 16, start=32)

        heads_max = [[("max", h, i) for i in range(2 * KT)] for h in range(2)]
        order = heads_max[0] + heads_max[1][:2] + [("turn", 0, 0)] + heads_max[1][2:]
        proj = [("proj", zz, half) for zz in range(3) for half in range(2)]
        slots = {(0, 1): [("sum", 0, 0)], (0, 3): [("sum", 0, 1)], (1, 0): [("vturn", 0, 0)], (1, 1): [("vturn", 0, 1)],
                 (6, 5): [("turn", 1, 0)]}
        slots.update({(2 + n // 2, 2 + 3 * (n % 2)): [proj[n]] for n in range(6)})
        free = [(kt, slot) for kt in range(1, 7) for slot in range(6) if (kt, slot) not in slots and (kt, slot) < (6, 4)]
        for n, where in enumerate(free):
            slots[where] = order[n * len(order) // len(free):(n + 1) * len(order) // len(free)]
        jobs = [job for where in sorted(slots) for job in slots[where]]
        assert len(jobs) == PREP_JOBS
        index = {job: n for n, job in enumerate(jobs)}
        sums_d = nc.dram_tensor("sums_d", [2, N], F32, kind="Internal").ap()
        inv_d = nc.dram_tensor("inv_d", [2, N], F32, kind="Internal").ap()
        compact_view = lambda d: d.rearrange("h (a b) -> (h a) b", b=2 * N // P)

        def job_read(eng, t, n):
            if isinstance(t, int) and t < 0 and n < 4:
                after(eng, s_proj_read, 0, 6)
                return
            t, n = (t, n - 2) if n >= 2 else (t - 1, n - 2 + PREP_JOBS)
            kind, h, i = jobs[n]
            read, pair, event = {"sum": (s_sum_read, t - 1, i), "vturn": (s_vturn_read, t + 1, i),
                                 "max": (s_max_read, t + 1, h * 2 * KT + i), "turn": (s_turn_read, t + 1, h),
                                 "proj": (s_proj_read, t + 2, 2 * h + i)}[kind]
            after(eng, read, pair, event + 1)

        def add_index(kt, h):
            return (max(kt, 1) - 1) * 2 + h + 1

        def next_tile(t, kt, u):
            return (t, kt + 1, u) if kt < KT - 1 else (t + 1, 0, 1 - u)

        x_cols = lambda xt, k, b, half: xt[:, k, bass.ds(b * N + half * HALF, HALF)]
        top, bot = slice(0, DH), slice(DH, P)

        with nc.Block() as block:
            @block.sync
            def _(sp):
                wait = lambda counter, r, n: after_sp(sp, counter, r, n, keep.s_carrier)
                sp.dma_start(cos[:], io["cos"]).then_inc(s_table, 16)
                sp.dma_start(sin[:], io["sin"]).then_inc(s_table, 16)
                sp.dma_start(w_raw[:], io["w_self"][0]).then_inc(s_w.sem, 16)

                def swap(n, p, first=False):
                    wait(s_proj_read, p, 2 * n + 2)
                    if not first:
                        wait(s_rope, p - 1, 2 * n + 2)
                    if n == 1 and not isinstance(p, int):
                        wait(s_norm, p - 3, 1)
                    for q in range(4):
                        sp.dma_start(z_swap[n][32 * q:32 * q + 32], z[n][32 * (q ^ 1):32 * (q ^ 1) + 32]) \
                          .then_inc(s_swap[n].sem, 16)

                def weights(p):
                    wait(s_whi, p - 1, 1)
                    wait(s_wlo, p - 1, 1)
                    src = io["w_self"][bass.ds((p // B) % HP, 1)].rearrange("o p k z m -> (o p) k z m")
                    sp.dma_start(w_raw[:], src).then_inc(s_w.sem, 16)

                def divisors(t):
                    wait(s_sum_read, t, 2)
                    for h in range(2):
                        sp.dma_start(sums_d[h:h + 1], divisor[h * DH:h * DH + 1]).then_inc(s_sum_out.sem, 16)
                    wait(s_sum_out, t, 2)
                    sp.dma_start(compact[:], compact_view(sums_d)).then_inc(s_sum_in.sem, 16)
                    wait(s_recip, t, 1)
                    sp.dma_start(compact_view(inv_d), compact[:]).then_inc(s_inv_out.sem, 16)
                    wait(s_inv_out, t, 1)
                    for h in range(2):
                        sp.dma_start(divisor[h * DH:(h + 1) * DH], inv_d[h].partition_broadcast(DH)) \
                          .then_inc(s_inv_in.sem, 16)

                def store(t):
                    wait(s_norm, t, 1)
                    sp.dma_start(o_dram[bass.ds(t + 1, 1)].rearrange("o p n -> (o p) n"), o_raw[:]) \
                      .then_inc(s_store.sem, 16)

                swap(0, 0, first=True)
                swap(1, 0, first=True)
                weights(1)
                swap(0, 1)
                swap(1, 1)
                weights(2)
                with sp.Fori(0, PAIRS // 2) as i:
                    for u in range(2):
                        t = 2 * i + u
                        divisors(t - 1)
                        swap(0, t + 2)
                        swap(1, t + 2)
                        weights(t + 3)
                        store(t - 1)
                divisors(PAIRS - 1)
                store(PAIRS - 1)
                wait(s_store, PAIRS - 1, 1)
                wait(s_w, PAIRS + 2, 1)

            @block.tensor
            def _(pe):
                pe.sem_inc(s_pv.sem, KT)

                def projection(zz, i, p, bank):
                    if (zz, i) == (0, 0):
                        after(pe, s_whi, p, 1)
                        after(pe, s_wlo, p, 1)
                    steps = [(w, x, k) for k in range(KD)
                             for w, x in split_products(w_hi, w_lo, keep.xt_hi, keep.xt_lo)]
                    for m, (w, x, k) in enumerate(steps):
                        mm = nc.tensor.matmul(bank, w[:, k, zz], x_cols(x, k, p % B, i), start=(m == 0),
                                              stop=(m == len(steps) - 1))
                    mm.then_inc(s_proj.sem, 1)

                def column_sums(t, i, n):
                    if i == 0:
                        after(pe, s_acc, t, 2 * (KT - 1))
                    for h in range(2):
                        mm = nc.tensor.matmul(work[h * DH:(h + 1) * DH, n % 2], ones[:],
                                              sums[h][:, i * HALF:(i + 1) * HALF], start=True, stop=True)
                    mm.then_inc(s_sum.sem, 1)

                def run_job(job, t, u):
                    kind, h, i = job
                    n, p = index[job], t + 1
                    job_read(pe, t, n)
                    bank = work[:, n % 2]
                    if kind == "proj":
                        projection(h, i, t + 2, bank)
                    elif kind == "sum":
                        column_sums(t - 1, i, n)
                    elif kind == "vturn":
                        if i == 0:
                            after(pe, s_proj_read, p, 6)
                        for c in range(4):
                            mm = nc.tensor.transpose(work[:, n % 2, c * P:(c + 1) * P],
                                                     vt[:, (4 * i + c) * P:(4 * i + c + 1) * P], keep.ident[:])
                        mm.then_inc(s_vturn.sem, 1)
                    elif kind == "max":
                        if (h, i) == (0, 0):
                            after(pe, s_qhi, p, 4)
                            after(pe, s_klo, p, 2)
                        qt, half = i // 2, i % 2
                        nc.tensor.matmul(bank, q1[1 - u][:, h, qt * P:(qt + 1) * P],
                                         k1[1 - u][:, h, half * HALF:(half + 1) * HALF], start=True, stop=True) \
                          .then_inc(s_max.sem, 1)
                    else:
                        after(pe, s_comb, p, h + 1)
                        nc.tensor.transpose(work[0:KT, n % 2, 0:P], row_max[:, h], keep.ident[:]) \
                          .then_inc(s_turn.sem, 1)

                def qk(t, kt, h, u, part):
                    if part == 0:
                        if kt == 0:
                            if not isinstance(t, int):
                                after(pe, s_exp, t - 1, 2 * KT - 1 + h)
                            after(pe, s_turn_read, t, h + 1)
                            after(pe, s_qlo, t, h + 1)
                        else:
                            after(pe, s_exp, t, 2 * kt - 1 + h)
                    q_side, k_side = ((q1, k1), (q2, k2))[part]
                    for half in range(2):
                        cols = slice(half * HALF, (half + 1) * HALF)
                        mm = nc.tensor.matmul(scores[h][:, cols], k_side[u][:, h, kt * P:(kt + 1) * P],
                                              q_side[u][:, h, cols], start=(part == 0), stop=(part == 1))
                    if part == 1:
                        mm.then_inc(s_score.sem, 1)

                def pv(t, kt, u, half):
                    if half == 0:
                        after(pe, s_exp, t, 2 * kt + 2)
                        if kt == 0:
                            after(pe, s_oraw, t - 1, 1)
                            after(pe, s_vturn_read, t, 2)
                    cols = slice(half * HALF, (half + 1) * HALF)
                    for h in range(2):
                        mm = nc.tensor.matmul(o_ps[h * DH:(h + 1) * DH, cols], v[u][:, kt, h * DH:(h + 1) * DH],
                                              probs[h][kt % 2][:, cols], start=(kt == 0), stop=(kt == KT - 1))
                    if half == 1:
                        mm.then_inc(s_pv.sem, 1)

                for n, (_, zz, i) in enumerate(proj):
                    if n >= 2:
                        after(pe, s_proj_read, 0, n - 1)
                    projection(zz, i, 0, work[:, n % 2])
                for job in jobs:
                    if job[0] != "sum":
                        run_job(job, -1, 1)
                for h in range(2):
                    for part in range(2):
                        qk(0, 0, h, 0, part)
                pe.wait_ge(s_const, n_const)
                with pe.Fori(0, PAIRS // 2) as it:
                    for u in range(2):
                        t = 2 * it + u
                        for kt in range(KT):
                            nt, nk, nu = next_tile(t, kt, u)
                            attention = [lambda h=h, part=part: qk(nt, nk, h, nu, part) for h in range(2)
                                         for part in range(2)]
                            products = [lambda half=half: pv(t, kt, u, half) for half in range(2)]
                            at = 4 if kt < KT - 1 else 2
                            attention[at:at] = products
                            for slot in range(6):
                                attention[slot]()
                                for job in slots.get((kt, slot), []):
                                    run_job(job, t, u)
                job_read(pe, PAIRS, 0)
                job_read(pe, PAIRS, 1)
                for i in range(2):
                    column_sums(PAIRS - 1, i, i)

            @block.scalar
            def _(act):
                def split_w(p, first=False):
                    after(act, s_w, p, 1)
                    if not first:
                        after(act, s_proj, p - 1, 6)
                    nc.scalar.activation(w_hi[:], w_raw[:], ACT.Copy).then_inc(s_whi.sem, 1)

                def rows(job, p, n):
                    _, zz, i = job
                    after(act, s_proj, p, 2 * zz + i + 1)
                    if not (isinstance(p, int) and p == 0) and i == 0:
                        after(act, *((s_qlo, p - 1, 2), (s_klo, p - 1, 2), (s_vturn, p - 1, 2))[zz])
                    dst = (z + [vt])[zz][:, i * HALF:(i + 1) * HALF]
                    nc.scalar.activation(dst, work[:, n % 2], ACT.Copy).then_inc(s_proj_read.sem, 1)

                def evac(job, t, u):
                    n = index[job]
                    kind, h, i = job
                    if kind == "proj":
                        rows(job, t + 2, n)
                    elif kind == "vturn":
                        after(act, s_vturn, t + 1, i + 1)
                        if i == 0 and not isinstance(t, int):
                            after(act, s_pv, t - 1, KT)
                        nc.scalar.activation(v[1 - u][:, 4 * i:4 * i + 4].rearrange("p c m -> p (c m)"),
                                             work[:, n % 2], ACT.Copy).then_inc(s_vturn_read.sem, 1)
                    elif kind == "sum":
                        sum_evac(t - 1, i, n)

                def sum_evac(t, i, n):
                    after(act, s_sum, t, i + 1)
                    if i == 0:
                        after(act, s_rope, t + 2, 4)
                    nc.scalar.activation(divisor[:, i * HALF:(i + 1) * HALF], work[:, n % 2], ACT.Copy) \
                      .then_inc(s_sum_read.sem, 1)

                def q_high(p, u, n):
                    if n == 0:
                        after(act, s_rope, p, 2)
                    for h, src in ((0, top), (1, bot))[n:n + 1]:
                        for dst in (top, bot):
                            nc.scalar.activation(q1[u][dst, h], z[0][src], ACT.Copy).then_inc(s_qhi.sem, 1)

                def exp(t, kt, h):
                    after(act, s_score, t, 2 * kt + h + 1)
                    if not isinstance(t, int):
                        r, k_old = (t, kt - 2) if kt >= 2 else (t - 1, kt - 2 + KT)
                        after(act, s_pv, r, k_old + 1)
                        after(act, s_acc, r, add_index(k_old, h))
                    nc.scalar.activation(probs[h][kt % 2][:], scores[h][:], ACT.Exp, scale=SCALE) \
                      .then_inc(s_exp.sem, 1)

                def read_outputs(t):
                    after(act, s_pv, t, KT)
                    after(act, s_store, t - 1, 1)
                    nc.scalar.activation(o_raw[:], o_ps[:], ACT.Copy).then_inc(s_oraw.sem, 1)

                split_w(0, first=True)
                for n, job in enumerate(proj):
                    rows(job, 0, n)
                q_high(0, 0, 0)
                q_high(0, 0, 1)
                split_w(1)
                for job in jobs:
                    if job[0] in ("proj", "vturn"):
                        evac(job, -1, 1)
                for h in range(2):
                    exp(0, 0, h)
                act.wait_ge(s_const, n_const)
                q_high(1, 1, 0)
                q_high(1, 1, 1)
                with act.Fori(0, PAIRS // 2) as it:
                    for u in range(2):
                        t = 2 * it + u
                        for kt in range(KT):
                            nt, nk, _ = next_tile(t, kt, u)
                            if kt == 0:
                                read_outputs(t - 1)
                            for h in range(3):
                                for job in slots.get((kt, 2 * h), []) + slots.get((kt, 2 * h + 1), []):
                                    evac(job, t, u)
                                if h < 2:
                                    if (kt, h) == (KT - 1, 1):
                                        q_high(t + 2, u, 1)
                                    exp(nt, nk, h)
                            if kt == 1:
                                split_w(t + 2)
                            if kt == KT - 2:
                                after(act, s_score, t, 2 * KT)
                                q_high(t + 2, u, 0)
                read_outputs(PAIRS - 1)
                for i in range(2):
                    sum_evac(PAIRS - 1, i, i)

            @block.vector
            def _(dve):
                nc.vector.memset(ones[:], 1.0).then_inc(s_const, 1)
                for h in range(2):
                    nc.vector.memset(sums[h][:], 1.0).then_inc(s_const, 1)
                nc.vector.memset(o_ps[:], 0.0).then_inc(s_const, 1)
                for u in range(2):
                    nc.vector.memset(as_f32(q2[u][:]), 0.0).then_inc(s_const, 1)
                    nc.vector.memset(as_f32(k2[u][:]), 0.0).then_inc(s_const, 1)
                dve.wait_ge(s_const, n_const - 4)
                for u in range(2):
                    nc.vector.memset(as_f32(k2[u][DH:DH + KT, 0]), 1.0).then_inc(s_const, 1)
                    nc.vector.memset(as_f32(k2[u][0:KT, 1]), 1.0).then_inc(s_const, 1)
                dve.wait_ge(s_const, n_const)
                dve.wait_ge(s_table, 32)
                dve.sem_inc(s_norm.sem, 1)

                def lo_w(p):
                    after(dve, s_whi, p, 1)
                    nc.vector.tensor_tensor(w_lo[:], w_raw[:], as_f32(w_hi[:]), ALU.subtract).then_inc(s_wlo.sem, 1)

                def reciprocals(t):
                    after(dve, s_sum_in, t, 1)
                    nc.vector.reciprocal(compact[:], compact[:]).then_inc(s_recip.sem, 1)

                def normalise(t):
                    after(dve, s_inv_in, t, 2)
                    after(dve, s_oraw, t, 1)
                    nc.vector.tensor_tensor(o_raw[:], o_raw[:], divisor[:], ALU.mult).then_inc(s_norm.sem, 1)

                def rope_cos(n, p):
                    after(dve, s_proj_read, p, 2 * n + 2)
                    after(dve, s_swap[n], p, 4)
                    nc.vector.tensor_tensor(z[n][:], z[n][:], cos[:], ALU.mult).then_inc(s_rope.sem, 1)

                def rope_add(n, p):
                    after(dve, s_rope, p, 2 * n + 1)
                    after(dve, s_sin, p, n + 1)
                    nc.vector.tensor_tensor(z[n][:], z[n][:], z_swap[n][:], ALU.add).then_inc(s_rope.sem, 1)

                def k_high(p, u):
                    after(dve, s_rope, p, 4)
                    for dst, src in ((k1[u][top, 0], top), (k1[u][bot, 1], bot), (k2[u][top, 0], top),
                                     (k2[u][bot, 1], bot)):
                        nc.vector.tensor_copy(dst, z[1][src]).then_inc(s_khi.sem, 1)

                def k_low(p, u):
                    for h, (src, dst) in enumerate(((top, bot), (bot, top))):
                        after(dve, s_khi, p, h + 1)
                        nc.vector.tensor_tensor(k1[u][dst, h], z[1][src], as_f32(k1[u][src, h]), ALU.subtract) \
                          .then_inc(s_klo.sem, 1)

                def q_low(p, u):
                    after(dve, s_qhi, p, 4)
                    for h, rows in ((0, top), (1, bot)):
                        nc.vector.tensor_tensor(q2[u][rows, h], z[0][rows], as_f32(q1[u][rows, h]), ALU.subtract) \
                          .then_inc(s_qlo.sem, 1)

                def reduce(job, p, u):
                    kind, h, i = job
                    n = index[job]
                    if kind == "max":
                        after(dve, s_max, p, h * 2 * KT + i + 1)
                        nc.vector.tensor_reduce(maxima[:, h, i // 2, i % 2:i % 2 + 1], work[:, n % 2], AX.X, ALU.max) \
                          .then_inc(s_max_read.sem, 1)
                        if i == 2 * KT - 1:
                            after(dve, s_max_read, p, h * 2 * KT + i + 1)
                            nc.vector.tensor_reduce(row_max[:, h], maxima[:, h], AX.X, ALU.max) \
                              .then_inc(s_comb.sem, 1)
                    elif kind == "turn":
                        after(dve, s_turn, p, h + 1)
                        rows = slice(DH, DH + KT) if h == 0 else slice(0, KT)
                        turned = work[0:KT, n % 2, 0:P].rearrange("p (a q) -> p a q", a=1).to_broadcast([KT, KT, P])
                        nc.vector.tensor_tensor(q2[u][rows, h].rearrange("p (a q) -> p a q", q=P), turned,
                                                keep.neg_block[0:KT], ALU.mult).then_inc(s_turn_read.sem, 1)

                beside = {
                    (0, 0): lambda t, u: q_low(t + 1, 1 - u),
                    (2, 0): lambda t, u: lo_w(t + 2),
                    (1, 3): lambda t, u: reciprocals(t - 1),
                    (4, 0): lambda t, u: rope_cos(0, t + 2),
                    (4, 2): lambda t, u: rope_add(0, t + 2),
                    (4, 4): lambda t, u: rope_cos(1, t + 2),
                    (5, 4): lambda t, u: rope_add(1, t + 2),
                    (2, 5): lambda t, u: normalise(t - 1),
                }

                def keys(t, u):
                    if not isinstance(t, int):
                        after(dve, s_score, t, 2 * KT)
                    k_high(t + 2, u)
                    k_low(t + 2, u)

                lo_w(0)
                for n in range(2):
                    rope_cos(n, 0)
                    rope_add(n, 0)
                k_high(0, 0)
                k_low(0, 0)
                q_low(0, 0)
                lo_w(1)
                for where in [(kt, slot) for kt in range(KT) for slot in range(6)]:
                    for job in slots.get(where, []):
                        reduce(job, 0, 0)
                    if where in ((4, 0), (4, 2), (4, 4), (5, 4)):
                        beside[where](-1, 1)
                keys(-1, 1)
                with dve.Fori(0, PAIRS // 2) as it:
                    for u in range(2):
                        t = 2 * it + u
                        for where in [(kt, slot) for kt in range(KT) for slot in range(6)]:
                            for job in slots.get(where, []):
                                reduce(job, t + 1, 1 - u)
                            if where in beside:
                                beside[where](t, u)
                        keys(t, u)
                reciprocals(PAIRS - 1)
                normalise(PAIRS - 1)

            @block.gpsimd
            def _(pool):
                pool.sem_inc(s_acc.sem, 2 * (KT - 1))
                pool.sem_inc(s_store.sem, 16)
                pool.wait_ge(s_table, 32)

                def sine(n, p):
                    after(pool, s_swap[n], p, 4)
                    nc.gpsimd.tensor_tensor(z_swap[n][:], z_swap[n][:], sin[:], ALU.mult).then_inc(s_sin.sem, 1)

                def add(t, kt, h):
                    after(pool, s_exp, t, 2 * kt + h + 1)
                    if kt == 1:
                        after(pool, s_sum, t - 1, 2)
                        first_term = probs[h][0][:]
                    else:
                        after(pool, s_acc, t, add_index(kt - 1, h))
                        first_term = sums[h][:]
                    nc.gpsimd.tensor_tensor(sums[h][:], first_term, probs[h][kt % 2][:], ALU.add) \
                      .then_inc(s_acc.sem, 1)

                for p in range(2):
                    for n in range(2):
                        sine(n, p)
                with pool.Fori(0, PAIRS // 2) as it:
                    for u in range(2):
                        t = 2 * it + u
                        for kt in range(1, KT):
                            for h in range(2):
                                add(t, kt, h)
                            if kt in (4, 5):
                                sine(kt - 4, t + 2)

def phase_project(nc, io, keep, sem, name, o_pairs, wo, bias, m):
    first = m == 0
    chunk_tiles = GT // 2
    chunk = chunk_tiles * P
    with ExitStack() as ctx:
        sb = lambda n, s, d: ctx.enter_context(nc.sbuf_tensor(f"{name}_{n}", s, d))
        ps = lambda n, s, d: ctx.enter_context(nc.psum_tensor(f"{name}_{n}", s, d))
        ln = Layernorm(nc, lambda n, s, d: ctx.enter_context(nc.sbuf_tensor(n, s, d)),
                       lambda n, s, d: ctx.enter_context(nc.psum_tensor(n, s, d)), sem, f"{name}_ln", keep.s_carrier)
        w_raw = sb("w_raw", [P, HP, D], F32)
        w_hi = sb("w_hi", [P, HP, D], F32R)
        w_lo = sb("w_lo", [P, HP, D], F32R)
        bias_row = sb("bias", [P, D], F32)
        o_raw = [sb(f"o_raw{c}", [P, HP, chunk], F32) for c in range(2)]
        o_hi = [sb(f"o_hi{c}", [P, HP, chunk], F32R) for c in range(2)]
        o_lo = [sb(f"o_lo{c}", [P, HP, chunk], F32R) for c in range(2)]
        x_bias = sb("x_bias", [P, GT, D], F32)
        x_old = sb("x_old", [P, GT, D], F32) if first else None
        acc = [ps(f"acc{c}", [P, chunk_tiles, D], F32) for c in range(2)]
        s_w = sem(f"{name}_w")
        s_w_hi = sem(f"{name}_w_hi")
        s_w_lo = sem(f"{name}_w_lo")
        s_o = [Counter(sem(f"{name}_o{c}"), 1, 16) for c in range(2)]
        s_xold = Counter(sem(f"{name}_xold"), 1, 16)
        s_hi = Counter(sem(f"{name}_hi"), 2, start=2)
        s_lo = Counter(sem(f"{name}_lo"), 2, start=2)
        s_mm = Counter(sem(f"{name}_mm"), 2, start=2)
        s_xb = Counter(sem(f"{name}_xb"), GT, start=GT)
        s_x = Counter(sem(f"{name}_x"), 2, start=2)
        x_d = io["x"].rearrange("(g j p) d -> g p j d", p=P, j=GT)
        o_d = o_pairs.rearrange("(h b) p n -> b p h n", b=B)

        with nc.Block() as block:
            @block.sync
            def _(sp):
                sp.dma_start(w_raw[:], io[wo].rearrange("(h p) d -> p h d", p=P)).then_inc(s_w, 16)
                sp.dma_start(bias_row[:], io[bias].partition_broadcast(P)).then_inc(s_w, 16)
                with sp.Fori(0, GROUPS) as g:
                    for c in range(2):
                        after_sp(sp, s_hi, g - 1, c + 1, keep.s_carrier)
                        after_sp(sp, s_lo, g - 1, c + 1, keep.s_carrier)
                        start = (g % 2) * HALF + c * chunk
                        src = o_d[bass.ds(g // 2, 1), :, :, bass.ds(start, chunk)].rearrange("o p h n -> (o p) h n")
                        sp.dma_start(o_raw[c][:], src).then_inc(s_o[c].sem, 16)
                    if first:
                        after_sp(sp, s_xb, g - 1, GT, keep.s_carrier)
                        sp.dma_start(x_old[:], x_d[bass.ds(g, 1)].rearrange("o p j d -> (o p) j d")) \
                          .then_inc(s_xold.sem, 16)

            @block.gpsimd
            def _(pool):
                pool.sem_inc(s_xb.sem, GT)
                pool.wait_ge(s_w, 32)
                pool.wait_ge(ln.s_half, 1)

                def old_rows(g):
                    if first:
                        after(pool, s_xold, g, 1)
                    after(pool, s_x, g - 1, 2)
                    for j in range(GT):
                        src = x_old[:, j] if first else keep.x[:, bass.ds(g * GT + j, 1)].rearrange("p o d -> p (o d)")
                        nc.gpsimd.tensor_tensor(x_bias[:, j], src, bias_row[:], ALU.add).then_inc(s_xb.sem, 1)

                old_rows(0)
                with pool.Fori(1, GROUPS) as g:
                    old_rows(g)
                    pool_rstd(nc, pool, ln, g - 1)
                pool_rstd(nc, pool, ln, GROUPS - 1)

            @block.scalar
            def _(act):
                act.sem_inc(s_hi.sem, 2)
                ln.start_act(act)
                act.wait_ge(s_w, 32)
                nc.scalar.activation(w_hi[:], w_raw[:], ACT.Copy).then_inc(s_w_hi, 1)

                def halves(g):
                    for c in range(2):
                        after(act, s_o[c], g, 1)
                        after(act, s_mm, g - 1, c + 1)
                        nc.scalar.activation(o_hi[c][:], o_raw[c][:], ACT.Copy).then_inc(s_hi.sem, 1)

                halves(0)
                with act.Fori(1, GROUPS) as g:
                    halves(g)
                    act_modulate(nc, act, ln, keep, m, g - 1)
                act_modulate(nc, act, ln, keep, m, GROUPS - 1)

            @block.tensor
            def _(pe):
                pe.sem_inc(s_mm.sem, 2)
                ln.start_pe(pe)
                pe.wait_ge(s_w_hi, 1)
                pe.wait_ge(s_w_lo, 1)

                def products(g, c):
                    after(pe, s_lo, g, c + 1)
                    after(pe, s_hi, g, c + 1)
                    after(pe, s_x, g - 1, c + 1)
                    for j in range(chunk_tiles):
                        steps = [(o, w, h) for h in range(HP) for o, w in split_products(o_hi[c], o_lo[c], w_hi, w_lo)]
                        for n, (o, w, h) in enumerate(steps):
                            mm = nc.tensor.matmul(acc[c][:, j], o[:, h, j * P:(j + 1) * P], w[:, h], start=(n == 0),
                                                  stop=(n == len(steps) - 1))
                    mm.then_inc(s_mm.sem, 1)

                products(0, 0)
                products(0, 1)
                with pe.Fori(1, GROUPS) as g:
                    products(g, 0)
                    pe_turn(nc, pe, ln, keep.ident[:], g - 1)
                    products(g, 1)
                pe_turn(nc, pe, ln, keep.ident[:], GROUPS - 1)

            @block.vector
            def _(dve):
                dve.sem_inc(s_lo.sem, 2)
                dve.sem_inc(s_x.sem, 2)
                ln.start_dve(nc, dve)
                dve.wait_ge(s_w_hi, 1)
                nc.vector.tensor_tensor(w_lo[:], w_raw[:], as_f32(w_hi[:]), ALU.subtract).then_inc(s_w_lo, 1)

                def low_half(g, c):
                    after(dve, s_hi, g, c + 1)
                    nc.vector.tensor_tensor(o_lo[c][:], o_raw[c][:], as_f32(o_hi[c][:]), ALU.subtract) \
                      .then_inc(s_lo.sem, 1)

                def new_rows(g, c):
                    after(dve, s_mm, g, c + 1)
                    after(dve, s_xb, g, GT)
                    tiles = bass.ds(g * GT + c * chunk_tiles, chunk_tiles)
                    nc.vector.tensor_tensor(keep.x[:, tiles], acc[c][:], x_bias[:, c * chunk_tiles:(c + 1) * chunk_tiles],
                                            ALU.add).then_inc(s_x.sem, 1)

                def norm(g):
                    after(dve, s_x, g, 2)
                    dve.sem_inc(keep.s_carrier, 1)
                    dve_norm(nc, dve, ln, lambda j: keep.x[:, bass.ds(g * GT + j, 1)].rearrange("p o d -> p (o d)"), g)
                    dve_modulated_lo(nc, dve, ln, keep, g)

                low_half(0, 0)
                low_half(0, 1)
                with dve.Fori(1, GROUPS) as g:
                    low_half(g, 0)
                    new_rows(g - 1, 0)
                    low_half(g, 1)
                    new_rows(g - 1, 1)
                    norm(g - 1)
                new_rows(GROUPS - 1, 0)
                new_rows(GROUPS - 1, 1)
                norm(GROUPS - 1)

def phase_context(nc, io, keep, sem, kv_dram):
    ct = B * M // P
    kw = (P, DC - P)
    with ExitStack() as ctx:
        sb = lambda n, s, d: ctx.enter_context(nc.sbuf_tensor(f"cx_{n}", s, d))
        ps = lambda n, s, d: ctx.enter_context(nc.psum_tensor(f"cx_{n}", s, d))
        rows = sb("rows", [P, ct, DC], F32)
        scale = sb("scale", [P, 2], F32)
        shift = sb("shift", [P, 2], F32)
        stats = sb("stats", [P, ct, 6], F32)
        moments = sb("moments", [P, ct, 2], F32)
        var_eps = sb("var_eps", [P, ct], F32)
        minus_half = sb("minus_half", [P, ct], F32)
        rstd = sb("rstd", [P, ct], F32)
        xn = sb("xn", [P, ct, DC], F32)
        y = sb("y", [P, 2, ct * P], F32)
        y_hi = sb("y_hi", [P, 2, ct * P], F32R)
        y_lo = sb("y_lo", [P, 2, ct * P], F32R)
        w_raw = sb("w_raw", [P, 2, 2, P], F32)
        w_hi = sb("w_hi", [P, 2, 2, P], F32R)
        w_lo = sb("w_lo", [P, 2, 2, P], F32R)
        cos = sb("cos", [P, M], F32)
        sin = sb("sin", [P, M], F32)
        z = sb("k_rows", [P, B, M], F32)
        z_swap = sb("k_swapped", [P, B, M], F32)
        kv = sb("kv", [P, B, 4, P], F32R)
        turned = ps("turned", [P, 2, ct * P], F32)
        k_ps = ps("k_ps", [P, B * M], F32)
        v_ps = ps("v_ps", [P, ct, P], F32)
        s_in, s_stat, s_mom, s_var, s_rstd, s_xn, s_turned, s_mod, s_ylo, s_half, s_zero = (
            sem(f"cx_{n}") for n in ("in", "stat", "mom", "var", "rstd", "xn", "turned", "mod", "ylo", "half", "zero"))
        s_w = Counter(sem("cx_w"), 1, 16)
        s_whi = Counter(sem("cx_whi"), 1)
        s_wlo = Counter(sem("cx_wlo"), 1)
        s_k = Counter(sem("cx_k"), 1)
        s_v = Counter(sem("cx_v"), 1)
        s_evac = Counter(sem("cx_evac"), 1)
        s_swap = Counter(sem("cx_swap"), 4, 16)
        s_sin = Counter(sem("cx_sin"), 1)
        s_rope = Counter(sem("cx_rope"), 2)
        s_hi = Counter(sem("cx_hi"), 6)
        s_lo = Counter(sem("cx_lo"), 6, start=6)
        s_store = Counter(sem("cx_store"), 1, 16)
        top, bot = slice(0, DH), slice(DH, P)
        k_places = [(top, slice(0, M)), (bot, slice(M, 2 * M))]
        v_places = [(par, h) for par in range(2) for h in range(2)]

        with nc.Block() as block:
            @block.sync
            def _(sp):
                for dst, src in ((rows[:], io["ctx"].rearrange("(j p) d -> p j d", p=P)), (scale[:], io["lnc_w"]),
                                 (shift[:], io["lnc_b"]), (cos[:], io["cos"][:, 0:M]), (sin[:], io["sin"][:, 0:M])):
                    sp.dma_start(dst, src).then_inc(s_in, 16)
                sp.dma_start(w_raw[:], io["w_ctx"][0]).then_inc(s_w.sem, 16)

                def body(r, last=False):
                    after_sp(sp, s_evac, r, 1, keep.s_carrier)
                    if isinstance(r, int) is False:
                        after_sp(sp, s_rope, r - 1, 2, keep.s_carrier)
                    for q in range(4):
                        sp.dma_start(z_swap[32 * q:32 * q + 32], z[32 * (q ^ 1):32 * (q ^ 1) + 32]) \
                          .then_inc(s_swap.sem, 16)
                    if not last:
                        after_sp(sp, s_whi, r, 1, keep.s_carrier)
                        after_sp(sp, s_wlo, r, 1, keep.s_carrier)
                        src = io["w_ctx"][bass.ds((r + 1) % HP, 1)].rearrange("o p k z m -> (o p) k z m")
                        sp.dma_start(w_raw[:], src).then_inc(s_w.sem, 16)
                    after_sp(sp, s_hi, r, 6, keep.s_carrier)
                    after_sp(sp, s_lo, r, 6, keep.s_carrier)
                    sp.dma_start(kv_dram[bass.ds(r * B, B)].rearrange("b p n -> p b n"),
                                 as_f32(kv[:].rearrange("p b f n -> p b (f n)"))).then_inc(s_store.sem, 16)

                body(0)
                with sp.Fori(1, HP) as r:
                    body(r)
                after_sp(sp, s_store, HP - 1, 1, keep.s_carrier)
                after_sp(sp, s_w, HP, 1, keep.s_carrier)

            @block.gpsimd
            def _(pool):
                nc.gpsimd.memset(minus_half[:], -0.5).then_inc(s_half, 1)
                nc.gpsimd.memset(as_f32(kv[:]), 0.0).then_inc(s_zero, 1)
                pool.wait_ge(s_var, 1)
                pool.wait_ge(s_half, 1)
                nc.gpsimd.tensor_tensor(rstd[:], var_eps[:], minus_half[:], ALU.pow).then_inc(s_rstd, 1)
                with pool.Fori(0, HP) as r:
                    after(pool, s_swap, r, 4)
                    nc.gpsimd.tensor_tensor(z_swap[:], z_swap[:], sin[:].unsqueeze(1).to_broadcast([P, B, M]),
                                            ALU.mult).then_inc(s_sin.sem, 1)

            @block.vector
            def _(dve):
                dve.sem_inc(s_lo.sem, 6)
                dve.wait_ge(s_in, 80)
                for j in range(ct):
                    nc.vector.bn_stats(stats[:, j], rows[:, j]).then_inc(s_stat, 1)
                for j in range(ct):
                    dve.wait_ge(s_stat, j + 1)
                    nc.vector.bn_aggr(moments[:, j], stats[:, j]).then_inc(s_mom, 1)
                dve.wait_ge(s_mom, ct)
                nc.vector.tensor_scalar(var_eps[:], moments[:, :, 1], EPS, None, ALU.add).then_inc(s_var, 1)
                dve.wait_ge(s_rstd, 1)
                for j in range(ct):
                    nc.vector.tensor_scalar(xn[:, j], rows[:, j], moments[:, j, 0:1], rstd[:, j:j + 1], ALU.subtract,
                                            ALU.mult).then_inc(s_xn, 1)
                after(dve, s_whi, 0, 1)
                nc.vector.tensor_tensor(w_lo[:], w_raw[:], as_f32(w_hi[:]), ALU.subtract).then_inc(s_wlo.sem, 1)
                for k in range(2):
                    dve.wait_ge(s_mod, 2 * k + 2)
                    n = kw[k]
                    nc.vector.tensor_tensor(y_lo[0:n, k], y[0:n, k], as_f32(y_hi[0:n, k]), ALU.subtract) \
                        .then_inc(s_ylo, 1)
                dve.wait_ge(s_zero, 1)
                with dve.Fori(0, HP) as r:
                    after(dve, s_evac, r, 1)
                    after(dve, s_swap, r, 4)
                    nc.vector.tensor_tensor(z[:], z[:], cos[:].unsqueeze(1).to_broadcast([P, B, M]), ALU.mult) \
                        .then_inc(s_rope.sem, 1)
                    after(dve, s_whi, r + 1, 1)
                    nc.vector.tensor_tensor(w_lo[:], w_raw[:], as_f32(w_hi[:]), ALU.subtract).then_inc(s_wlo.sem, 1)
                    after(dve, s_sin, r, 1)
                    after(dve, s_rope, r, 1)
                    nc.vector.tensor_tensor(z[:], z[:], z_swap[:], ALU.add).then_inc(s_rope.sem, 1)
                    for n, (par, h) in enumerate(v_places):
                        after(dve, s_hi, r, 4)
                        half = k_places[h][0]
                        nc.vector.tensor_tensor(kv[half, par::2, 3, h * DH:(h + 1) * DH],
                                                v_ps[par * M:(par + 1) * M, :, h * DH:(h + 1) * DH],
                                                as_f32(kv[half, par::2, 2, h * DH:(h + 1) * DH]), ALU.subtract) \
                            .then_inc(s_lo.sem, 1)
                    for n, (half, cols) in enumerate(k_places):
                        after(dve, s_hi, r, 5 + n)
                        nc.vector.tensor_tensor(kv[half, :, 1, cols], z[half], as_f32(kv[half, :, 0, cols]),
                                                ALU.subtract).then_inc(s_lo.sem, 1)

            @block.scalar
            def _(act):
                def split_w(r):
                    after(act, s_w, r, 1)
                    nc.scalar.activation(w_hi[:], w_raw[:], ACT.Copy).then_inc(s_whi.sem, 1)

                split_w(0)
                act.wait_ge(s_in, 80)
                for k in range(2):
                    n = kw[k]
                    act.wait_ge(s_turned, 2)
                    for dst in (y, y_hi):
                        nc.scalar.activation(dst[0:n, k], turned[0:n, k], ACT.Identity, scale=scale[0:n, k:k + 1],
                                             bias=shift[0:n, k:k + 1]).then_inc(s_mod, 1)
                act.wait_ge(s_zero, 1)

                def body(r, stored):
                    after(act, s_k, r, 1)
                    after(act, s_lo, r - 1, 6)
                    nc.scalar.activation(z[:].rearrange("p b m -> p (b m)"), k_ps[:], ACT.Copy) \
                        .then_inc(s_evac.sem, 1)
                    after(act, s_v, r, 1)
                    split_w(r + 1)
                    if stored:
                        after(act, s_store, r - 1, 1)
                    for par, h in v_places:
                        half = k_places[h][0]
                        nc.scalar.activation(kv[half, par::2, 2, h * DH:(h + 1) * DH],
                                             v_ps[par * M:(par + 1) * M, :, h * DH:(h + 1) * DH], ACT.Copy) \
                            .then_inc(s_hi.sem, 1)
                    after(act, s_rope, r, 2)
                    for half, cols in k_places:
                        nc.scalar.activation(kv[half, :, 0, cols], z[half], ACT.Copy).then_inc(s_hi.sem, 1)

                body(0, False)
                with act.Fori(1, HP) as r:
                    body(r, True)

            @block.tensor
            def _(pe):
                for k in range(2):
                    for j in range(ct):
                        pe.wait_ge(s_xn, j + 1)
                        mm = nc.tensor.transpose(turned[0:kw[k], k, j * P:(j + 1) * P],
                                                 xn[:, j, k * P:k * P + kw[k]], keep.ident[:])
                    mm.then_inc(s_turned, 1)
                pe.wait_ge(s_ylo, 2)
                steps = lambda: [(a, b, k) for k in range(2) for a, b in split_products(w_hi, w_lo, y_hi, y_lo)]
                with pe.Fori(0, HP) as r:
                    after(pe, s_whi, r, 1)
                    after(pe, s_wlo, r, 1)
                    after(pe, s_lo, r - 1, 6)
                    for n, (w, x, k) in enumerate(steps()):
                        mm = nc.tensor.matmul(k_ps[:], w[0:kw[k], k, 0], x[0:kw[k], k], start=(n == 0), stop=(n == 5))
                    mm.then_inc(s_k.sem, 1)
                    for j in range(ct):
                        for n, (w, x, k) in enumerate(steps()):
                            mm = nc.tensor.matmul(v_ps[:, j], x[0:kw[k], k, j * P:(j + 1) * P], w[0:kw[k], k, 1],
                                                  start=(n == 0), stop=(n == 5))
                    mm.then_inc(s_v.sem, 1)


def phase_cross_attention(nc, io, keep, sem, kv_dram, o_dram):
    with ExitStack() as ctx:
        sb = lambda n, s, d: ctx.enter_context(nc.sbuf_tensor(f"ca_{n}", s, d))
        ps = lambda n, s, d: ctx.enter_context(nc.psum_tensor(f"ca_{n}", s, d))
        w_raw = sb("w_raw", [P, KD, P], F32)
        w_hi = sb("w_hi", [P, KD, P], F32R)
        w_lo = sb("w_lo", [P, KD, P], F32R)
        cos = sb("cos", [P, N], F32)
        sin = sb("sin", [P, N], F32)
        z = sb("q_rows", [P, N], F32)
        z_swap = sb("q_swapped", [P, N], F32)
        q_hi = [sb(f"q_hi{u}", [P, N], F32R) for u in range(2)]
        q_lo = [sb(f"q_lo{u}", [P, N], F32R) for u in range(2)]
        kv = [sb(f"kv{u}", [P, 4, P], F32R) for u in range(2)]
        row_max = sb("row_max", [P, 2, KT], F32)
        neg_max = sb("neg_max", [2 * KT, KT, P], F32R)
        heads_raw = sb("heads_raw", [2 * KT, P], F32)
        heads = sb("heads", [2 * KT, P], F32R)
        ones_raw = sb("ones_raw", [P, P], F32)
        ones = sb("ones", [P, P], F32R)
        probs = sb("probs", [P, N], F32)
        p_hi = sb("p_hi", [P, N], F32R)
        p_lo = sb("p_lo", [P, N], F32R)
        inv_sum = sb("inv_sum", [P, N], F32)
        o_sb = sb("o_sb", [P, N], F32)
        work = ps("work", [P, N], F32)
        scores = ps("scores", [P, N], F32)
        o_ps = ps("o_ps", [P, N], F32)
        sum_ps = ps("sum_ps", [P, N], F32)

        s_in, s_const = (sem(f"ca_{n}") for n in ("in", "const"))
        s_w = Counter(sem("ca_w"), 1, 16)
        s_whi = Counter(sem("ca_whi"), 1)
        s_wlo = Counter(sem("ca_wlo"), 1)
        s_proj = Counter(sem("ca_proj"), 2)
        s_evac = Counter(sem("ca_evac"), 2)
        s_swap = Counter(sem("ca_swap"), 4, 16)
        s_sin = Counter(sem("ca_sin"), 1)
        s_rope = Counter(sem("ca_rope"), 2)
        s_hi = Counter(sem("ca_hi"), 1)
        s_lo = Counter(sem("ca_lo"), 1)
        s_kv = [Counter(sem(f"ca_kv{u}"), 1, 16) for u in range(2)]
        s_max = Counter(sem("ca_max"), 2)
        s_mred = Counter(sem("ca_mred"), 2)
        s_turn = Counter(sem("ca_turn"), 1)
        s_shift = Counter(sem("ca_shift"), 1)
        s_score = Counter(sem("ca_score"), 1, start=2)
        s_exp = Counter(sem("ca_exp"), 2, start=4)
        s_plo = Counter(sem("ca_plo"), 1, start=2)
        s_pv = Counter(sem("ca_pv"), 2, start=4)
        s_inv = Counter(sem("ca_inv"), 1, start=2)
        s_out = Counter(sem("ca_out"), 1, start=2)
        s_store = Counter(sem("ca_store"), 1, 16, start=32)
        halves = [slice(i * HALF, (i + 1) * HALF) for i in range(2)]
        pair_kv = lambda u: [kv[u][:, n] for n in range(4)]

        with nc.Block() as block:
            @block.sync
            def _(sp):
                for dst, src in ((cos[:], io["cos"]), (sin[:], io["sin"]), (heads_raw[:], io["heads"]),
                                 (ones_raw[:], io["ones_block"])):
                    sp.dma_start(dst, src).then_inc(s_in, 16)
                for u in range(2):
                    sp.dma_start(as_f32(kv[u][:].rearrange("p f n -> p (f n)")), kv_dram[u]).then_inc(s_kv[u].sem, 16)
                sp.dma_start(w_raw[:], io["w_cross"][0]).then_inc(s_w.sem, 16)

                def swap(r, first=False):
                    after_sp(sp, s_evac, r, 2, keep.s_carrier)
                    if not first:
                        after_sp(sp, s_rope, r - 1, 2, keep.s_carrier)
                    for q in range(4):
                        sp.dma_start(z_swap[32 * q:32 * q + 32], z[32 * (q ^ 1):32 * (q ^ 1) + 32]) \
                          .then_inc(s_swap.sem, 16)

                def weights(r):
                    after_sp(sp, s_whi, r - 1, 1, keep.s_carrier)
                    after_sp(sp, s_wlo, r - 1, 1, keep.s_carrier)
                    src = io["w_cross"][bass.ds((r // B) % HP, 1)].rearrange("o p k m -> (o p) k m")
                    sp.dma_start(w_raw[:], src).then_inc(s_w.sem, 16)

                weights(1)
                swap(0, first=True)
                weights(2)
                swap(1)
                with sp.Fori(0, PAIRS // 2) as i:
                    for u in range(2):
                        t = 2 * i + u
                        swap(t + 2)
                        weights(t + 3)
                        after_sp(sp, s_out, t, 1, keep.s_carrier)
                        sp.dma_start(o_dram[bass.ds(t, 1)].rearrange("o p n -> (o p) n"), o_sb[:]) \
                          .then_inc(s_store.sem, 16)
                        after_sp(sp, s_pv, t, 2, keep.s_carrier)
                        sp.dma_start(as_f32(kv[u][:].rearrange("p f n -> p (f n)")),
                                     kv_dram[bass.ds((t + 2) % PAIRS, 1)].rearrange("o p n -> (o p) n")) \
                          .then_inc(s_kv[u].sem, 16)
                after_sp(sp, s_store, PAIRS - 1, 1, keep.s_carrier)
                after_sp(sp, s_w, PAIRS + 2, 1, keep.s_carrier)
                for u in range(2):
                    after_sp(sp, s_kv[u], PAIRS // 2, 1, keep.s_carrier)

            @block.gpsimd
            def _(pool):
                pool.sem_inc(s_store.sem, 32)
                pool.wait_ge(s_in, 64)
                with pool.Fori(0, PAIRS + 2) as r:
                    after(pool, s_swap, r, 4)
                    nc.gpsimd.tensor_tensor(z_swap[:], z_swap[:], sin[:], ALU.mult).then_inc(s_sin.sem, 1)

            @block.tensor
            def _(pe):
                pe.sem_inc(s_score.sem, 2)
                pe.sem_inc(s_pv.sem, 4)
                pe.wait_ge(s_const, 2)

                def queries(r):
                    after(pe, s_whi, r, 1)
                    after(pe, s_wlo, r, 1)
                    for i in range(2):
                        steps = [(w, x, k) for k in range(KD) for w, x in split_products(w_hi, w_lo, keep.xt_hi, keep.xt_lo)]
                        for n, (w, x, k) in enumerate(steps):
                            cols = bass.ds((r % B) * N + i * HALF, HALF)
                            mm = nc.tensor.matmul(work[:, halves[i]], w[:, k], x[:, k, cols], start=(n == 0),
                                                  stop=(n == len(steps) - 1))
                        mm.then_inc(s_proj.sem, 1)

                def maxima(r, u, kv_round):
                    after(pe, s_kv[u], kv_round, 1)
                    after(pe, s_hi, r, 1)
                    for qt in range(KT):
                        mm = nc.tensor.matmul(work[:, qt * P:(qt + 1) * P], q_hi[u][:, qt * P:(qt + 1) * P], pair_kv(u)[0],
                                              start=True, stop=True)
                        if qt % 4 == 3:
                            mm.then_inc(s_max.sem, 1)

                def turn(r):
                    after(pe, s_mred, r, 2)
                    after(pe, s_exp, r - 1, 2)
                    nc.tensor.transpose(scores[0:2 * KT, 0:P], row_max[:].rearrange("p h q -> p (h q)"),
                                        keep.ident[:]).then_inc(s_turn.sem, 1)

                def score(r, u):
                    after(pe, s_shift, r, 1)
                    after(pe, s_lo, r, 1)
                    k_hi, k_lo = pair_kv(u)[:2]
                    for i in range(2):
                        sh = neg_max[:].rearrange("r a q -> r (a q)")[:, halves[i]]
                        steps = [(k_hi, q_hi[u][:, halves[i]]), (k_hi, q_lo[u][:, halves[i]]),
                                 (k_lo, q_hi[u][:, halves[i]]), (heads[:], sh)]
                        for n, (a, b) in enumerate(steps):
                            mm = nc.tensor.matmul(scores[:, halves[i]], a, b, start=(n == 0), stop=(n == 3))
                    mm.then_inc(s_score.sem, 1)

                def outputs(r, u):
                    after(pe, s_exp, r, 2)
                    after(pe, s_plo, r, 1)
                    after(pe, s_inv, r - 1, 1)
                    v_hi, v_lo = pair_kv(u)[2:]
                    for i in range(2):
                        for n, p in enumerate((p_hi, p_lo)):
                            mm = nc.tensor.matmul(sum_ps[:, halves[i]], ones[:], p[:, halves[i]], start=(n == 0),
                                                  stop=(n == 1))
                    mm.then_inc(s_pv.sem, 1)
                    after(pe, s_out, r - 1, 1)
                    for i in range(2):
                        steps = split_products(v_hi, v_lo, p_hi[:, halves[i]], p_lo[:, halves[i]])
                        for n, (a, b) in enumerate(steps):
                            mm = nc.tensor.matmul(o_ps[:, halves[i]], a, b, start=(n == 0), stop=(n == 2))
                    mm.then_inc(s_pv.sem, 1)

                queries(0)
                after(pe, s_evac, 0, 2)
                queries(1)
                after(pe, s_evac, 1, 2)
                maxima(0, 0, 0)
                turn(0)
                with pe.Fori(0, PAIRS // 2) as i:
                    for u in range(2):
                        t = 2 * i + u
                        after(pe, s_mred, t, 2)
                        queries(t + 2)
                        score(t, u)
                        after(pe, s_evac, t + 2, 2)
                        maxima(t + 1, 1 - u, i + u)
                        outputs(t, u)
                        turn(t + 1)

            @block.scalar
            def _(act):
                act.sem_inc(s_exp.sem, 4)
                act.wait_ge(s_in, 64)
                nc.scalar.activation(ones[:], ones_raw[:], ACT.Copy).then_inc(s_const, 1)
                nc.scalar.activation(heads[:], heads_raw[:], ACT.Copy).then_inc(s_const, 1)

                def split_w(r, proj_done=True):
                    after(act, s_w, r, 1)
                    if proj_done:
                        after(act, s_proj, r - 1, 2)
                    nc.scalar.activation(w_hi[:], w_raw[:], ACT.Copy).then_inc(s_whi.sem, 1)

                def evac(r, first=False):
                    for i in range(2):
                        after(act, s_proj, r, i + 1)
                        if i == 0 and not first:
                            after(act, s_lo, r - 1, 1)
                        nc.scalar.activation(z[:, halves[i]], work[:, halves[i]], ACT.Copy).then_inc(s_evac.sem, 1)

                def high_half(r, u):
                    after(act, s_rope, r, 2)
                    after(act, s_score, r - 2, 1)
                    nc.scalar.activation(q_hi[u][:], z[:], ACT.Copy).then_inc(s_hi.sem, 1)

                split_w(0, proj_done=False)
                evac(0, first=True)
                split_w(1)
                high_half(0, 0)
                evac(1)
                split_w(2)
                high_half(1, 1)
                with act.Fori(0, PAIRS // 2) as i:
                    for u in range(2):
                        t = 2 * i + u
                        evac(t + 2)
                        split_w(t + 3)
                        after(act, s_score, t, 1)
                        after(act, s_plo, t - 1, 1)
                        nc.scalar.activation(probs[:], scores[:], ACT.Exp, scale=SCALE).then_inc(s_exp.sem, 1)
                        after(act, s_pv, t - 1, 2)
                        nc.scalar.activation(p_hi[:], scores[:], ACT.Exp, scale=SCALE).then_inc(s_exp.sem, 1)
                        high_half(t + 2, u)

            @block.vector
            def _(dve):
                dve.sem_inc(s_plo.sem, 2)
                dve.sem_inc(s_inv.sem, 2)
                dve.sem_inc(s_out.sem, 2)
                dve.wait_ge(s_in, 64)

                def lo_w(r):
                    after(dve, s_whi, r, 1)
                    nc.vector.tensor_tensor(w_lo[:], w_raw[:], as_f32(w_hi[:]), ALU.subtract).then_inc(s_wlo.sem, 1)

                def rope(r):
                    after(dve, s_evac, r, 2)
                    after(dve, s_swap, r, 4)
                    nc.vector.tensor_tensor(z[:], z[:], cos[:], ALU.mult).then_inc(s_rope.sem, 1)
                    after(dve, s_rope, r, 1)
                    after(dve, s_sin, r, 1)
                    nc.vector.tensor_tensor(z[:], z[:], z_swap[:], ALU.add).then_inc(s_rope.sem, 1)

                def low_half(r, u):
                    after(dve, s_hi, r, 1)
                    nc.vector.tensor_tensor(q_lo[u][:], z[:], as_f32(q_hi[u][:]), ALU.subtract).then_inc(s_lo.sem, 1)

                def reduce(r, first=False):
                    if not first:
                        after(dve, s_turn, r - 1, 1)
                    for i in range(2):
                        after(dve, s_max, r, i + 1)
                        dst = row_max[:].rearrange("p h q -> p q h")[:, 4 * i:4 * i + 4]
                        nc.vector.tensor_reduce(dst, work[:, halves[i]].rearrange("p (q h m) -> p q h m", h=2, m=M), AX.X,
                                                ALU.max).then_inc(s_mred.sem, 1)

                def shift(r):
                    after(dve, s_turn, r, 1)
                    after(dve, s_score, r - 1, 1)
                    turned = scores[0:2 * KT, 0:P].unsqueeze(1).to_broadcast([2 * KT, KT, P])
                    nc.vector.tensor_tensor(neg_max[:], turned, keep.neg_block[:], ALU.mult).then_inc(s_shift.sem, 1)

                lo_w(0)
                rope(0)
                lo_w(1)
                low_half(0, 0)
                rope(1)
                lo_w(2)
                low_half(1, 1)
                reduce(0, first=True)
                shift(0)
                with dve.Fori(0, PAIRS // 2) as i:
                    for u in range(2):
                        t = 2 * i + u
                        reduce(t + 1)
                        lo_w(t + 3)
                        after(dve, s_exp, t, 2)
                        after(dve, s_pv, t - 1, 2)
                        nc.vector.tensor_tensor(p_lo[:], probs[:], as_f32(p_hi[:]), ALU.subtract).then_inc(s_plo.sem, 1)
                        rope(t + 2)
                        after(dve, s_pv, t, 1)
                        after(dve, s_out, t - 1, 1)
                        nc.vector.reciprocal(inv_sum[:], sum_ps[:]).then_inc(s_inv.sem, 1)
                        shift(t + 1)
                        low_half(t + 2, u)
                        after(dve, s_inv, t, 1)
                        after(dve, s_pv, t, 2)
                        after(dve, s_store, t - 1, 1)
                        nc.vector.tensor_tensor(o_sb[:], o_ps[:], inv_sum[:], ALU.mult).then_inc(s_out.sem, 1)

def phase_feed_forward(nc, io, keep, sem, out):
    tiles, ring, skew = F // P, 4, 2
    with ExitStack() as ctx:
        sb = lambda n, s, d: ctx.enter_context(nc.sbuf_tensor(f"ff_{n}", s, d))
        ps = lambda n, s, d: ctx.enter_context(nc.psum_tensor(f"ff_{n}", s, d))
        w1_raw = sb("w1_raw", [P, KD, F], F32)
        w1_hi = sb("w1_hi", [P, KD, F], F32R)
        w1_lo = sb("w1_lo", [P, KD, F], F32R)
        w2_raw = sb("w2_raw", [P, tiles, D], F32)
        w2_hi = sb("w2_hi", [P, tiles, D], F32R)
        w2_lo = sb("w2_lo", [P, tiles, D], F32R)
        b1 = sb("b1", [P, tiles], F32)
        bias_row = sb("bias", [P, D], F32)
        hidden = sb("hidden", [P, ring, HALF], F32)
        h_hi = sb("h_hi", [P, ring, HALF], F32R)
        h_lo = sb("h_lo", [P, ring, HALF], F32R)
        x_bias = sb("x_bias", [P, GT, D], F32)
        out_sb = sb("out_sb", [P, GT, D], F32)
        h_ps = [ps(f"h_ps{i}", [P, HALF], F32) for i in range(ring)]
        acc = [ps(f"acc{j}", [P, HALF], F32) for j in range(GT)]
        s_w = sem("ff_w")
        s_w_hi = sem("ff_w_hi")
        s_w_lo = sem("ff_w_lo")
        s_hmm = Counter(sem("ff_hmm"), tiles)
        s_gelu = Counter(sem("ff_gelu"), tiles, start=tiles)
        s_hi = Counter(sem("ff_hi"), tiles)
        s_lo = Counter(sem("ff_lo"), tiles, start=tiles)
        s_mm = Counter(sem("ff_mm"), tiles, start=tiles)
        s_xb = Counter(sem("ff_xb"), GT)
        s_out = Counter(sem("ff_out"), GT, start=GT)
        s_store = Counter(sem("ff_store"), 1, 16, start=0)
        out_d = out.rearrange("(g j p) d -> g p j d", p=P, j=GT)

        def before(g, i, back):
            return (g, i - back + 1) if i >= back else (g - 1, i - back + 1 + tiles)

        with nc.Block() as block:
            @block.sync
            def _(sp):
                sp.dma_start(w1_raw[:], io["ff_w1"].rearrange("(k p) f -> p k f", p=P)).then_inc(s_w, 16)
                sp.dma_start(w2_raw[:], io["ff_w2"].rearrange("(i p) d -> p i d", p=P)).then_inc(s_w, 16)
                sp.dma_start(b1[:], io["ff_b1"]).then_inc(s_w, 16)
                sp.dma_start(bias_row[:], io["ff_b2"].partition_broadcast(P)).then_inc(s_w, 16)
                with sp.Fori(0, GROUPS) as g:
                    after_sp(sp, s_out, g, GT, keep.s_carrier)
                    sp.dma_start(out_d[bass.ds(g, 1)].rearrange("o p j d -> (o p) j d"), out_sb[:]) \
                      .then_inc(s_store.sem, 16)
                after_sp(sp, s_store, GROUPS - 1, 1, keep.s_carrier)

            @block.gpsimd
            def _(pool):
                pool.wait_ge(s_w, 64)
                with pool.Fori(0, GROUPS) as g:
                    after(pool, s_out, g - 1, GT)
                    for j in range(GT):
                        src = keep.x[:, bass.ds(g * GT + j, 1)].rearrange("p o d -> p (o d)")
                        nc.gpsimd.tensor_tensor(x_bias[:, j], src, bias_row[:], ALU.add).then_inc(s_xb.sem, 1)

            @block.scalar
            def _(act):
                act.sem_inc(s_gelu.sem, tiles)
                act.wait_ge(s_w, 64)
                nc.scalar.activation(w1_hi[:], w1_raw[:], ACT.Copy).then_inc(s_w_hi, 1)
                nc.scalar.activation(w2_hi[:], w2_raw[:], ACT.Copy).then_inc(s_w_hi, 1)
                with act.Fori(0, GROUPS) as g:
                    for i in range(tiles):
                        after(act, s_lo, *before(g, i, ring))
                        after(act, s_hmm, g, i + 1)
                        nc.scalar.activation(hidden[:, i % ring], h_ps[i % ring][:], ACT.Gelu, bias=b1[:, i:i + 1]) \
                          .then_inc(s_gelu.sem, 1)
                        after(act, s_mm, *before(g, i, ring))
                        after(act, s_gelu, g, i + 1)
                        nc.scalar.activation(h_hi[:, i % ring], hidden[:, i % ring], ACT.Copy).then_inc(s_hi.sem, 1)

            @block.tensor
            def _(pe):
                pe.sem_inc(s_mm.sem, tiles)
                pe.wait_ge(s_w_hi, 2)
                pe.wait_ge(s_w_lo, 2)

                def hidden_products(g, i):
                    after(pe, s_gelu, *before(g, i, ring))
                    cols = bass.ds(g * HALF, HALF)
                    steps = [(w, x, k) for k in range(KD) for w, x in split_products(w1_hi, w1_lo, keep.xt_hi, keep.xt_lo)]
                    for n, (w, x, k) in enumerate(steps):
                        mm = nc.tensor.matmul(h_ps[i % ring][:], w[:, k, i * P:(i + 1) * P], x[:, k, cols],
                                              start=(n == 0), stop=(n == len(steps) - 1))
                    mm.then_inc(s_hmm.sem, 1)

                def out_products(g, i):
                    after(pe, s_hi, g, i + 1)
                    after(pe, s_lo, g, i + 1)
                    if i == 0:
                        after(pe, s_out, g - 1, GT)
                    for j in range(GT):
                        for n, (h, w) in enumerate(split_products(h_hi, h_lo, w2_hi, w2_lo)):
                            mm = nc.tensor.matmul(acc[j][:, 0:D], h[:, i % ring, j * P:(j + 1) * P], w[:, i],
                                                  start=(i == 0 and n == 0), stop=(i == tiles - 1 and n == 2))
                    mm.then_inc(s_mm.sem, 1)

                def group(g, first=False):
                    for i in range(tiles):
                        hidden_products(g, i)
                        if i >= skew:
                            out_products(g, i - skew)
                        elif not first:
                            out_products(g - 1, i - skew + tiles)

                group(0, first=True)
                with pe.Fori(1, GROUPS) as g:
                    group(g)
                for i in range(tiles - skew, tiles):
                    out_products(GROUPS - 1, i)

            @block.vector
            def _(dve):
                dve.sem_inc(s_lo.sem, tiles)
                dve.sem_inc(s_out.sem, GT)
                for n, (raw, hi, lo) in enumerate(((w1_raw, w1_hi, w1_lo), (w2_raw, w2_hi, w2_lo))):
                    dve.wait_ge(s_w_hi, n + 1)
                    nc.vector.tensor_tensor(lo[:], raw[:], as_f32(hi[:]), ALU.subtract).then_inc(s_w_lo, 1)

                def low_halves(g, i):
                    after(dve, s_hi, g, i + 1)
                    nc.vector.tensor_tensor(h_lo[:, i % ring], hidden[:, i % ring], as_f32(h_hi[:, i % ring]),
                                            ALU.subtract).then_inc(s_lo.sem, 1)

                def sums(g, stored):
                    after(dve, s_mm, g, tiles)
                    after(dve, s_xb, g, GT)
                    if stored:
                        after(dve, s_store, g - 1, 1)
                    for j in range(GT):
                        nc.vector.tensor_tensor(out_sb[:, j], acc[j][:, 0:D], x_bias[:, j], ALU.add) \
                          .then_inc(s_out.sem, 1)

                def group(g, last_sums):
                    for i in range(tiles):
                        low_halves(g, i)
                        if i == skew:
                            last_sums()

                group(0, lambda: None)
                group(1, lambda: sums(0, False))
                with dve.Fori(2, GROUPS) as g:
                    group(g, lambda: sums(g - 1, True))
                sums(GROUPS - 1, True)

class Keep:
    pass


ROPE_ORDER = np.concatenate([np.arange(0, DH, 2), np.arange(1, DH, 2)])


def build(nc, io, out):
    with ExitStack() as used:
        sem = lambda name: used.enter_context(nc.semaphore("s_" + name))
        sb = lambda n, s, d: used.enter_context(nc.sbuf_tensor(n, s, d))
        keep = Keep()
        keep.s_carrier = sem("sp_carrier")
        keep.ident = sb("ident_sb", [P, P], F32)
        keep.neg_block = sb("neg_block_sb", [2 * KT, KT, P], F32)
        keep.mod_a = sb("mod_a", [P, 2, KD, B], F32)
        keep.mod_c = sb("mod_c", [P, 2, KD, B], F32)
        keep.xt_hi = sb("xt_hi", [P, KD, TOK], F32R)
        keep.xt_lo = sb("xt_lo", [P, KD, TOK], F32R)
        o_self = nc.dram_tensor("o_self", [PAIRS + 1, P, N], F32, kind="Internal").ap()
        o_cross = nc.dram_tensor("o_cross", [PAIRS, P, N], F32, kind="Internal").ap()
        kv_ctx = nc.dram_tensor("kv_ctx", [PAIRS, P, 4 * P], F32, kind="Internal").ap()
        phase_setup(nc, io, keep, sem)
        phase_first_norm(nc, io, keep, sem)
        phase_self_attention(nc, io, keep, sem, o_self)
        keep.x = sb("x_rows", [P, TOK // P, D], F32)
        phase_project(nc, io, keep, sem, "po", o_self[1:PAIRS + 1], "sa_wo", "sa_bo", 0)
        phase_context(nc, io, keep, sem, kv_ctx)
        phase_cross_attention(nc, io, keep, sem, kv_ctx, o_cross)
        phase_project(nc, io, keep, sem, "pc", o_cross, "ca_wo", "ca_bo", 1)
        phase_feed_forward(nc, io, keep, sem, out)

def table(positions):
    f32 = np.float32
    inv = (f32(1.0) / np.power(f32(10000.0), np.arange(0, DH, 2, dtype=f32) / f32(DH))).astype(f32)
    ang = (inv[:, None] * np.arange(positions, dtype=f32)[None, :]).astype(f32)
    c, s = np.cos(ang).astype(f32), np.sin(ang).astype(f32)
    return np.ascontiguousarray(np.tile(c, (4, 1))), np.ascontiguousarray(np.concatenate([-s, s, -s, s]))


def layouts(inputs):
    get = lambda n: np.asarray(inputs["L0_xcond_" + n])
    cols = lambda v: v.reshape(KD, P).T
    order = (np.arange(H)[:, None] * DH + ROPE_ORDER[None, :]).reshape(-1)
    block = np.zeros((16, KT, P), np.float32)
    for r in range(16):
        block[r, r % KT] = -1.0
    cos, sin = table(N)
    pair = lambda w: w.reshape(w.shape[0], HP, P)
    wkv = get("sa_wkv")
    w_self = np.stack([pair(get("sa_wq")[:, order]), pair(wkv[:, :MID][:, order]), pair(wkv[:, MID:])], 2)
    w_self = w_self.reshape(KD, P, HP, 3, P).transpose(2, 1, 0, 3, 4)
    heads = np.zeros((2 * KT, P), np.float32)
    ones = np.zeros((P, P), np.float32)
    for h in range(2):
        heads[h * KT:(h + 1) * KT, h * M:(h + 1) * M] = 1.0
        ones[h * M:(h + 1) * M, h * DH:(h + 1) * DH] = 1.0
    ckv = get("ca_wkv")
    pad = np.zeros((2 * P, HP, 2, P), np.float32)
    pad[:DC] = np.stack([pair(ckv[:, :MID][:, order]), pair(ckv[:, MID:])], 2)
    vec_pad = lambda v: np.concatenate([v, np.zeros(2 * P - DC, np.float32)])
    vecs = [get(n) for n in ("ln1_w", "ln1_b", "ln2_w", "ln2_b", "g1_b", "b1_b", "g2_b", "b2_b")]
    arrays = {
        "x": np.asarray(inputs["x"]).reshape(TOK, D),
        "cond": np.asarray(inputs["cond_1024"]).reshape(B, KD, P).transpose(2, 1, 0).reshape(P, KD * B),
        "gate_vec": np.stack([cols(v) for v in vecs], 1).reshape(P, -1),
        "gate_w0": get("g1_w"), "gate_w1": get("b1_w"), "gate_w2": get("g2_w"), "gate_w3": get("b2_w"),
        "ident": np.eye(P, dtype=np.float32), "neg_block": block.reshape(16, KT * P), "cos": cos, "sin": sin,
        "w_self": w_self, "heads": heads, "ones_block": ones,
        "w_ctx": pad.reshape(2, P, HP, 2, P).transpose(2, 1, 0, 3, 4),
        "w_cross": pair(get("ca_wq")[:, order]).reshape(KD, P, HP, P).transpose(2, 1, 0, 3),
        "ctx": np.asarray(inputs["ctx_768"]).reshape(B * M, DC),
        "lnc_w": cols(vec_pad(get("ca_lnc_w"))), "lnc_b": cols(vec_pad(get("ca_lnc_b"))),
        "sa_wo": get("sa_wo"), "sa_bo": get("sa_bo"), "ca_wo": get("ca_wo"), "ca_bo": get("ca_bo"),
        "ff_w1": get("ff_w1"), "ff_b1": get("ff_b1").reshape(F // P, P).T, "ff_w2": get("ff_w2"),
        "ff_b2": get("ff_b2"),
    }
    return {n: np.ascontiguousarray(a) for n, a in arrays.items()}



def kernel(**inputs):
    import concourse.bacc as bacc
    from concourse.bass_utils import run_bass_kernel_spmd

    nc = bacc.Bacc("TRN2", target_bir_lowering=False, num_devices=1)
    arrays = {f"in_{n}": a for n, a in layouts(inputs).items()}
    io = {n[3:]: nc.dram_tensor(n, a.shape, mybir.dt.from_np(a.dtype), kind="ExternalInput").ap()
          for n, a in arrays.items()}
    out = nc.dram_tensor("out_rows", (TOK, D), F32, kind="ExternalOutput").ap()
    build(nc, io, out)
    result = run_bass_kernel_spmd(nc, [arrays], core_ids=[0])
    return result.results[0]["out_rows"].reshape(B, N, D)
```

```python
from contextlib import ExitStack

import numpy as np

import concourse.bass as bass
from concourse import mybir

F32 = mybir.dt.float32
F32R = mybir.dt.float32r
ALU = mybir.AluOpType
ACT = mybir.ActivationFunctionType
AX = mybir.AxisListType

P = 128
B, N, D = 4, 1024, 256
H, DH = 16, 64
MID = H * DH
M, DC = 64, 192
F = 4 * D
KD = D // P
HP = H // 2
PAIRS = HP * B
KT = N // P
HALF = 512
TOK = B * N
GROUPS = TOK // HALF
GT = HALF // P
EPS = 1e-5
SCALE = DH ** -0.5
PREP_JOBS = 44


class Counter:

    def __init__(self, sem, per_round, step=1, start=0):
        self.sem, self.per, self.step, self.start = sem, per_round, step, start

    def at(self, r, n):
        return (r * self.per + n) * self.step + self.start


def after(eng, counter, r, n):
    eng.wait_ge(counter.sem, counter.at(r, n))


def after_sp(sp, counter, r, n, carrier):
    sp.wait_ge(counter.sem, counter.at(r, n))
    sp.sem_inc(carrier, 1)


def split_products(hi_a, lo_a, hi_b, lo_b):
    return ((hi_a, hi_b), (hi_a, lo_b), (lo_a, hi_b))


def as_f32(ap):
    return ap.bitcast(F32)


class NormCounters:

    def __init__(self, sem):
        self.norms = 0
        self.half = sem("norm_half")
        self.stat = Counter(sem("norm_stat"), GT)
        self.mom = Counter(sem("norm_mom"), GT)
        self.var = Counter(sem("norm_var"), 1)
        self.rstd = Counter(sem("norm_rstd"), 1)
        self.xn = Counter(sem("norm_xn"), GT, start=GT)
        self.turned = Counter(sem("norm_turned"), KD, start=KD)
        self.mod = Counter(sem("norm_mod"), 2 * KD, start=2 * KD)
        self.lo = Counter(sem("norm_lo"), KD, start=KD)

    def all_passed(self):
        self.norms += 1
        for c in (self.stat, self.mom, self.var, self.rstd, self.xn, self.turned, self.mod, self.lo):
            c.start += GROUPS * c.per * c.step


class Layernorm:

    def __init__(self, nc, sb, ps, count, name, carrier):
        self.stats = sb(f"{name}_stats", [P, GT, 6], F32)
        self.moments = sb(f"{name}_moments", [P, GT, 2], F32)
        self.var_eps = sb(f"{name}_var_eps", [P, GT], F32)
        self.rstd = sb(f"{name}_rstd", [P, GT], F32)
        self.minus_half = sb(f"{name}_minus_half", [P, GT], F32)
        self.xn = sb(f"{name}_xn", [P, GT, D], F32)
        self.y = sb(f"{name}_y", [P, KD, HALF], F32)
        self.turned = [ps(f"{name}_turned{k}", [P, HALF], F32) for k in range(KD)]
        self.count = count
        self.s_carrier = carrier
        self.s_stat, self.s_mom, self.s_var, self.s_rstd = count.stat, count.mom, count.var, count.rstd
        self.s_xn, self.s_turned, self.s_mod, self.s_lo = count.xn, count.turned, count.mod, count.lo

    def start_dve(self, nc, dve):
        nc.vector.memset(self.minus_half[:], -0.5).then_inc(self.count.half, 1)
        if self.count.norms == 0:
            dve.sem_inc(self.s_xn.sem, GT)
            dve.sem_inc(self.s_lo.sem, KD)

    def start_pe(self, pe):
        if self.count.norms == 0:
            pe.sem_inc(self.s_turned.sem, KD)

    def start_act(self, act):
        if self.count.norms == 0:
            act.sem_inc(self.s_mod.sem, 2 * KD)

    def start_pool(self, pool):
        pool.wait_ge(self.count.half, self.count.norms + 1)


class Weights:

    def __init__(self, sb, sem, name, parts):
        self.tile = {n: sb(f"{name}_{n}", shape, F32) for n, (shape, _) in parts.items()}
        self.source = {n: source for n, (_, source) in parts.items()}
        self.loaded = sem(f"{name}_loaded")
        self.total = 16 * len(parts)

    def load(self, sp):
        for n, tile in self.tile.items():
            sp.dma_start(tile[:], self.source[n]).then_inc(self.loaded, 16)


def phase_setup(nc, io, keep, sem):
    with ExitStack() as ctx:
        sb = lambda n, s, d: ctx.enter_context(nc.sbuf_tensor(n, s, d))
        ps = lambda n, s, d: ctx.enter_context(nc.psum_tensor(n, s, d))
        cond = sb("cond", [P, KD, B], F32)
        gw = sb("gate_weights", [P, 4, KD, D], F32)
        vec = sb("gate_vectors", [P, 8, KD], F32)
        gate = sb("gates", [P, 4, KD, B], F32)
        gate_ps = ps("gate_ps", [P, 4, KD, B], F32)
        s_in, s_mm, s_g, s_f = (sem(f"setup_{n}") for n in ("in", "mm", "g", "f"))
        loads = [(keep.ident[:], io["ident"]), (keep.neg_block[:], io["neg_block"].rearrange("p (a q) -> p a q", q=P)),
                 (cond[:], io["cond"].rearrange("p (k b) -> p k b", b=B)),
                 (vec[:], io["gate_vec"].rearrange("p (v k) -> p v k", k=KD))]
        loads += [(gw[:, n], io[f"gate_w{n}"].rearrange("(k p) d -> p k d", p=P)) for n in range(4)]
        with nc.Block() as block:
            @block.sync
            def _(sp):
                for dst, src in loads:
                    sp.dma_start(dst, src).then_inc(s_in, 16)

            @block.tensor
            def _(pe):
                pe.wait_ge(s_in, 16 * len(loads))
                for n in range(4):
                    for k_out in range(KD):
                        for k in range(KD):
                            mm = nc.tensor.matmul(gate_ps[:, n, k_out], gw[:, n, k, k_out * P:(k_out + 1) * P],
                                                  cond[:, k], start=(k == 0), stop=(k == KD - 1))
                mm.then_inc(s_mm, 1)

            @block.vector
            def _(dve):
                dve.wait_ge(s_in, 16 * len(loads))
                dve.wait_ge(s_mm, 1)
                for n in range(4):
                    for k in range(KD):
                        last = nc.vector.tensor_scalar(gate[:, n, k], gate_ps[:, n, k], vec[:, 4 + n, k:k + 1],
                                                       1.0 if n % 2 == 0 else 0.0, ALU.add, ALU.add)
                last.then_inc(s_g, 1)
                dve.wait_ge(s_g, 1)
                for m in range(2):
                    for k in range(KD):
                        nc.vector.tensor_scalar(keep.mod_a[:, m, k], gate[:, 2 * m, k], vec[:, 2 * m, k:k + 1], None,
                                                ALU.mult).then_inc(s_f, 1)
                        nc.vector.scalar_tensor_tensor(out=keep.mod_c[:, m, k], in0=gate[:, 2 * m, k],
                                                       scalar=vec[:, 2 * m + 1, k:k + 1], in1=gate[:, 2 * m + 1, k],
                                                       op0=ALU.mult, op1=ALU.add).then_inc(s_f, 1)


def dve_statistics(nc, ln, x_tile):
    for j in range(GT):
        nc.vector.bn_stats(ln.stats[:, j], x_tile(j)).then_inc(ln.s_stat.sem, 1)


def dve_moments(nc, dve, ln, g):
    after(dve, ln.s_xn, g - 1, GT)
    for j in range(GT):
        after(dve, ln.s_stat, g, j + 1)
        dve.sem_inc(ln.s_carrier, 1)
        nc.vector.bn_aggr(ln.moments[:, j], ln.stats[:, j]).then_inc(ln.s_mom.sem, 1)
    after(dve, ln.s_mom, g, GT)
    nc.vector.tensor_scalar(ln.var_eps[:], ln.moments[:, :, 1], EPS, None, ALU.add).then_inc(ln.s_var.sem, 1)


def dve_normalised(nc, dve, ln, x_tile, g):
    after(dve, ln.s_rstd, g, 1)
    after(dve, ln.s_turned, g - 1, KD)
    for j in range(GT):
        nc.vector.tensor_scalar(ln.xn[:, j], x_tile(j), ln.moments[:, j, 0:1], ln.rstd[:, j:j + 1],
                                ALU.subtract, ALU.mult).then_inc(ln.s_xn.sem, 1)


def pool_rstd(nc, pool, ln, g):
    after(pool, ln.s_var, g, 1)
    nc.gpsimd.tensor_tensor(ln.rstd[:], ln.var_eps[:], ln.minus_half[:], ALU.pow).then_inc(ln.s_rstd.sem, 1)


def pe_turn(nc, pe, ln, ident, g):
    after(pe, ln.s_mod, g - 1, 2 * KD)
    for k in range(KD):
        for j in range(GT):
            if k == 0:
                after(pe, ln.s_xn, g, j + 1)
            mm = nc.tensor.transpose(ln.turned[k][:, j * P:(j + 1) * P], ln.xn[:, j, k * P:(k + 1) * P], ident)
        mm.then_inc(ln.s_turned.sem, 1)


def act_modulate(nc, act, ln, keep, m, g):
    batch = g // (N // HALF)
    after(act, ln.s_lo, g - 1, KD)
    for k in range(KD):
        after(act, ln.s_turned, g, k + 1)
        scale = keep.mod_a[:, m, k, bass.ds(batch, 1)]
        bias = keep.mod_c[:, m, k, bass.ds(batch, 1)]
        nc.scalar.activation(ln.y[:, k], ln.turned[k][:], ACT.Identity, scale=scale,
                             bias=bias).then_inc(ln.s_mod.sem, 1)
        nc.scalar.activation(keep.xt_hi[:, k, bass.ds(g * HALF, HALF)], ln.turned[k][:], ACT.Identity, scale=scale,
                             bias=bias).then_inc(ln.s_mod.sem, 1)


def dve_modulated_lo(nc, dve, ln, keep, g):
    for k in range(KD):
        after(dve, ln.s_mod, g, 2 * k + 2)
        cols = bass.ds(g * HALF, HALF)
        nc.vector.tensor_tensor(keep.xt_lo[:, k, cols], ln.y[:, k], as_f32(keep.xt_hi[:, k, cols]),
                                ALU.subtract).then_inc(ln.s_lo.sem, 1)


def phase_first_norm(nc, io, keep, sem):
    with ExitStack() as ctx:
        sb = lambda n, s, d: ctx.enter_context(nc.sbuf_tensor(n, s, d))
        ps = lambda n, s, d: ctx.enter_context(nc.psum_tensor(n, s, d))
        ln = Layernorm(nc, sb, ps, keep.norm_counters, "n1", keep.s_carrier)
        x_sb = sb("x_first", [P, 2, GT, D], F32)
        s_x = [Counter(sem(f"n1_x{u}"), 1, 16) for u in range(2)]
        s_used = Counter(sem("n1_x_used"), 1, start=2)
        x_d = io["x"].rearrange("(g j p) d -> g p j d", p=P, j=GT)
        with nc.Block() as block:
            @block.sync
            def _(sp):
                with sp.Fori(0, GROUPS // 2) as i:
                    for u in range(2):
                        after_sp(sp, s_used, 2 * i + u - 2, 1, keep.s_carrier)
                        sp.dma_start(x_sb[:, u], x_d[2 * i + u]).then_inc(s_x[u].sem, 16)

            @block.vector
            def _(dve):
                ln.start_dve(nc, dve)
                dve.sem_inc(s_used.sem, 2)

                def statistics(i, u):
                    after(dve, s_x[u], i, 1)
                    dve.sem_inc(keep.s_carrier, 1)
                    dve_statistics(nc, ln, lambda j: x_sb[:, u, j])

                def group(i, u, first=False, last=False):
                    g = 2 * i + u
                    if not last:
                        statistics(i + u, 1 - u)
                    dve_normalised(nc, dve, ln, lambda j: x_sb[:, u, j], g)
                    if not first:
                        dve_modulated_lo(nc, dve, ln, keep, g - 1)
                    after(dve, ln.s_xn, g, GT)
                    dve.sem_inc(s_used.sem, 1)
                    if not last:
                        dve_moments(nc, dve, ln, g + 1)

                statistics(0, 0)
                dve_moments(nc, dve, ln, 0)
                group(0, 0, first=True)
                group(0, 1)
                with dve.Fori(1, GROUPS // 2 - 1) as i:
                    for u in range(2):
                        group(i, u)
                group(GROUPS // 2 - 1, 0)
                group(GROUPS // 2 - 1, 1, last=True)
                dve_modulated_lo(nc, dve, ln, keep, GROUPS - 1)

            @block.gpsimd
            def _(pool):
                ln.start_pool(pool)
                with pool.Fori(0, GROUPS) as g:
                    pool_rstd(nc, pool, ln, g)

            @block.tensor
            def _(pe):
                ln.start_pe(pe)
                with pe.Fori(0, GROUPS) as g:
                    pe_turn(nc, pe, ln, keep.ident[:], g)

            @block.scalar
            def _(act):
                ln.start_act(act)
                with act.Fori(0, GROUPS) as g:
                    act_modulate(nc, act, ln, keep, 0, g)



def phase_self_attention(nc, io, keep, sem, o_dram):
    with ExitStack() as ctx:
        sb = lambda n, s, d: ctx.enter_context(nc.sbuf_tensor(n, s, d))
        ps = lambda n, s, d: ctx.enter_context(nc.psum_tensor(n, s, d))
        w_raw = sb("w_raw", [P, KD, 3, P], F32)
        w_hi = sb("w_hi", [P, KD, 3, P], F32R)
        w_lo = sb("w_lo", [P, KD, 3, P], F32R)
        cos = sb("cos", [P, N], F32)
        sin = sb("sin", [P, N], F32)
        z = [sb("q_rows", [P, N], F32), sb("k_rows", [P, N], F32)]
        z_swap = [sb("q_swapped", [P, N], F32), sb("k_swapped", [P, N], F32)]
        vt = sb("v_turned", [P, N], F32)
        q1 = [sb(f"q_first{u}", [P, 2, N], F32R) for u in range(2)]
        q2 = [sb(f"q_second{u}", [P, 2, N], F32R) for u in range(2)]
        k1 = [sb(f"k_first{u}", [P, 2, N], F32R) for u in range(2)]
        k2 = [sb(f"k_second{u}", [P, 2, N], F32R) for u in range(2)]
        v = [sb(f"v_tokens{u}", [P, KT, P], F32) for u in range(2)]
        maxima = sb("maxima", [P, 2, KT, 2], F32)
        row_max = sb("row_max", [P, 2, KT], F32)
        probs = [[sb(f"probs{h}{i}", [P, N], F32) for i in range(2)] for h in range(2)]
        sums = [sb(f"sums{h}", [P, N], F32) for h in range(2)]
        o_raw = sb("o_raw", [P, N], F32)
        compact = sb("compact_sums", [P, 2 * N // P], F32)
        ones = sb("ones", [P, DH], F32)
        scores = [ps(f"scores{h}", [P, N], F32) for h in range(2)]
        o_ps = ps("o_ps", [P, N], F32)
        work = ps("work", [P, 2, HALF], F32)

        divisor = z_swap[1]
        s_const = sem("sa_const")
        n_const = 4
        s_table = sem("sa_table")
        s_zero = sem("sa_zero")
        s_w = Counter(sem("sa_w"), 1, 16)
        s_whi = Counter(sem("sa_whi"), 1)
        s_wlo = Counter(sem("sa_wlo"), 1)
        s_proj, s_proj_read = (Counter(sem(f"sa_{n}"), 6) for n in ("proj", "proj_read"))
        s_vturn, s_vturn_read = (Counter(sem(f"sa_{n}"), 2) for n in ("vturn", "vturn_read"))
        s_max, s_max_read = (Counter(sem(f"sa_{n}"), 4 * KT) for n in ("max", "max_read"))
        s_turn, s_turn_read = (Counter(sem(f"sa_{n}"), 2) for n in ("turn", "turn_read"))
        s_sum, s_sum_read = (Counter(sem(f"sa_{n}"), 2, start=2) for n in ("sum", "sum_read"))
        s_swap = [Counter(sem(f"sa_swap{n}"), 2, 16) for n in range(2)]
        s_sin = Counter(sem("sa_sin"), 2)
        s_rope = Counter(sem("sa_rope"), 4)
        s_qhi = Counter(sem("sa_qhi"), 4)
        s_khi = Counter(sem("sa_khi"), 4)
        s_qlo = Counter(sem("sa_qlo"), 2)
        s_klo = Counter(sem("sa_klo"), 2)
        s_comb = Counter(sem("sa_comb"), 2)
        s_score = Counter(sem("sa_score"), 2 * KT)
        s_exp = Counter(sem("sa_exp"), 2 * KT)
        s_pv = Counter(sem("sa_pv"), KT, start=KT)
        s_acc = Counter(sem("sa_acc"), 2 * (KT - 1), start=2 * (KT - 1))
        s_oraw = Counter(sem("sa_oraw"), 1, start=1)
        s_sum_out = Counter(sem("sa_sum_out"), 1, 16, start=16)
        s_sum_in = Counter(sem("sa_sum_in"), 1, 16, start=16)
        s_recip = Counter(sem("sa_recip"), 1, start=1)
        s_inv_out = Counter(sem("sa_inv_out"), 1, 16, start=16)
        s_inv_in = Counter(sem("sa_inv_in"), 2, 16, start=32)
        s_norm = Counter(sem("sa_norm"), 1, start=2)
        s_store = Counter(sem("sa_store"), 1, 16, start=32)

        heads_max = [[("max", h, i) for i in range(2 * KT)] for h in range(2)]
        order = heads_max[0] + heads_max[1][:2] + [("turn", 0, 0)] + heads_max[1][2:]
        proj = [("proj", zz, half) for zz in range(3) for half in range(2)]
        slots = {(0, 1): [("sum", 0, 0)], (0, 3): [("sum", 0, 1)], (1, 0): [("vturn", 0, 0)], (1, 1): [("vturn", 0, 1)],
                 (6, 5): [("turn", 1, 0)]}
        slots.update({(2 + n // 2, 2 + 3 * (n % 2)): [proj[n]] for n in range(6)})
        counts = {1: (0, 0, 2, 1, 2, 2), 2: (1, 1, 0, 1, 2, 0), 3: (1, 1, 0, 2, 2, 0), 4: (1, 1, 0, 1, 2, 0),
                  5: (1, 1, 0, 1, 2, 1), 6: (1, 1, 1, 1, 0, 0)}
        rest = iter(order)
        for kt, numbers in counts.items():
            slots.update({(kt, slot): [next(rest) for _ in range(n)] for slot, n in enumerate(numbers) if n})
        assert next(rest, None) is None
        jobs = [job for where in sorted(slots) for job in slots[where]]
        assert len(jobs) == PREP_JOBS
        index = {job: n for n, job in enumerate(jobs)}
        sums_d = nc.dram_tensor("sums_d", [2, N], F32, kind="Internal").ap()
        inv_d = nc.dram_tensor("inv_d", [2, N], F32, kind="Internal").ap()
        compact_view = lambda d: d.rearrange("h (a b) -> (h a) b", b=2 * N // P)

        def job_read(eng, t, n):
            if isinstance(t, int) and t < 0 and n < 4:
                after(eng, s_proj_read, 0, 6)
                return
            t, n = (t, n - 2) if n >= 2 else (t - 1, n - 2 + PREP_JOBS)
            kind, h, i = jobs[n]
            read, pair, event = {"sum": (s_sum_read, t - 1, i), "vturn": (s_vturn_read, t + 1, i),
                                 "max": (s_max_read, t + 1, h * 2 * KT + i), "turn": (s_turn_read, t + 1, h),
                                 "proj": (s_proj_read, t + 2, 2 * h + i)}[kind]
            after(eng, read, pair, event + 1)

        def add_index(kt, h):
            return (max(kt, 1) - 1) * 2 + h + 1

        def next_tile(t, kt, u):
            return (t, kt + 1, u) if kt < KT - 1 else (t + 1, 0, 1 - u)

        x_cols = lambda xt, k, b, half: xt[:, k, bass.ds(b * N + half * HALF, HALF)]
        top, bot = slice(0, DH), slice(DH, P)

        with nc.Block() as block:
            @block.sync
            def _(sp):
                wait = lambda counter, r, n: after_sp(sp, counter, r, n, keep.s_carrier)
                sp.dma_start(cos[:], io["cos"]).then_inc(s_table, 16)
                sp.dma_start(sin[:], io["sin"]).then_inc(s_table, 16)
                sp.dma_start(w_raw[:], io["w_self"][0]).then_inc(s_w.sem, 16)

                def swap(n, p, first=False):
                    wait(s_proj_read, p, 2 * n + 2)
                    if not first:
                        wait(s_rope, p - 1, 2 * n + 2)
                    if n == 1 and not isinstance(p, int):
                        wait(s_norm, p - 3, 1)
                    for q in range(2):
                        sp.dma_start(z_swap[n][q:P:2], z[n][1 - q:P:2]).then_inc(s_swap[n].sem, 16)

                def weights(p):
                    wait(s_whi, p - 1, 1)
                    wait(s_wlo, p - 1, 1)
                    src = io["w_self"][bass.ds((p // B) % HP, 1)].rearrange("o p k z m -> (o p) k z m")
                    sp.dma_start(w_raw[:], src).then_inc(s_w.sem, 16)

                def divisors(t):
                    wait(s_sum_read, t, 2)
                    sp.dma_start(sums_d, divisor[0:P:DH]).then_inc(s_sum_out.sem, 16)
                    wait(s_sum_out, t, 1)
                    sp.dma_start(compact[:], compact_view(sums_d)).then_inc(s_sum_in.sem, 16)
                    wait(s_recip, t, 1)
                    sp.dma_start(compact_view(inv_d), compact[:]).then_inc(s_inv_out.sem, 16)
                    wait(s_inv_out, t, 1)
                    for h in range(2):
                        sp.dma_start(divisor[h * DH:(h + 1) * DH], inv_d[h].partition_broadcast(DH)) \
                          .then_inc(s_inv_in.sem, 16)

                def store(t):
                    wait(s_norm, t, 1)
                    sp.dma_start(o_dram[bass.ds(t + 1, 1)].rearrange("o p n -> (o p) n"), o_raw[:]) \
                      .then_inc(s_store.sem, 16)

                swap(0, 0, first=True)
                swap(1, 0, first=True)
                weights(1)
                swap(0, 1)
                swap(1, 1)
                weights(2)
                with sp.Fori(0, PAIRS // 2) as i:
                    for u in range(2):
                        t = 2 * i + u
                        divisors(t - 1)
                        swap(0, t + 2)
                        swap(1, t + 2)
                        weights(t + 3)
                        store(t - 1)
                store(PAIRS - 1)
                wait(s_store, PAIRS - 1, 1)
                wait(s_w, PAIRS + 2, 1)

            @block.tensor
            def _(pe):
                pe.sem_inc(s_pv.sem, KT)

                def projection(zz, i, p, bank):
                    if (zz, i) == (0, 0):
                        after(pe, s_whi, p, 1)
                        after(pe, s_wlo, p, 1)
                    steps = [(w, x, k) for k in range(KD)
                             for w, x in split_products(w_hi, w_lo, keep.xt_hi, keep.xt_lo)]
                    for m, (w, x, k) in enumerate(steps):
                        mm = nc.tensor.matmul(bank, w[:, k, zz], x_cols(x, k, p % B, i), start=(m == 0),
                                              stop=(m == len(steps) - 1))
                    mm.then_inc(s_proj.sem, 1)

                def column_sums(t, i, n):
                    if i == 0:
                        after(pe, s_acc, t, 2 * (KT - 1))
                    for h in range(2):
                        mm = nc.tensor.matmul(work[h * DH:(h + 1) * DH, n % 2], ones[:],
                                              sums[h][:, i * HALF:(i + 1) * HALF], start=True, stop=True)
                    mm.then_inc(s_sum.sem, 1)

                def run_job(job, t, u):
                    kind, h, i = job
                    n, p = index[job], t + 1
                    job_read(pe, t, n)
                    bank = work[:, n % 2]
                    if kind == "proj":
                        projection(h, i, t + 2, bank)
                    elif kind == "sum":
                        column_sums(t - 1, i, n)
                    elif kind == "vturn":
                        if i == 0:
                            after(pe, s_proj_read, p, 6)
                        for c in range(4):
                            mm = nc.tensor.transpose(work[:, n % 2, c * P:(c + 1) * P],
                                                     vt[:, (4 * i + c) * P:(4 * i + c + 1) * P], keep.ident[:])
                        mm.then_inc(s_vturn.sem, 1)
                    elif kind == "max":
                        if (h, i) == (0, 0):
                            after(pe, s_qhi, p, 4)
                            after(pe, s_klo, p, 2)
                        qt, half = i // 2, i % 2
                        nc.tensor.matmul(bank, q1[1 - u][:, h, qt * P:(qt + 1) * P],
                                         k1[1 - u][:, h, half * HALF:(half + 1) * HALF], start=True, stop=True) \
                          .then_inc(s_max.sem, 1)
                    else:
                        after(pe, s_comb, p, h + 1)
                        nc.tensor.transpose(work[0:KT, n % 2, 0:P], row_max[:, h], keep.ident[:]) \
                          .then_inc(s_turn.sem, 1)

                def qk(t, kt, h, u, part):
                    if part == 0:
                        if kt == 0:
                            if not isinstance(t, int):
                                after(pe, s_exp, t - 1, 2 * KT - 1 + h)
                            after(pe, s_turn_read, t, h + 1)
                            after(pe, s_qlo, t, h + 1)
                        else:
                            after(pe, s_exp, t, 2 * kt - 1 + h)
                    q_side, k_side = ((q1, k1), (q2, k2))[part]
                    for half in range(2):
                        cols = slice(half * HALF, (half + 1) * HALF)
                        mm = nc.tensor.matmul(scores[h][:, cols], k_side[u][:, h, kt * P:(kt + 1) * P],
                                              q_side[u][:, h, cols], start=(part == 0), stop=(part == 1))
                    if part == 1:
                        mm.then_inc(s_score.sem, 1)

                def pv(t, kt, u, half):
                    if half == 0:
                        after(pe, s_exp, t, 2 * kt + 2)
                        if kt == 0:
                            after(pe, s_oraw, t - 1, 1)
                            after(pe, s_vturn_read, t, 2)
                    cols = slice(half * HALF, (half + 1) * HALF)
                    for h in range(2):
                        mm = nc.tensor.matmul(o_ps[h * DH:(h + 1) * DH, cols], v[u][:, kt, h * DH:(h + 1) * DH],
                                              probs[h][kt % 2][:, cols], start=(kt == 0), stop=(kt == KT - 1))
                    if half == 1:
                        mm.then_inc(s_pv.sem, 1)

                for n, (_, zz, i) in enumerate(proj):
                    if n >= 2:
                        after(pe, s_proj_read, 0, n - 1)
                    projection(zz, i, 0, work[:, n % 2])
                for job in jobs:
                    if job[0] != "sum":
                        run_job(job, -1, 1)
                for h in range(2):
                    for part in range(2):
                        qk(0, 0, h, 0, part)
                pe.wait_ge(s_const, n_const)
                with pe.Fori(0, PAIRS // 2) as it:
                    for u in range(2):
                        t = 2 * it + u
                        for kt in range(KT):
                            nt, nk, nu = next_tile(t, kt, u)
                            attention = [lambda h=h, part=part: qk(nt, nk, h, nu, part) for h in range(2)
                                         for part in range(2)]
                            products = [lambda half=half: pv(t, kt, u, half) for half in range(2)]
                            at = 4 if kt < KT - 1 else 2
                            attention[at:at] = products
                            for slot in range(6):
                                attention[slot]()
                                for job in slots.get((kt, slot), []):
                                    run_job(job, t, u)
                job_read(pe, PAIRS, 0)
                job_read(pe, PAIRS, 1)
                for i in range(2):
                    column_sums(PAIRS - 1, i, i)

            @block.scalar
            def _(act):
                def split_w(p, first=False):
                    after(act, s_w, p, 1)
                    if not first:
                        after(act, s_proj, p - 1, 6)
                    nc.scalar.activation(w_hi[:], w_raw[:], ACT.Copy).then_inc(s_whi.sem, 1)

                def rows(job, p, n):
                    _, zz, i = job
                    after(act, s_proj, p, 2 * zz + i + 1)
                    if not (isinstance(p, int) and p == 0) and i == 0:
                        after(act, *((s_qlo, p - 1, 2), (s_klo, p - 1, 2), (s_vturn, p - 1, 2))[zz])
                    dst = (z + [vt])[zz][:, i * HALF:(i + 1) * HALF]
                    nc.scalar.activation(dst, work[:, n % 2], ACT.Copy).then_inc(s_proj_read.sem, 1)

                def evac(job, t, u):
                    n = index[job]
                    kind, h, i = job
                    if kind == "proj":
                        rows(job, t + 2, n)
                    elif kind == "vturn":
                        after(act, s_vturn, t + 1, i + 1)
                        if i == 0 and not isinstance(t, int):
                            after(act, s_pv, t - 1, KT)
                        nc.scalar.activation(v[1 - u][:, 4 * i:4 * i + 4].rearrange("p c m -> p (c m)"),
                                             work[:, n % 2], ACT.Copy).then_inc(s_vturn_read.sem, 1)
                    elif kind == "sum":
                        sum_evac(t - 1, i, n)

                def sum_evac(t, i, n):
                    after(act, s_sum, t, i + 1)
                    if i == 0:
                        after(act, s_rope, t + 2, 4)
                    nc.scalar.activation(divisor[:, i * HALF:(i + 1) * HALF], work[:, n % 2], ACT.Copy) \
                      .then_inc(s_sum_read.sem, 1)

                def q_high(p, u, n):
                    if n == 0:
                        after(act, s_rope, p, 2)
                    for h, src in ((0, top), (1, bot))[n:n + 1]:
                        for dst in (top, bot):
                            nc.scalar.activation(q1[u][dst, h], z[0][src], ACT.Copy).then_inc(s_qhi.sem, 1)

                def exp(t, kt, h):
                    after(act, s_score, t, 2 * kt + h + 1)
                    if not isinstance(t, int):
                        r, k_old = (t, kt - 2) if kt >= 2 else (t - 1, kt - 2 + KT)
                        after(act, s_pv, r, k_old + 1)
                        after(act, s_acc, r, add_index(k_old, h))
                    nc.scalar.activation(probs[h][kt % 2][:], scores[h][:], ACT.Exp, scale=SCALE) \
                      .then_inc(s_exp.sem, 1)

                def read_outputs(t):
                    after(act, s_pv, t, KT)
                    after(act, s_store, t - 1, 1)
                    nc.scalar.activation(o_raw[:], o_ps[:], ACT.Copy).then_inc(s_oraw.sem, 1)

                split_w(0, first=True)
                for n, job in enumerate(proj):
                    rows(job, 0, n)
                q_high(0, 0, 0)
                q_high(0, 0, 1)
                split_w(1)
                for job in jobs:
                    if job[0] in ("proj", "vturn"):
                        evac(job, -1, 1)
                for h in range(2):
                    exp(0, 0, h)
                act.wait_ge(s_const, n_const)
                q_high(1, 1, 0)
                q_high(1, 1, 1)
                with act.Fori(0, PAIRS // 2) as it:
                    for u in range(2):
                        t = 2 * it + u
                        for kt in range(KT):
                            nt, nk, _ = next_tile(t, kt, u)
                            if kt == 0:
                                read_outputs(t - 1)
                            for h in range(3):
                                for job in slots.get((kt, 2 * h), []) + slots.get((kt, 2 * h + 1), []):
                                    evac(job, t, u)
                                if h < 2:
                                    if (kt, h) == (KT - 1, 1):
                                        q_high(t + 2, u, 1)
                                    exp(nt, nk, h)
                            if kt == 0:
                                split_w(t + 2)
                            if kt == KT - 2:
                                after(act, s_score, t, 2 * KT)
                                q_high(t + 2, u, 0)
                read_outputs(PAIRS - 1)
                for i in range(2):
                    sum_evac(PAIRS - 1, i, i)

            @block.vector
            def _(dve):
                nc.vector.memset(ones[:], 1.0).then_inc(s_const, 1)
                for h in range(2):
                    nc.vector.memset(sums[h][:], 1.0).then_inc(s_const, 1)
                nc.vector.memset(o_ps[:], 0.0).then_inc(s_const, 1)
                dve.wait_ge(s_table, 32)
                dve.sem_inc(s_norm.sem, 1)

                def lo_w(p):
                    after(dve, s_whi, p, 1)
                    nc.vector.tensor_tensor(w_lo[:], w_raw[:], as_f32(w_hi[:]), ALU.subtract).then_inc(s_wlo.sem, 1)

                def reciprocals(t):
                    after(dve, s_sum_in, t, 1)
                    nc.vector.reciprocal(compact[:], compact[:]).then_inc(s_recip.sem, 1)

                def normalise(t, by_dma=True):
                    if by_dma:
                        after(dve, s_inv_in, t, 2)
                    after(dve, s_oraw, t, 1)
                    nc.vector.tensor_tensor(o_raw[:], o_raw[:], divisor[:], ALU.mult).then_inc(s_norm.sem, 1)

                def rope_cos(n, p):
                    after(dve, s_proj_read, p, 2 * n + 2)
                    after(dve, s_swap[n], p, 2)
                    nc.vector.tensor_tensor(z[n][:], z[n][:], cos[:], ALU.mult).then_inc(s_rope.sem, 1)

                def rope_add(n, p):
                    after(dve, s_rope, p, 2 * n + 1)
                    after(dve, s_sin, p, n + 1)
                    nc.vector.tensor_tensor(z[n][:], z[n][:], z_swap[n][:], ALU.add).then_inc(s_rope.sem, 1)

                def k_high(p, u):
                    after(dve, s_rope, p, 4)
                    for dst, src in ((k1[u][top, 0], top), (k1[u][bot, 1], bot), (k2[u][top, 0], top),
                                     (k2[u][bot, 1], bot)):
                        nc.vector.tensor_copy(dst, z[1][src]).then_inc(s_khi.sem, 1)

                def k_low(p, u):
                    for h, (src, dst) in enumerate(((top, bot), (bot, top))):
                        after(dve, s_khi, p, h + 1)
                        nc.vector.tensor_tensor(k1[u][dst, h], z[1][src], as_f32(k1[u][src, h]), ALU.subtract) \
                          .then_inc(s_klo.sem, 1)

                def q_low(p, u):
                    after(dve, s_qhi, p, 4)
                    for h, rows in ((0, top), (1, bot)):
                        nc.vector.tensor_tensor(q2[u][rows, h], z[0][rows], as_f32(q1[u][rows, h]), ALU.subtract) \
                          .then_inc(s_qlo.sem, 1)

                def reduce(job, p, u):
                    kind, h, i = job
                    n = index[job]
                    if kind == "max":
                        after(dve, s_max, p, h * 2 * KT + i + 1)
                        nc.vector.tensor_reduce(maxima[:, h, i // 2, i % 2:i % 2 + 1], work[:, n % 2], AX.X, ALU.max) \
                          .then_inc(s_max_read.sem, 1)
                        if i == 2 * KT - 1:
                            after(dve, s_max_read, p, h * 2 * KT + i + 1)
                            nc.vector.tensor_reduce(row_max[:, h], maxima[:, h], AX.X, ALU.max) \
                              .then_inc(s_comb.sem, 1)
                    elif kind == "turn":
                        after(dve, s_turn, p, h + 1)
                        rows = slice(DH, DH + KT) if h == 0 else slice(0, KT)
                        turned = work[0:KT, n % 2, 0:P].rearrange("p (a q) -> p a q", a=1).to_broadcast([KT, KT, P])
                        nc.vector.tensor_tensor(q2[u][rows, h].rearrange("p (a q) -> p a q", q=P), turned,
                                                keep.neg_block[0:KT], ALU.mult).then_inc(s_turn_read.sem, 1)

                beside = {
                    (0, 0): lambda t, u: q_low(t + 1, 1 - u),
                    (0, 5): lambda t, u: lo_w(t + 2),
                    (1, 3): lambda t, u: reciprocals(t - 1),
                    (4, 2): lambda t, u: rope_cos(0, t + 2),
                    (4, 5): lambda t, u: rope_add(0, t + 2),
                    (5, 1): lambda t, u: rope_cos(1, t + 2),
                    (5, 4): lambda t, u: rope_add(1, t + 2),
                    (2, 5): lambda t, u: normalise(t - 1),
                }

                def keys(t, u):
                    if not isinstance(t, int):
                        after(dve, s_score, t, 2 * KT)
                    k_high(t + 2, u)
                    k_low(t + 2, u)

                lo_w(0)
                for n in range(2):
                    rope_cos(n, 0)
                    rope_add(n, 0)
                dve.wait_ge(s_zero, 8)
                k_high(0, 0)
                k_low(0, 0)
                q_low(0, 0)
                lo_w(1)
                for where in [(kt, slot) for kt in range(KT) for slot in range(6)]:
                    for job in slots.get(where, []):
                        reduce(job, 0, 0)
                    if where in ((4, 2), (4, 5), (5, 1), (5, 4)):
                        beside[where](-1, 1)
                keys(-1, 1)
                with dve.Fori(0, PAIRS // 2) as it:
                    for u in range(2):
                        t = 2 * it + u
                        for where in [(kt, slot) for kt in range(KT) for slot in range(6)]:
                            for job in slots.get(where, []):
                                reduce(job, t + 1, 1 - u)
                            if where in beside:
                                beside[where](t, u)
                        keys(t, u)
                after(dve, s_sum_read, PAIRS - 1, 2)
                nc.vector.reciprocal(divisor[:], divisor[:]).then_inc(s_recip.sem, 1)
                after(dve, s_recip, PAIRS - 1, 1)
                normalise(PAIRS - 1, by_dma=False)

            @block.gpsimd
            def _(pool):
                fills = [(tile[u][:], 0.0) for u in range(2) for tile in (k2, q2)]
                ones_at = ((slice(DH, DH + KT), 0), (slice(0, KT), 1))
                fills += [(k2[u][rows, h], 1.0) for u in range(2) for rows, h in ones_at]
                for n, (part, value) in enumerate(fills):
                    if n:
                        pool.wait_ge(s_zero, n)
                    nc.gpsimd.memset(as_f32(part), value).then_inc(s_zero, 1)
                pool.sem_inc(s_acc.sem, 2 * (KT - 1))
                pool.sem_inc(s_store.sem, 16)
                pool.wait_ge(s_table, 32)

                def sine(n, p):
                    after(pool, s_swap[n], p, 2)
                    nc.gpsimd.tensor_tensor(z_swap[n][:], z_swap[n][:], sin[:], ALU.mult).then_inc(s_sin.sem, 1)

                def add(t, kt, h):
                    after(pool, s_exp, t, 2 * kt + h + 1)
                    if kt == 1:
                        after(pool, s_sum, t - 1, 2)
                        first_term = probs[h][0][:]
                    else:
                        after(pool, s_acc, t, add_index(kt - 1, h))
                        first_term = sums[h][:]
                    nc.gpsimd.tensor_tensor(sums[h][:], first_term, probs[h][kt % 2][:], ALU.add) \
                      .then_inc(s_acc.sem, 1)

                for p in range(2):
                    for n in range(2):
                        sine(n, p)
                with pool.Fori(0, PAIRS // 2) as it:
                    for u in range(2):
                        t = 2 * it + u
                        for kt in range(1, KT):
                            for h in range(2):
                                add(t, kt, h)
                            if kt in (4, 5):
                                sine(kt - 4, t + 2)

def project_weights(sb, sem, name, io, wo, bias):
    return Weights(sb, sem, name, {"w_raw": ([P, HP, D], io[wo].rearrange("(h p) d -> p h d", p=P)),
                                   "bias": ([P, D], io[bias].partition_broadcast(P))})


def phase_project(nc, io, keep, sem, name, o_pairs, m, weights, loaded_before, next_weights=None):
    first = m == 0
    chunk_tiles = GT // 2
    chunk = chunk_tiles * P
    with ExitStack() as ctx:
        sb = lambda n, s, d: ctx.enter_context(nc.sbuf_tensor(f"{name}_{n}", s, d))
        ps = lambda n, s, d: ctx.enter_context(nc.psum_tensor(f"{name}_{n}", s, d))
        ln = Layernorm(nc, lambda n, s, d: ctx.enter_context(nc.sbuf_tensor(n, s, d)),
                       lambda n, s, d: ctx.enter_context(nc.psum_tensor(n, s, d)), keep.norm_counters, f"{name}_ln",
                       keep.s_carrier)
        w_raw, bias_row = weights.tile["w_raw"], weights.tile["bias"]
        w_hi = sb("w_hi", [P, HP, D], F32R)
        w_lo = sb("w_lo", [P, HP, D], F32R)
        o_raw = [sb(f"o_raw{c}", [P, HP, chunk], F32) for c in range(2)]
        o_hi = [sb(f"o_hi{c}", [P, HP, chunk], F32R) for c in range(2)]
        o_lo = [sb(f"o_lo{c}", [P, HP, chunk], F32R) for c in range(2)]
        x_bias = sb("x_bias", [P, GT, D], F32)
        x_old = sb("x_old", [P, GT, D], F32) if first else None
        acc = [ps(f"acc{c}", [P, chunk_tiles, D], F32) for c in range(2)]
        s_w = weights.loaded
        s_w_hi = sem(f"{name}_w_hi")
        s_w_lo = sem(f"{name}_w_lo")
        s_o = [Counter(sem(f"{name}_o{c}"), 1, 16) for c in range(2)]
        s_xold = Counter(sem(f"{name}_xold"), 1, 16)
        s_hi = Counter(sem(f"{name}_hi"), 2, start=2)
        s_lo = Counter(sem(f"{name}_lo"), 2, start=2)
        s_mm = Counter(sem(f"{name}_mm"), 2, start=2)
        s_xb = Counter(sem(f"{name}_xb"), GT, start=GT)
        s_x = Counter(sem(f"{name}_x"), 2, start=2)
        x_d = io["x"].rearrange("(g j p) d -> g p j d", p=P, j=GT)
        o_d = o_pairs.rearrange("(h b) p n -> b p h n", b=B)

        with nc.Block() as block:
            @block.sync
            def _(sp):
                if not loaded_before:
                    weights.load(sp)

                def loads(g):
                    for c in range(2):
                        after_sp(sp, s_hi, g - 1, c + 1, keep.s_carrier)
                        after_sp(sp, s_lo, g - 1, c + 1, keep.s_carrier)
                        start = (g % 2) * HALF + c * chunk
                        src = o_d[bass.ds(g // 2, 1), :, :, bass.ds(start, chunk)].rearrange("o p h n -> (o p) h n")
                        sp.dma_start(o_raw[c][:], src).then_inc(s_o[c].sem, 16)
                    if first:
                        after_sp(sp, s_xb, g - 1, GT, keep.s_carrier)
                        sp.dma_start(x_old[:], x_d[bass.ds(g, 1)].rearrange("o p j d -> (o p) j d")) \
                          .then_inc(s_xold.sem, 16)

                loads(0)
                if next_weights:
                    next_weights.load(sp)
                with sp.Fori(1, GROUPS) as g:
                    loads(g)

            @block.gpsimd
            def _(pool):
                pool.sem_inc(s_xb.sem, GT)
                pool.wait_ge(s_w, weights.total)
                ln.start_pool(pool)

                def old_rows(g):
                    if first:
                        after(pool, s_xold, g, 1)
                    after(pool, s_x, g - 1, 2)
                    for j in range(GT):
                        src = x_old[:, j] if first else keep.x[:, bass.ds(g * GT + j, 1)].rearrange("p o d -> p (o d)")
                        nc.gpsimd.tensor_tensor(x_bias[:, j], src, bias_row[:], ALU.add).then_inc(s_xb.sem, 1)

                old_rows(0)
                with pool.Fori(0, GROUPS - 1) as g:
                    pool_rstd(nc, pool, ln, g)
                    old_rows(g + 1)
                pool_rstd(nc, pool, ln, GROUPS - 1)

            @block.scalar
            def _(act):
                act.sem_inc(s_hi.sem, 2)
                ln.start_act(act)
                act.wait_ge(s_w, weights.total)
                nc.scalar.activation(w_hi[:], w_raw[:], ACT.Copy).then_inc(s_w_hi, 1)

                def halves(g, c):
                    after(act, s_o[c], g, 1)
                    after(act, s_mm, g - 1, c + 1)
                    nc.scalar.activation(o_hi[c][:], o_raw[c][:], ACT.Copy).then_inc(s_hi.sem, 1)

                halves(0, 0)
                halves(0, 1)
                halves(1, 0)
                halves(1, 1)
                with act.Fori(1, GROUPS - 1) as g:
                    halves(g + 1, 0)
                    act_modulate(nc, act, ln, keep, m, g - 1)
                    halves(g + 1, 1)
                act_modulate(nc, act, ln, keep, m, GROUPS - 2)
                act_modulate(nc, act, ln, keep, m, GROUPS - 1)

            @block.tensor
            def _(pe):
                pe.sem_inc(s_mm.sem, 2)
                ln.start_pe(pe)
                pe.wait_ge(s_w_hi, 1)
                pe.wait_ge(s_w_lo, 1)

                def products(g, c):
                    after(pe, s_lo, g, c + 1)
                    after(pe, s_hi, g, c + 1)
                    after(pe, s_x, g - 1, c + 1)
                    for j in range(chunk_tiles):
                        steps = [(o, w, h) for h in range(HP) for o, w in split_products(o_hi[c], o_lo[c], w_hi, w_lo)]
                        for n, (o, w, h) in enumerate(steps):
                            mm = nc.tensor.matmul(acc[c][:, j], o[:, h, j * P:(j + 1) * P], w[:, h], start=(n == 0),
                                                  stop=(n == len(steps) - 1))
                    mm.then_inc(s_mm.sem, 1)

                products(0, 0)
                products(0, 1)
                with pe.Fori(1, GROUPS) as g:
                    products(g, 0)
                    pe_turn(nc, pe, ln, keep.ident[:], g - 1)
                    products(g, 1)
                pe_turn(nc, pe, ln, keep.ident[:], GROUPS - 1)

            @block.vector
            def _(dve):
                dve.sem_inc(s_lo.sem, 2)
                dve.sem_inc(s_x.sem, 2)
                ln.start_dve(nc, dve)
                dve.wait_ge(s_w_hi, 1)
                nc.vector.tensor_tensor(w_lo[:], w_raw[:], as_f32(w_hi[:]), ALU.subtract).then_inc(s_w_lo, 1)

                def low_half(g, c):
                    after(dve, s_hi, g, c + 1)
                    nc.vector.tensor_tensor(o_lo[c][:], o_raw[c][:], as_f32(o_hi[c][:]), ALU.subtract) \
                      .then_inc(s_lo.sem, 1)

                def new_rows(g, c):
                    after(dve, s_mm, g, c + 1)
                    after(dve, s_xb, g, GT)
                    tiles = bass.ds(g * GT + c * chunk_tiles, chunk_tiles)
                    nc.vector.tensor_tensor(keep.x[:, tiles], acc[c][:], x_bias[:, c * chunk_tiles:(c + 1) * chunk_tiles],
                                            ALU.add).then_inc(s_x.sem, 1)

                rows = lambda g: lambda j: keep.x[:, bass.ds(g * GT + j, 1)].rearrange("p o d -> p (o d)")

                def statistics(g):
                    after(dve, s_x, g, 2)
                    dve.sem_inc(keep.s_carrier, 1)
                    dve_statistics(nc, ln, rows(g))
                    dve_moments(nc, dve, ln, g)

                low_half(0, 0)
                low_half(0, 1)
                new_rows(0, 0)
                low_half(1, 0)
                new_rows(0, 1)
                statistics(0)
                low_half(1, 1)
                with dve.Fori(1, GROUPS - 1) as g:
                    dve_normalised(nc, dve, ln, rows(g - 1), g - 1)
                    new_rows(g, 0)
                    low_half(g + 1, 0)
                    dve_modulated_lo(nc, dve, ln, keep, g - 1)
                    new_rows(g, 1)
                    statistics(g)
                    low_half(g + 1, 1)
                last = GROUPS - 1
                dve_normalised(nc, dve, ln, rows(last - 1), last - 1)
                new_rows(last, 0)
                dve_modulated_lo(nc, dve, ln, keep, last - 1)
                new_rows(last, 1)
                statistics(last)
                dve_normalised(nc, dve, ln, rows(last), last)
                dve_modulated_lo(nc, dve, ln, keep, last)

def phase_context(nc, io, keep, sem, kv_dram):
    ct = B * M // P
    kw = (P, DC - P)
    hr = HP // 2
    with ExitStack() as ctx:
        sb = lambda n, s, d: ctx.enter_context(nc.sbuf_tensor(f"cx_{n}", s, d))
        ps = lambda n, s, d: ctx.enter_context(nc.psum_tensor(f"cx_{n}", s, d))
        rows = sb("rows", [P, ct, DC], F32)
        scale = sb("scale", [P, 2], F32)
        shift = sb("shift", [P, 2], F32)
        stats = sb("stats", [P, ct, 6], F32)
        moments = sb("moments", [P, ct, 2], F32)
        var_eps = sb("var_eps", [P, ct], F32)
        minus_half = sb("minus_half", [P, ct], F32)
        rstd = sb("rstd", [P, ct], F32)
        xn = sb("xn", [P, ct, DC], F32)
        y = sb("y", [P, 2, ct * P], F32)
        y_hi = sb("y_hi", [P, 2, ct * P], F32R)
        y_lo = sb("y_lo", [P, 2, ct * P], F32R)
        w_raw = sb("w_raw", [P, HP, 4 * P], F32)
        w_hi = sb("w_hi", [P, HP, 4 * P], F32R)
        w_lo = sb("w_lo", [P, HP, 4 * P], F32R)
        cos = sb("cos", [P, M], F32)
        sin = sb("sin", [P, M], F32)
        z = sb("k_rows", [P, HP, B, M], F32)
        z_swap = sb("k_swapped", [P, HP, B, M], F32)
        kv = sb("kv", [P, HP, B, 4, M], F32R)
        turned = ps("turned", [P, 2, ct * P], F32)
        k_ps = [ps(f"k_ps{u}", [P, 2 * B * M], F32) for u in range(2)]
        v_ps = [ps(f"v_ps{u}", [P, 2 * ct, P], F32) for u in range(2)]
        s_in, s_stat, s_mom, s_var, s_rstd, s_xn, s_turned, s_mod, s_ylo, s_half = (
            sem(f"cx_{n}") for n in ("in", "stat", "mom", "var", "rstd", "xn", "turned", "mod", "ylo", "half"))
        s_w = [sem(f"cx_w{n}") for n in range(2)]
        s_swap = [sem(f"cx_swap{n}") for n in range(2)]
        s_store = sem("cx_store")
        s_whi, s_wlo, s_k, s_v, s_evac, s_sin, s_cos, s_sum, s_khi, s_klo = (
            sem(f"cx_{n}") for n in ("whi", "wlo", "k", "v", "evac", "sin", "cos", "sum", "khi", "klo"))
        s_vhi = Counter(sem("cx_vhi"), 4)
        s_vlo = Counter(sem("cx_vlo"), 4)
        half = lambda n: slice(n * hr, (n + 1) * hr)
        v_places = [(par, h) for par in range(2) for h in range(2)]

        def v_source(r, par, h):
            return v_ps[r % 2][par * M:(par + 1) * M, 0:ct, h * DH:(h + 1) * DH]

        def v_target(r, par, h, f):
            return kv[h * DH:(h + 1) * DH, r, par::2, f]

        with nc.Block() as block:
            @block.sync
            def _(sp):
                for dst, src in ((rows[:], io["ctx"].rearrange("(j p) d -> p j d", p=P)), (scale[:], io["lnc_w"]),
                                 (shift[:], io["lnc_b"]), (cos[:], io["cos"][:, 0:M]), (sin[:], io["sin"][:, 0:M])):
                    sp.dma_start(dst, src).then_inc(s_in, 16)
                for n in range(2):
                    sp.dma_start(w_raw[:, half(n)], io["w_ctx"][half(n)].rearrange("h p k z m -> p h (k z m)")) \
                      .then_inc(s_w[n], 16)
                for n in range(2):
                    sp.wait_ge(s_evac, (n + 1) * hr)
                    for q in range(2):
                        sp.dma_start(z_swap[q:P:2, half(n)], z[1 - q:P:2, half(n)]).then_inc(s_swap[n], 16)
                for n in range(2):
                    sp.wait_ge(s_khi, n + 1)
                    sp.wait_ge(s_klo, n + 1)
                    sp.wait_ge(s_vhi.sem, 4 * hr * (n + 1))
                    sp.wait_ge(s_vlo.sem, 4 * hr * (n + 1))
                    sp.dma_start(kv_dram[n * hr * B:(n + 1) * hr * B].rearrange("(h b) p n -> p h b n", b=B),
                                 as_f32(kv[:, half(n)].rearrange("p h b f n -> p h b (f n)"))).then_inc(s_store, 16)
                sp.wait_ge(s_store, 32)

            @block.gpsimd
            def _(pool):
                nc.gpsimd.memset(minus_half[:], -0.5).then_inc(s_half, 1)
                pool.wait_ge(s_var, 1)
                pool.wait_ge(s_half, 1)
                nc.gpsimd.tensor_tensor(rstd[:], var_eps[:], minus_half[:], ALU.pow).then_inc(s_rstd, 1)
                for n in range(2):
                    pool.wait_ge(s_swap[n], 32)
                    rows_n = z_swap[:, half(n)].rearrange("p h b m -> p (h b) m")
                    nc.gpsimd.tensor_tensor(rows_n, rows_n, sin[:].unsqueeze(1).to_broadcast([P, hr * B, M]),
                                            ALU.mult).then_inc(s_sin, 1)

            @block.vector
            def _(dve):
                dve.wait_ge(s_in, 80)
                for j in range(ct):
                    nc.vector.bn_stats(stats[:, j], rows[:, j]).then_inc(s_stat, 1)
                for j in range(ct):
                    dve.wait_ge(s_stat, j + 1)
                    nc.vector.bn_aggr(moments[:, j], stats[:, j]).then_inc(s_mom, 1)
                dve.wait_ge(s_mom, ct)
                nc.vector.tensor_scalar(var_eps[:], moments[:, :, 1], EPS, None, ALU.add).then_inc(s_var, 1)
                dve.wait_ge(s_rstd, 1)
                for j in range(ct):
                    nc.vector.tensor_scalar(xn[:, j], rows[:, j], moments[:, j, 0:1], rstd[:, j:j + 1], ALU.subtract,
                                            ALU.mult).then_inc(s_xn, 1)

                def lo_w(n):
                    dve.wait_ge(s_whi, n + 1)
                    nc.vector.tensor_tensor(w_lo[:, half(n)], w_raw[:, half(n)], as_f32(w_hi[:, half(n)]), ALU.subtract) \
                      .then_inc(s_wlo, 1)

                for k in range(2):
                    dve.wait_ge(s_mod, 2 * k + 2)
                    nc.vector.tensor_tensor(y_lo[0:kw[k], k], y[0:kw[k], k], as_f32(y_hi[0:kw[k], k]), ALU.subtract) \
                      .then_inc(s_ylo, 1)
                lo_w(0)
                lo_w(1)

                def v_low(r):
                    after(dve, s_vhi, r, 4)
                    for par, h in v_places:
                        nc.vector.tensor_tensor(v_target(r, par, h, 3), v_source(r, par, h),
                                                as_f32(v_target(r, par, h, 2)), ALU.subtract).then_inc(s_vlo.sem, 1)

                def cosines(n):
                    dve.wait_ge(s_evac, (n + 1) * hr)
                    dve.wait_ge(s_swap[n], 32)
                    rows_n = z[:, half(n)].rearrange("p h b m -> p (h b) m")
                    nc.vector.tensor_tensor(rows_n, rows_n, cos[:].unsqueeze(1).to_broadcast([P, hr * B, M]), ALU.mult) \
                      .then_inc(s_cos, 1)

                def sines(n):
                    dve.wait_ge(s_cos, n + 1)
                    dve.wait_ge(s_sin, n + 1)
                    nc.vector.tensor_tensor(z[:, half(n)], z[:, half(n)], z_swap[:, half(n)], ALU.add).then_inc(s_sum, 1)

                def k_low(n):
                    dve.wait_ge(s_khi, n + 1)
                    nc.vector.tensor_tensor(kv[:, half(n), :, 1].rearrange("p h b m -> p (h b) m"),
                                            z[:, half(n)].rearrange("p h b m -> p (h b) m"),
                                            as_f32(kv[:, half(n), :, 0]).rearrange("p h b m -> p (h b) m"),
                                            ALU.subtract).then_inc(s_klo, 1)

                for r in range(HP):
                    v_low(r)
                    if r == hr + 1:
                        cosines(0)
                    if r == HP - 1:
                        sines(0)
                k_low(0)
                cosines(1)
                sines(1)
                k_low(1)

            @block.scalar
            def _(act):
                act.wait_ge(s_in, 80)
                for k in range(2):
                    n = kw[k]
                    act.wait_ge(s_turned, 2)
                    for dst in (y, y_hi):
                        nc.scalar.activation(dst[0:n, k], turned[0:n, k], ACT.Identity, scale=scale[0:n, k:k + 1],
                                             bias=shift[0:n, k:k + 1]).then_inc(s_mod, 1)
                for n in range(2):
                    act.wait_ge(s_w[n], 16)
                    nc.scalar.activation(w_hi[:, half(n)], w_raw[:, half(n)], ACT.Copy).then_inc(s_whi, 1)

                def k_high(n):
                    act.wait_ge(s_sum, n + 1)
                    nc.scalar.activation(kv[:, half(n), :, 0].rearrange("p h b m -> p (h b) m"),
                                         z[:, half(n)].rearrange("p h b m -> p (h b) m"), ACT.Copy).then_inc(s_khi, 1)

                for r in range(HP):
                    act.wait_ge(s_k, r + 1)
                    nc.scalar.activation(z[:, r].rearrange("p b m -> p (b m)"), k_ps[r % 2][:, 0:B * M], ACT.Copy) \
                      .then_inc(s_evac, 1)
                    act.wait_ge(s_v, r + 1)
                    for par, h in v_places:
                        nc.scalar.activation(v_target(r, par, h, 2), v_source(r, par, h), ACT.Copy) \
                          .then_inc(s_vhi.sem, 1)
                for n in range(2):
                    k_high(n)

            @block.tensor
            def _(pe):
                for k in range(2):
                    for j in range(ct):
                        pe.wait_ge(s_xn, j + 1)
                        mm = nc.tensor.transpose(turned[0:kw[k], k, j * P:(j + 1) * P],
                                                 xn[:, j, k * P:k * P + kw[k]], keep.ident[:])
                    mm.then_inc(s_turned, 1)
                pe.wait_ge(s_ylo, 2)
                cols = lambda w, r, k, zz: w[0:kw[k], r, (2 * k + zz) * P:(2 * k + zz + 1) * P]
                products = [(a, b, k) for k in range(2) for a, b in split_products(w_hi, w_lo, y_hi, y_lo)]
                for r in range(HP):
                    if r % hr == 0:
                        pe.wait_ge(s_whi, r // hr + 1)
                        pe.wait_ge(s_wlo, r // hr + 1)
                    if r >= 2:
                        pe.wait_ge(s_evac, r - 1)
                    for n, (w, x, k) in enumerate(products):
                        mm = nc.tensor.matmul(k_ps[r % 2][:, 0:B * M], cols(w, r, k, 0), x[0:kw[k], k], start=(n == 0),
                                              stop=(n == 5))
                    mm.then_inc(s_k, 1)
                    if r >= 2:
                        after(pe, s_vlo, r - 2, 4)
                    for j in range(ct):
                        for n, (w, x, k) in enumerate(products):
                            mm = nc.tensor.matmul(v_ps[r % 2][:, j], x[0:kw[k], k, j * P:(j + 1) * P], cols(w, r, k, 1),
                                                  start=(n == 0), stop=(n == 5))
                    mm.then_inc(s_v, 1)


def phase_cross_attention(nc, io, keep, sem, kv_dram, o_dram, next_weights):
    with ExitStack() as ctx:
        sb = lambda n, s, d: ctx.enter_context(nc.sbuf_tensor(f"ca_{n}", s, d))
        ps = lambda n, s, d: ctx.enter_context(nc.psum_tensor(f"ca_{n}", s, d))
        two = lambda n, s, d: [sb(f"{n}{u}", s, d) for u in range(2)]
        w_raw = sb("w_raw", [P, KD, P], F32)
        w_hi = sb("w_hi", [P, KD, P], F32R)
        w_lo = sb("w_lo", [P, KD, P], F32R)
        cos = sb("cos", [P, N], F32)
        sin = sb("sin", [P, N], F32)
        z = two("q_rows", [P, N], F32)
        z_swap = two("q_swapped", [P, N], F32)
        q_hi = two("q_hi", [P, N], F32R)
        q_lo = two("q_lo", [P, N], F32R)
        kv = [sb(f"kv{b}", [P, 4, P], F32R) for b in range(B)]
        row_max = sb("row_max", [P, 2, KT], F32)
        neg_max = sb("neg_max", [2 * KT, KT, P], F32R)
        heads_raw = sb("heads_raw", [2 * KT, P], F32)
        heads = sb("heads", [2 * KT, P], F32R)
        ones_raw = sb("ones_raw", [P, P], F32)
        ones = sb("ones", [P, P], F32R)
        probs = sb("probs", [P, N], F32)
        p_hi = two("p_hi", [P, N], F32R)
        p_lo = two("p_lo", [P, N], F32R)
        o_raw = two("o_raw", [P, N], F32)
        divisor = two("divisor", [P, N], F32)
        compact = sb("compact_sums", [P, 2 * N // P], F32)
        o_sb = sb("o_sb", [P, N], F32)
        work = ps("work", [P, N], F32)
        scores = ps("scores", [P, N], F32)
        o_ps = ps("o_ps", [P, N], F32)
        sum_ps = ps("sum_ps", [P, N], F32)
        sums_d = nc.dram_tensor("ca_sums_d", [2, N], F32, kind="Internal").ap()
        inv_d = nc.dram_tensor("ca_inv_d", [2, N], F32, kind="Internal").ap()
        compact_view = lambda d: d.rearrange("h (a b) -> (h a) b", b=2 * N // P)

        s_in, s_const, s_zero = (sem(f"ca_{n}") for n in ("in", "const", "zero"))
        s_w = Counter(sem("ca_w"), 1, 16)
        s_whi, s_wlo = (Counter(sem(f"ca_{n}"), 1) for n in ("whi", "wlo"))
        s_proj = Counter(sem("ca_proj"), 2)
        s_evac = Counter(sem("ca_evac"), 2)
        s_sin = Counter(sem("ca_sin"), 1)
        s_rope = Counter(sem("ca_rope"), 2)
        s_hi, s_lo = (Counter(sem(f"ca_{n}"), 1) for n in ("hi", "lo"))
        s_kv = [sem(f"ca_kv{b}") for b in range(B)]
        s_swap = [sem(f"ca_swap{u}") for u in range(2)]
        s_max, s_mred = (Counter(sem(f"ca_{n}"), 2) for n in ("max", "mred"))
        s_turn, s_shift = (Counter(sem(f"ca_{n}"), 1) for n in ("turn", "shift"))
        s_score = Counter(sem("ca_score"), 1)
        s_exp = Counter(sem("ca_exp"), 2)
        s_plo = Counter(sem("ca_plo"), 1)
        s_sum, s_sum_read = (Counter(sem(f"ca_{n}"), 1) for n in ("sum", "sum_read"))
        s_pv, s_oraw = (Counter(sem(f"ca_{n}"), 1) for n in ("pv", "oraw"))
        s_sum_out = Counter(sem("ca_sum_out"), 1, 16)
        s_sum_in = Counter(sem("ca_sum_in"), 1, 16)
        s_recip = Counter(sem("ca_recip"), 1)
        s_inv_out = Counter(sem("ca_inv_out"), 1, 16)
        s_inv_in = Counter(sem("ca_inv_in"), 2, 16)
        s_norm = Counter(sem("ca_norm"), 1)
        s_store = Counter(sem("ca_store"), 1, 16)
        halves = [slice(i * HALF, (i + 1) * HALF) for i in range(2)]

        def real(t):
            return not isinstance(t, int) or 0 <= t < PAIRS

        def done(eng, counter, t, n):
            if real(t):
                after(eng, counter, t, n)

        def last(t):
            return isinstance(t, int) and t >= PAIRS - 2

        def steps(eng, step):
            for t in range(-2, B):
                step(t, t % B)
            with eng.Fori(1, HP - 2) as hp:
                for b in range(B):
                    step(B * hp + b, b)
            for t in range(PAIRS - 2 * B, PAIRS + 4):
                step(t, t % B)

        with nc.Block() as block:
            @block.sync
            def _(sp):
                def wait(counter, t, n):
                    if real(t):
                        after_sp(sp, counter, t, n, keep.s_carrier)

                for dst, src in ((cos[:], io["cos"]), (sin[:], io["sin"]), (heads_raw[:], io["heads"]),
                                 (ones_raw[:], io["ones_block"])):
                    sp.dma_start(dst, src).then_inc(s_in, 16)
                sp.dma_start(w_raw[:], io["w_cross"][0]).then_inc(s_w.sem, 16)

                def load(t, b):
                    for h in range(2):
                        rows = slice(h * DH, (h + 1) * DH)
                        src = kv_dram[bass.ds(t, 1), rows].rearrange("o p (f n) -> (o p) f n", n=M)
                        sp.dma_start(as_f32(kv[b][rows, :, rows]), src).then_inc(s_kv[b], 16)

                def weights(hp):
                    wait(s_whi, hp - 1, 1)
                    wait(s_wlo, hp - 1, 1)
                    sp.dma_start(w_raw[:], io["w_cross"][bass.ds(hp, 1)].rearrange("o p k m -> (o p) k m")) \
                      .then_inc(s_w.sem, 16)

                sp.wait_ge(s_zero, 4)

                def step(t, b):
                    u = b % 2
                    if real(t - 2) and not last(t - 2):
                        wait(s_sum_out, t - 2, 1)
                        wait(s_inv_out, t - 3, 1)
                        sp.dma_start(compact[:], compact_view(sums_d)).then_inc(s_sum_in.sem, 16)
                    if real(t + 2):
                        wait(s_evac, t + 2, 2)
                        wait(s_rope, t, 2)
                        for q in range(2):
                            sp.dma_start(z_swap[u][q:P:2], z[u][1 - q:P:2]).then_inc(s_swap[u], 16)
                    if b == B - 2 and real(t + 2 + B):
                        weights((t + 2) // B + 1)
                    if real(t - 2) and not last(t - 2):
                        wait(s_recip, t - 2, 1)
                        sp.dma_start(compact_view(inv_d), compact[:]).then_inc(s_inv_out.sem, 16)
                    if real(t - 3):
                        wait(s_norm, t - 3, 1)
                        sp.dma_start(o_dram[bass.ds(t - 3, 1)].rearrange("o p n -> (o p) n"), o_sb[:]) \
                          .then_inc(s_store.sem, 16)
                    if real(t + 2):
                        wait(s_pv, t - 2, 1)
                        load(t + 2, (b + 2) % B)
                    if real(t - 2) and not last(t - 2):
                        wait(s_inv_out, t - 2, 1)
                        for h in range(2):
                            sp.dma_start(divisor[u][h * DH:(h + 1) * DH], inv_d[h].partition_broadcast(DH)) \
                              .then_inc(s_inv_in.sem, 16)
                    if real(t - 1) and not last(t - 1):
                        wait(s_sum_read, t - 1, 1)
                        sp.dma_start(sums_d, divisor[1 - u][0:P:DH]).then_inc(s_sum_out.sem, 16)

                next_weights.load(sp)
                steps(sp, step)
                wait(s_store, PAIRS - 1, 1)

            @block.gpsimd
            def _(pool):
                for n, tile in enumerate(kv):
                    if n:
                        pool.wait_ge(s_zero, n)
                    nc.gpsimd.memset(as_f32(tile[:]), 0.0).then_inc(s_zero, 1)
                pool.wait_ge(s_in, 64)

                def step(t, b):
                    u = b % 2
                    if real(t + 2):
                        pool.wait_ge(s_swap[u], ((t + 2) // 2 + 1) * 32)
                        nc.gpsimd.tensor_tensor(z_swap[u][:], z_swap[u][:], sin[:], ALU.mult).then_inc(s_sin.sem, 1)
                    if real(t - 2):
                        after(pool, *((s_recip, t - 2, 1) if last(t - 2) else (s_inv_in, t - 2, 2)))
                        after(pool, s_oraw, t - 2, 1)
                        done(pool, s_store, t - 3, 1)
                        nc.gpsimd.tensor_tensor(o_sb[:], o_raw[u][:], divisor[u][:], ALU.mult).then_inc(s_norm.sem, 1)

                steps(pool, step)

            @block.tensor
            def _(pe):
                pe.wait_ge(s_const, 2)

                def queries(t, i):
                    parts = [(w, x, k) for k in range(KD) for w, x in split_products(w_hi, w_lo, keep.xt_hi, keep.xt_lo)]
                    for n, (w, x, k) in enumerate(parts):
                        cols = bass.ds((t % B) * N + i * HALF, HALF)
                        mm = nc.tensor.matmul(work[:, halves[i]], w[:, k], x[:, k, cols], start=(n == 0),
                                              stop=(n == len(parts) - 1))
                    mm.then_inc(s_proj.sem, 1)

                def maxima(t, u, b):
                    pe.wait_ge(s_kv[b], (t // B + 1) * 32)
                    after(pe, s_hi, t, 1)
                    done(pe, s_evac, t + 1, 2)
                    for qt in range(KT):
                        mm = nc.tensor.matmul(work[:, qt * P:(qt + 1) * P], q_hi[u][:, qt * P:(qt + 1) * P], kv[b][:, 0],
                                              start=True, stop=True)
                        if qt % 4 == 3:
                            mm.then_inc(s_max.sem, 1)

                def turn(t):
                    after(pe, s_mred, t, 2)
                    done(pe, s_exp, t - 1, 2)
                    nc.tensor.transpose(scores[0:2 * KT, 0:P], row_max[:].rearrange("p h q -> p (h q)"),
                                        keep.ident[:]).then_inc(s_turn.sem, 1)

                def score(t, u, b):
                    after(pe, s_shift, t, 1)
                    after(pe, s_lo, t, 1)
                    k_hi, k_lo = kv[b][:, 0], kv[b][:, 1]
                    for i in range(2):
                        shifts = neg_max[:].rearrange("r a q -> r (a q)")[:, halves[i]]
                        parts = [(k_hi, q_hi[u][:, halves[i]]), (k_hi, q_lo[u][:, halves[i]]),
                                 (k_lo, q_hi[u][:, halves[i]]), (heads[:], shifts)]
                        for n, (w, x) in enumerate(parts):
                            mm = nc.tensor.matmul(scores[:, halves[i]], w, x, start=(n == 0), stop=(n == 3))
                    mm.then_inc(s_score.sem, 1)

                def outputs(t, u, b):
                    after(pe, s_exp, t, 2)
                    after(pe, s_plo, t, 1)
                    done(pe, s_sum_read, t - 1, 1)
                    for i in range(2):
                        for n, p in enumerate((p_hi[u], p_lo[u])):
                            mm = nc.tensor.matmul(sum_ps[:, halves[i]], ones[:], p[:, halves[i]], start=(n == 0),
                                                  stop=(n == 1))
                    mm.then_inc(s_sum.sem, 1)
                    done(pe, s_oraw, t - 1, 1)
                    for i in range(2):
                        parts = split_products(kv[b][:, 2], kv[b][:, 3], p_hi[u][:, halves[i]],
                                               p_lo[u][:, halves[i]])
                        for n, (w, x) in enumerate(parts):
                            mm = nc.tensor.matmul(o_ps[:, halves[i]], w, x, start=(n == 0), stop=(n == 2))
                    mm.then_inc(s_pv.sem, 1)

                def step(t, b):
                    u = b % 2
                    if real(t + 2):
                        if b == B - 2:
                            after(pe, s_whi, (t + 2) // B, 1)
                            after(pe, s_wlo, (t + 2) // B, 1)
                        done(pe, s_evac, t + 1, 2)
                        done(pe, s_mred, t, 1)
                        queries(t + 2, 0)
                    if real(t):
                        turn(t)
                    if real(t + 2):
                        queries(t + 2, 1)
                    if real(t):
                        score(t, u, b)
                    if real(t + 1):
                        maxima(t + 1, 1 - u, (b + 1) % B)
                    if real(t - 1):
                        outputs(t - 1, 1 - u, (b - 1) % B)

                steps(pe, step)

            @block.scalar
            def _(act):
                act.wait_ge(s_in, 64)
                nc.scalar.activation(ones[:], ones_raw[:], ACT.Copy).then_inc(s_const, 1)
                nc.scalar.activation(heads[:], heads_raw[:], ACT.Copy).then_inc(s_const, 1)

                def split_w(hp):
                    after(act, s_w, hp, 1)
                    nc.scalar.activation(w_hi[:], w_raw[:], ACT.Copy).then_inc(s_whi.sem, 1)

                def step(t, b):
                    u = b % 2
                    if real(t + 2):
                        for i in range(2):
                            after(act, s_proj, t + 2, i + 1)
                            if i == 0:
                                done(act, s_lo, t, 1)
                            nc.scalar.activation(z[u][:, halves[i]], work[:, halves[i]], ACT.Copy).then_inc(s_evac.sem, 1)
                    if b == B - 3 and real(t + 3):
                        split_w((t + 3) // B)
                    if real(t + 1):
                        after(act, s_rope, t + 1, 2)
                        done(act, s_score, t - 1, 1)
                        nc.scalar.activation(q_hi[1 - u][:], z[1 - u][:], ACT.Copy).then_inc(s_hi.sem, 1)
                    if real(t):
                        after(act, s_score, t, 1)
                        done(act, s_plo, t - 1, 1)
                        nc.scalar.activation(probs[:], scores[:], ACT.Exp, scale=SCALE).then_inc(s_exp.sem, 1)
                        done(act, s_pv, t - 2, 1)
                        nc.scalar.activation(p_hi[u][:], scores[:], ACT.Exp, scale=SCALE).then_inc(s_exp.sem, 1)
                    if real(t - 1):
                        after(act, s_sum, t - 1, 1)
                        done(act, s_norm, t - 3, 1)
                        nc.scalar.activation(divisor[1 - u][:], sum_ps[:], ACT.Copy).then_inc(s_sum_read.sem, 1)
                        after(act, s_pv, t - 1, 1)
                        nc.scalar.activation(o_raw[1 - u][:], o_ps[:], ACT.Copy).then_inc(s_oraw.sem, 1)

                split_w(0)
                steps(act, step)

            @block.vector
            def _(dve):
                dve.wait_ge(s_in, 64)

                def lo_w(hp):
                    after(dve, s_whi, hp, 1)
                    nc.vector.tensor_tensor(w_lo[:], w_raw[:], as_f32(w_hi[:]), ALU.subtract).then_inc(s_wlo.sem, 1)

                def step(t, b):
                    u = b % 2
                    if real(t):
                        after(dve, s_turn, t, 1)
                        done(dve, s_score, t - 1, 1)
                        turned = scores[0:2 * KT, 0:P].unsqueeze(1).to_broadcast([2 * KT, KT, P])
                        nc.vector.tensor_tensor(neg_max[:], turned, keep.neg_block[:], ALU.mult).then_inc(s_shift.sem, 1)
                    if real(t + 1):
                        after(dve, s_rope, t + 1, 1)
                        after(dve, s_sin, t + 1, 1)
                        nc.vector.tensor_tensor(z[1 - u][:], z[1 - u][:], z_swap[1 - u][:], ALU.add).then_inc(s_rope.sem, 1)
                    if real(t - 1):
                        after(dve, s_exp, t - 1, 2)
                        done(dve, s_pv, t - 3, 1)
                        nc.vector.tensor_tensor(p_lo[1 - u][:], probs[:], as_f32(p_hi[1 - u][:]), ALU.subtract) \
                          .then_inc(s_plo.sem, 1)
                    if b == B - 3 and real(t + 3):
                        lo_w((t + 3) // B)
                    if real(t + 1):
                        after(dve, s_hi, t + 1, 1)
                        nc.vector.tensor_tensor(q_lo[1 - u][:], z[1 - u][:], as_f32(q_hi[1 - u][:]), ALU.subtract) \
                          .then_inc(s_lo.sem, 1)
                    if real(t - 2):
                        if last(t - 2):
                            after(dve, s_sum_read, t - 2, 1)
                        else:
                            after(dve, s_sum_in, t - 2, 1)
                        sums = divisor[u] if last(t - 2) else compact
                        nc.vector.reciprocal(sums[:], sums[:]).then_inc(s_recip.sem, 1)
                    if real(t + 1):
                        done(dve, s_turn, t, 1)
                        for i in range(2):
                            after(dve, s_max, t + 1, i + 1)
                            dst = row_max[:].rearrange("p h q -> p q h")[:, 4 * i:4 * i + 4]
                            nc.vector.tensor_reduce(dst, work[:, halves[i]].rearrange("p (q h m) -> p q h m", h=2, m=M),
                                                    AX.X, ALU.max).then_inc(s_mred.sem, 1)
                    if real(t + 2):
                        after(dve, s_evac, t + 2, 2)
                        dve.wait_ge(s_swap[u], ((t + 2) // 2 + 1) * 32)
                        nc.vector.tensor_tensor(z[u][:], z[u][:], cos[:], ALU.mult).then_inc(s_rope.sem, 1)

                lo_w(0)
                steps(dve, step)

def feed_forward_weights(sb, sem, io):
    tiles = F // P
    return Weights(sb, sem, "ff", {"w1_raw": ([P, KD, F], io["ff_w1"].rearrange("(k p) f -> p k f", p=P)),
                                   "w2_raw": ([P, tiles, D], io["ff_w2"].rearrange("(i p) d -> p i d", p=P)),
                                   "b1": ([P, tiles], io["ff_b1"]),
                                   "bias": ([P, D], io["ff_b2"].partition_broadcast(P))})


def phase_feed_forward(nc, io, keep, sem, out, weights):
    tiles, ring, skew = F // P, 4, 2
    with ExitStack() as ctx:
        sb = lambda n, s, d: ctx.enter_context(nc.sbuf_tensor(f"ff_{n}", s, d))
        ps = lambda n, s, d: ctx.enter_context(nc.psum_tensor(f"ff_{n}", s, d))
        w1_raw, w2_raw, b1, bias_row = (weights.tile[n] for n in ("w1_raw", "w2_raw", "b1", "bias"))
        w1_hi = sb("w1_hi", [P, KD, F], F32R)
        w1_lo = sb("w1_lo", [P, KD, F], F32R)
        w2_hi = sb("w2_hi", [P, tiles, D], F32R)
        w2_lo = sb("w2_lo", [P, tiles, D], F32R)
        hidden = sb("hidden", [P, ring, HALF], F32)
        h_hi = sb("h_hi", [P, ring, HALF], F32R)
        h_lo = sb("h_lo", [P, ring, HALF], F32R)
        x_bias = sb("x_bias", [P, GT, D], F32)
        out_sb = sb("out_sb", [P, GT, D], F32)
        h_ps = [ps(f"h_ps{i}", [P, HALF], F32) for i in range(ring)]
        acc = [ps(f"acc{j}", [P, HALF], F32) for j in range(GT)]
        s_w = weights.loaded
        s_w_hi = sem("ff_w_hi")
        s_w_lo = sem("ff_w_lo")
        s_hmm = Counter(sem("ff_hmm"), tiles)
        s_gelu = Counter(sem("ff_gelu"), tiles, start=tiles)
        s_hi = Counter(sem("ff_hi"), tiles)
        s_lo = Counter(sem("ff_lo"), tiles, start=tiles)
        s_mm = Counter(sem("ff_mm"), tiles, start=tiles)
        s_xb = Counter(sem("ff_xb"), GT)
        s_out = Counter(sem("ff_out"), GT, start=GT)
        s_store = Counter(sem("ff_store"), 1, 16, start=0)
        out_d = out.rearrange("(g j p) d -> g p j d", p=P, j=GT)

        def before(g, i, back):
            return (g, i - back + 1) if i >= back else (g - 1, i - back + 1 + tiles)

        with nc.Block() as block:
            @block.sync
            def _(sp):
                with sp.Fori(0, GROUPS) as g:
                    after_sp(sp, s_out, g, GT, keep.s_carrier)
                    sp.dma_start(out_d[bass.ds(g, 1)].rearrange("o p j d -> (o p) j d"), out_sb[:]) \
                      .then_inc(s_store.sem, 16)
                after_sp(sp, s_store, GROUPS - 1, 1, keep.s_carrier)

            @block.gpsimd
            def _(pool):
                pool.wait_ge(s_w, weights.total)
                with pool.Fori(0, GROUPS) as g:
                    after(pool, s_out, g - 1, GT)
                    for j in range(GT):
                        src = keep.x[:, bass.ds(g * GT + j, 1)].rearrange("p o d -> p (o d)")
                        nc.gpsimd.tensor_tensor(x_bias[:, j], src, bias_row[:], ALU.add).then_inc(s_xb.sem, 1)

            @block.scalar
            def _(act):
                act.sem_inc(s_gelu.sem, tiles)
                act.wait_ge(s_w, weights.total)
                nc.scalar.activation(w1_hi[:], w1_raw[:], ACT.Copy).then_inc(s_w_hi, 1)
                nc.scalar.activation(w2_hi[:], w2_raw[:], ACT.Copy).then_inc(s_w_hi, 1)
                with act.Fori(0, GROUPS) as g:
                    for i in range(tiles):
                        after(act, s_lo, *before(g, i, ring))
                        after(act, s_hmm, g, i + 1)
                        nc.scalar.activation(hidden[:, i % ring], h_ps[i % ring][:], ACT.Gelu, bias=b1[:, i:i + 1]) \
                          .then_inc(s_gelu.sem, 1)
                        after(act, s_mm, *before(g, i, ring))
                        after(act, s_gelu, g, i + 1)
                        nc.scalar.activation(h_hi[:, i % ring], hidden[:, i % ring], ACT.Copy).then_inc(s_hi.sem, 1)

            @block.tensor
            def _(pe):
                pe.sem_inc(s_mm.sem, tiles)
                pe.wait_ge(s_w_hi, 2)
                pe.wait_ge(s_w_lo, 2)

                def hidden_products(g, i):
                    after(pe, s_gelu, *before(g, i, ring))
                    cols = bass.ds(g * HALF, HALF)
                    steps = [(w, x, k) for k in range(KD) for w, x in split_products(w1_hi, w1_lo, keep.xt_hi, keep.xt_lo)]
                    for n, (w, x, k) in enumerate(steps):
                        mm = nc.tensor.matmul(h_ps[i % ring][:], w[:, k, i * P:(i + 1) * P], x[:, k, cols],
                                              start=(n == 0), stop=(n == len(steps) - 1))
                    mm.then_inc(s_hmm.sem, 1)

                def out_products(g, i):
                    after(pe, s_hi, g, i + 1)
                    after(pe, s_lo, g, i + 1)
                    if i == 0:
                        after(pe, s_out, g - 1, GT)
                    for j in range(GT):
                        for n, (h, w) in enumerate(split_products(h_hi, h_lo, w2_hi, w2_lo)):
                            mm = nc.tensor.matmul(acc[j][:, 0:D], h[:, i % ring, j * P:(j + 1) * P], w[:, i],
                                                  start=(i == 0 and n == 0), stop=(i == tiles - 1 and n == 2))
                    mm.then_inc(s_mm.sem, 1)

                def group(g, first=False):
                    for i in range(tiles):
                        hidden_products(g, i)
                        if i >= skew:
                            out_products(g, i - skew)
                        elif not first:
                            out_products(g - 1, i - skew + tiles)

                group(0, first=True)
                with pe.Fori(1, GROUPS) as g:
                    group(g)
                for i in range(tiles - skew, tiles):
                    out_products(GROUPS - 1, i)

            @block.vector
            def _(dve):
                dve.sem_inc(s_lo.sem, tiles)
                dve.sem_inc(s_out.sem, GT)
                for n, (raw, hi, lo) in enumerate(((w1_raw, w1_hi, w1_lo), (w2_raw, w2_hi, w2_lo))):
                    dve.wait_ge(s_w_hi, n + 1)
                    nc.vector.tensor_tensor(lo[:], raw[:], as_f32(hi[:]), ALU.subtract).then_inc(s_w_lo, 1)

                def low_halves(g, i):
                    after(dve, s_hi, g, i + 1)
                    nc.vector.tensor_tensor(h_lo[:, i % ring], hidden[:, i % ring], as_f32(h_hi[:, i % ring]),
                                            ALU.subtract).then_inc(s_lo.sem, 1)

                def sums(g, stored):
                    after(dve, s_mm, g, tiles)
                    after(dve, s_xb, g, GT)
                    if stored:
                        after(dve, s_store, g - 1, 1)
                    for j in range(GT):
                        nc.vector.tensor_tensor(out_sb[:, j], acc[j][:, 0:D], x_bias[:, j], ALU.add) \
                          .then_inc(s_out.sem, 1)

                def group(g, last_sums):
                    for i in range(tiles):
                        low_halves(g, i)
                        if i == skew - 1:
                            last_sums()

                group(0, lambda: None)
                group(1, lambda: sums(0, False))
                with dve.Fori(2, GROUPS) as g:
                    group(g, lambda: sums(g - 1, True))
                sums(GROUPS - 1, True)

class Keep:
    pass


def build(nc, io, out):
    with ExitStack() as used:
        sem = lambda name: used.enter_context(nc.semaphore("s_" + name))
        sb = lambda n, s, d: used.enter_context(nc.sbuf_tensor(n, s, d))
        keep = Keep()
        keep.s_carrier = sem("sp_carrier")
        keep.norm_counters = NormCounters(sem)
        keep.ident = sb("ident_sb", [P, P], F32)
        keep.neg_block = sb("neg_block_sb", [2 * KT, KT, P], F32)
        keep.mod_a = sb("mod_a", [P, 2, KD, B], F32)
        keep.mod_c = sb("mod_c", [P, 2, KD, B], F32)
        keep.xt_hi = sb("xt_hi", [P, KD, TOK], F32R)
        keep.xt_lo = sb("xt_lo", [P, KD, TOK], F32R)
        o_self = nc.dram_tensor("o_self", [PAIRS + 1, P, N], F32, kind="Internal").ap()
        o_cross = nc.dram_tensor("o_cross", [PAIRS, P, N], F32, kind="Internal").ap()
        kv_ctx = nc.dram_tensor("kv_ctx", [PAIRS, P, 4 * M], F32, kind="Internal").ap()
        phase_setup(nc, io, keep, sem)
        phase_first_norm(nc, io, keep, sem)
        keep.norm_counters.all_passed()
        phase_self_attention(nc, io, keep, sem, o_self)
        keep.x = sb("x_rows", [P, TOK // P, D], F32)
        with ExitStack() as own:
            wo = project_weights(lambda n, s, d: own.enter_context(nc.sbuf_tensor(n, s, d)), sem, "po", io, "sa_wo",
                                 "sa_bo")
            phase_project(nc, io, keep, sem, "po", o_self[1:PAIRS + 1], 0, wo, False)
        keep.norm_counters.all_passed()
        phase_context(nc, io, keep, sem, kv_ctx)
        wo = project_weights(sb, sem, "pc", io, "ca_wo", "ca_bo")
        phase_cross_attention(nc, io, keep, sem, kv_ctx, o_cross, wo)
        ff = feed_forward_weights(sb, sem, io)
        phase_project(nc, io, keep, sem, "pc", o_cross, 1, wo, True, ff)
        phase_feed_forward(nc, io, keep, sem, out, ff)

def table(positions):
    f32 = np.float32
    inv = (f32(1.0) / np.power(f32(10000.0), np.arange(0, DH, 2, dtype=f32) / f32(DH))).astype(f32)
    ang = (inv[:, None] * np.arange(positions, dtype=f32)[None, :]).astype(f32)
    c, s = np.cos(ang).astype(f32), np.sin(ang).astype(f32)
    by_dim = lambda even, odd: np.ascontiguousarray(np.tile(np.stack([even, odd], 1).reshape(DH, positions), (2, 1)))
    return by_dim(c, c), by_dim(-s, s)


def layouts(inputs):
    get = lambda n: np.asarray(inputs["L0_xcond_" + n])
    cols = lambda v: v.reshape(KD, P).T
    block = np.zeros((16, KT, P), np.float32)
    for r in range(16):
        block[r, r % KT] = -1.0
    cos, sin = table(N)
    pair = lambda w: w.reshape(w.shape[0], HP, P)
    wkv = get("sa_wkv")
    w_self = np.stack([pair(get("sa_wq")), pair(wkv[:, :MID]), pair(wkv[:, MID:])], 2)
    w_self = w_self.reshape(KD, P, HP, 3, P).transpose(2, 1, 0, 3, 4)
    heads = np.zeros((2 * KT, P), np.float32)
    ones = np.zeros((P, P), np.float32)
    for h in range(2):
        heads[h * KT:(h + 1) * KT, h * M:(h + 1) * M] = 1.0
        ones[h * M:(h + 1) * M, h * DH:(h + 1) * DH] = 1.0
    ckv = get("ca_wkv")
    pad = np.zeros((2 * P, HP, 2, P), np.float32)
    pad[:DC] = np.stack([pair(ckv[:, :MID]), pair(ckv[:, MID:])], 2)
    vec_pad = lambda v: np.concatenate([v, np.zeros(2 * P - DC, np.float32)])
    vecs = [get(n) for n in ("ln1_w", "ln1_b", "ln2_w", "ln2_b", "g1_b", "b1_b", "g2_b", "b2_b")]
    arrays = {
        "x": np.asarray(inputs["x"]).reshape(TOK, D),
        "cond": np.asarray(inputs["cond_1024"]).reshape(B, KD, P).transpose(2, 1, 0).reshape(P, KD * B),
        "gate_vec": np.stack([cols(v) for v in vecs], 1).reshape(P, -1),
        "gate_w0": get("g1_w"), "gate_w1": get("b1_w"), "gate_w2": get("g2_w"), "gate_w3": get("b2_w"),
        "ident": np.eye(P, dtype=np.float32), "neg_block": block.reshape(16, KT * P), "cos": cos, "sin": sin,
        "w_self": w_self, "heads": heads, "ones_block": ones,
        "w_ctx": pad.reshape(2, P, HP, 2, P).transpose(2, 1, 0, 3, 4),
        "w_cross": pair(get("ca_wq")).reshape(KD, P, HP, P).transpose(2, 1, 0, 3),
        "ctx": np.asarray(inputs["ctx_768"]).reshape(B * M, DC),
        "lnc_w": cols(vec_pad(get("ca_lnc_w"))), "lnc_b": cols(vec_pad(get("ca_lnc_b"))),
        "sa_wo": get("sa_wo"), "sa_bo": get("sa_bo"), "ca_wo": get("ca_wo"), "ca_bo": get("ca_bo"),
        "ff_w1": get("ff_w1"), "ff_b1": get("ff_b1").reshape(F // P, P).T, "ff_w2": get("ff_w2"),
        "ff_b2": get("ff_b2"),
    }
    return {n: np.ascontiguousarray(a) for n, a in arrays.items()}



def kernel(**inputs):
    import concourse.bacc as bacc
    from concourse.bass_utils import run_bass_kernel_spmd

    nc = bacc.Bacc("TRN2", target_bir_lowering=False, num_devices=1)
    arrays = {f"in_{n}": a for n, a in layouts(inputs).items()}
    io = {n[3:]: nc.dram_tensor(n, a.shape, mybir.dt.from_np(a.dtype), kind="ExternalInput").ap()
          for n, a in arrays.items()}
    out = nc.dram_tensor("out_rows", (TOK, D), F32, kind="ExternalOutput").ap()
    build(nc, io, out)
    result = run_bass_kernel_spmd(nc, [arrays], core_ids=[0])
    return result.results[0]["out_rows"].reshape(B, N, D)
```
